# Optimizing a Trainium2 kernel written in Bass

```python
import numpy as np
import jax
import jax.numpy as jnp

def _softmax(x, axis=-1):
    return jax.nn.softmax(x, axis=axis)

def _gelu(x):
    return jax.nn.gelu(x, approximate=True)

def _silu(x):
    return jax.nn.silu(x)

def _sigmoid(x):
    return jax.nn.sigmoid(x)

def _layernorm(x, axis=-1, eps=1e-05):
    m = jnp.mean(x, axis=axis, keepdims=True)
    v = jnp.var(x, axis=axis, keepdims=True)
    return (x - m) / jnp.sqrt(v + eps)

def _scatter_add(tgt, idx, src, axis=0):
    return tgt.at[idx].add(src)

def _segment_sum(src, seg, n):
    return jax.ops.segment_sum(src, seg, n)
kernel_name = 'mk_sandwich_d1_jaxref_r8_dda21e'

def setup_inputs(seed: int=0):
    np.random.seed(seed)
    _w = jnp.asarray

    def _L0_attn_setup():
        import jax, jax.numpy as jnp
        import numpy as np
        B, S, D, H = (4, 256, 128, 16)
        HEAD = D // H
        DENOM = float(np.sqrt(D))

        def _split_heads(x):
            b, s, _ = x.shape
            return x.reshape(b, s, H, HEAD).transpose(0, 2, 1, 3)
        key = jax.random.key(seed)
        ks = jax.random.split(key, 5)
        scale = 1.0 / np.sqrt(D)
        return {'hidden_state': jax.random.normal(ks[0], (B, S, D), dtype=jnp.float32), 'attention_mask': jnp.ones((B, S), dtype=jnp.int32), 'w_q': jax.random.normal(ks[1], (D, D), dtype=jnp.float32) * scale, 'w_k': jax.random.normal(ks[2], (D, D), dtype=jnp.float32) * scale, 'w_v': jax.random.normal(ks[3], (D, D), dtype=jnp.float32) * scale, 'w_o': jax.random.normal(ks[4], (D, D), dtype=jnp.float32) * scale}
    _L0_attn_in = _L0_attn_setup()

    def _L0_ffn_setup():
        import jax, jax.numpy as jnp
        import numpy as np
        HIDDEN = 128
        INTER = 512
        NUM_EXPERTS = 8
        TOP_K = 2
        EPS = 1e-05

        def _layer_norm(x, g, b):
            m = jnp.mean(x, axis=-1, keepdims=True)
            v = jnp.mean(jnp.square(x - m), axis=-1, keepdims=True)
            return (x - m) * jax.lax.rsqrt(v + EPS) * g + b
        key = jax.random.key(seed)
        ks = jax.random.split(key, 8)
        s = 0.02
        return {'x': jax.random.normal(ks[0], (4, 256, HIDDEN), dtype=jnp.float32), 'ln1_g': jnp.ones((HIDDEN,), jnp.float32), 'ln1_b': jnp.zeros((HIDDEN,), jnp.float32), 'attn_w': jax.random.normal(ks[1], (HIDDEN, HIDDEN), jnp.float32) * s, 'ln2_g': jnp.ones((HIDDEN,), jnp.float32), 'ln2_b': jnp.zeros((HIDDEN,), jnp.float32), 'gate_w': jax.random.normal(ks[2], (NUM_EXPERTS, HIDDEN), jnp.float32) * s, 'gate_proj': jax.random.normal(ks[3], (NUM_EXPERTS, INTER, HIDDEN), jnp.float32) * s, 'up_proj': jax.random.normal(ks[4], (NUM_EXPERTS, INTER, HIDDEN), jnp.float32) * s, 'down_proj': jax.random.normal(ks[5], (NUM_EXPERTS, HIDDEN, INTER), jnp.float32) * s}
    _L0_ffn_in = _L0_ffn_setup()
    _d = {'L0_attn_hidden_state': _L0_attn_in['hidden_state'], 'L0_attn_attention_mask': _L0_attn_in['attention_mask'], 'L0_attn_w_q': _L0_attn_in['w_q'], 'L0_attn_w_k': _L0_attn_in['w_k'], 'L0_attn_w_v': _L0_attn_in['w_v'], 'L0_attn_w_o': _L0_attn_in['w_o'], 'L0_ffn_ln1_g': _L0_ffn_in['ln1_g'], 'L0_ffn_ln1_b': _L0_ffn_in['ln1_b'], 'L0_ffn_attn_w': _L0_ffn_in['attn_w'], 'L0_ffn_ln2_g': _L0_ffn_in['ln2_g'], 'L0_ffn_ln2_b': _L0_ffn_in['ln2_b'], 'L0_ffn_gate_w': _L0_ffn_in['gate_w'], 'L0_ffn_gate_proj': _L0_ffn_in['gate_proj'], 'L0_ffn_up_proj': _L0_ffn_in['up_proj'], 'L0_ffn_down_proj': _L0_ffn_in['down_proj']}
    _x0 = _d['L0_attn_hidden_state']
    _d['L0_attn_hidden_state'] = jax.random.normal(jax.random.fold_in(jax.random.key(seed), 1), (8, 256, 128), dtype=_x0.dtype)
    del _x0
    return _d

def reference(L0_attn_hidden_state, L0_attn_attention_mask, L0_attn_w_q, L0_attn_w_k, L0_attn_w_v, L0_attn_w_o, L0_ffn_ln1_g, L0_ffn_ln1_b, L0_ffn_attn_w, L0_ffn_ln2_g, L0_ffn_ln2_b, L0_ffn_gate_w, L0_ffn_gate_proj, L0_ffn_up_proj, L0_ffn_down_proj):

    def _L0_attn_ref(hidden_state, attention_mask, w_q, w_k, w_v, w_o):
        import jax, jax.numpy as jnp
        import numpy as np
        B, S, D, H = (4, 256, 128, 16)
        HEAD = D // H
        DENOM = float(np.sqrt(D))

        def _split_heads(x):
            b, s, _ = x.shape
            return x.reshape(b, s, H, HEAD).transpose(0, 2, 1, 3)
        q = _split_heads(hidden_state @ w_q.T)
        k = _split_heads(hidden_state @ w_k.T)
        v = _split_heads(hidden_state @ w_v.T)
        qk = jnp.einsum('bhqd,bhkd->bhqk', q, k) / DENOM
        attn = jax.nn.softmax(qk, axis=-1)
        ctx = jnp.einsum('bhqk,bhkd->bhqd', attn, v)
        ctx = ctx.transpose(0, 2, 1, 3).reshape(hidden_state.shape[0], hidden_state.shape[1], D)
        return ctx @ w_o.T

    def _L0_ffn_ref(x, ln1_g, ln1_b, attn_w, ln2_g, ln2_b, gate_w, gate_proj, up_proj, down_proj):
        import jax, jax.numpy as jnp
        import numpy as np
        HIDDEN = 128
        INTER = 512
        NUM_EXPERTS = 8
        TOP_K = 2
        EPS = 1e-05

        def _layer_norm(x, g, b):
            m = jnp.mean(x, axis=-1, keepdims=True)
            v = jnp.mean(jnp.square(x - m), axis=-1, keepdims=True)
            return (x - m) * jax.lax.rsqrt(v + EPS) * g + b
        B, S, H = x.shape
        h = x + jnp.einsum('bsh,oh->bso', _layer_norm(x, ln1_g, ln1_b), attn_w)
        t = _layer_norm(h, ln2_g, ln2_b).reshape(-1, H)
        T = t.shape[0]
        logits = jnp.einsum('th,eh->te', t, gate_w)
        top_vals, top_idx = jax.lax.top_k(logits, TOP_K)
        rw = jax.nn.softmax(top_vals, axis=-1)
        comb = jnp.zeros((T, NUM_EXPERTS), dtype=t.dtype)
        comb = comb.at[jnp.arange(T)[:, None], top_idx].add(rw)
        out = jnp.zeros_like(t)
        for e in range(NUM_EXPERTS):
            g = jnp.einsum('th,ih->ti', t, gate_proj[e])
            u = jnp.einsum('th,ih->ti', t, up_proj[e])
            oe = jnp.einsum('ti,hi->th', jax.nn.silu(g) * u, down_proj[e])
            out = out + comb[:, e:e + 1] * oe
        return h + out.reshape(B, S, H)
    x = L0_attn_hidden_state
    x = x + _layernorm(_L0_attn_ref(_layernorm(x, axis=-1), L0_attn_attention_mask, L0_attn_w_q, L0_attn_w_k, L0_attn_w_v, L0_attn_w_o), axis=-1)
    x = x + _layernorm(_L0_ffn_ref(_layernorm(x, axis=-1), L0_ffn_ln1_g, L0_ffn_ln1_b, L0_ffn_attn_w, L0_ffn_ln2_g, L0_ffn_ln2_b, L0_ffn_gate_w, L0_ffn_gate_proj, L0_ffn_up_proj, L0_ffn_down_proj), axis=-1)
    return x

_drawn_inputs = setup_inputs


def setup_inputs(seed=0):
    import zlib

    import numpy as np

    out = dict(_drawn_inputs(seed))
    spreads = {'L0_ffn_ln1_g': (1.0, 0.6),
     'L0_ffn_ln1_b': (0.0, 0.8),
     'L0_ffn_ln2_g': (1.0, 0.6),
     'L0_ffn_ln2_b': (0.0, 0.8)}
    factors = {'L0_ffn_gate_w': 8.0,
     'L0_ffn_gate_proj': 8.0,
     'L0_ffn_up_proj': 8.0,
     'L0_ffn_down_proj': 8.0}
    for name, (base, spread) in spreads.items():
        noise = np.random.default_rng([zlib.crc32(name.encode()), seed]).standard_normal(out[name].shape)
        drawn = base * np.exp(spread * noise) if base else spread * noise
        out[name] = jnp.asarray(drawn.astype(out[name].dtype))
    for name, factor in factors.items():
        out[name] = (out[name] * factor).astype(out[name].dtype)
    return out
```

```python
from contextlib import ExitStack

import concourse.bass as bass
from concourse import mybir

P = 128
F32 = mybir.dt.float32
BF16 = mybir.dt.bfloat16
U32 = mybir.dt.uint32
I32 = mybir.dt.int32
ALU = mybir.AluOpType
ACT = mybir.ActivationFunctionType
AX = mybir.AxisListType

EPS = 1e-5
HEADS = 16
HD = 8
PRODUCTS = 6
STACK = PRODUCTS * HD
SHIFT_ROWS = 2
EXPERTS = 8
TOP = 2
ROW = 132
C_IDENT, C_UPPER, C_ONES, C_IOTA, C_REGION, C_DEST = 0, 128, 256, 384, 400, 416
C_LOWER, C_STEP, C_TILE, C_PAD, C_END = 424, 488, 504, 544, 676


class Batch:

    def __init__(self, n, parity, pair):
        self.n, self.parity, self.pair = n, parity, pair

    def plus(self, d):
        p = self.parity + d
        return Batch(self.n + d, p % 2, self.pair + p // 2)


def fixed(n):
    return Batch(n, n % 2, n // 2)


def block_kernel(nc, x, wqk, wv, wo, attn_w, gate_w, norms, gate_up, down, consts, out):
    NB, S, D = x.shape
    QT = S // P
    NT = NB * QT
    TOKENS = NB * S
    INTER = down.shape[1] // EXPERTS
    IC = INTER // P
    REGION = TOKENS + P
    TILES = -(-(TOP * TOKENS + EXPERTS * (P - 1)) // P)
    TILES += TILES % 2
    SCALE = 1.0 / float(D) ** 0.5
    TABLE_STEPS = 16
    assert D == P and QT == 2 and HEADS * HD == D

    xs = nc.dram_tensor("routed_rows", [EXPERTS * REGION + P, ROW], F32, kind="Internal").ap()
    ys = nc.dram_tensor("routed_results", [TOP * TOKENS, D], F32, kind="Internal").ap()

    ctx = ExitStack()
    with ctx:
        def sb(name, shape, dt=F32):
            return ctx.enter_context(nc.sbuf_tensor(name, shape, dt))

        def bank(name):
            return ctx.enter_context(nc.psum_tensor(name, [P, 512], F32))

        def sem(name):
            return ctx.enter_context(nc.semaphore(name))

        cst = sb("cst", [P, C_END])
        ident = cst[:, C_IDENT:C_IDENT + P]
        iota8 = cst[:, C_IOTA:C_IOTA + 16].rearrange("p (t e) -> p t e", e=EXPERTS)
        region_base = cst[:, C_REGION:C_REGION + 16]
        ident_b = sb("ident_b", [P, P], BF16)
        upper_b = sb("upper_b", [P, P], BF16)
        ones_b = sb("ones_b", [P, P], BF16)
        neg_half = sb("neg_half", [P, 4])
        wqk_sb = sb("wqk_sb", [P, 2, P])
        wv_sb = sb("wv_sb", [P, P])
        wo_sb = sb("wo_sb", [P, P])
        attn_w_sb = sb("attn_w_sb", [P, P])
        gate_w_sb = sb("gate_w_sb", [P, EXPERTS])
        norms_sb = sb("norms_sb", [P, 4])
        gate_up_sb = sb("gate_up_sb", [P, EXPERTS * 2 * INTER])
        down_sb = sb("down_sb", [P, EXPERTS * INTER])

        x_sb = sb("x_sb", [P, NT, D])
        x2_sb = sb("x2_sb", [P, NT, D])
        h_sb = sb("h_sb", [P, NT, D])

        x_st = sb("x_st", [P, QT, 6])
        x_mv = sb("x_mv", [P, QT, 2])
        x_ve = sb("x_ve", [P, QT])
        x_r = sb("x_r", [P, QT])
        xn = sb("xn", [P, QT, D])
        xnT = sb("xnT", [P, 2, S])
        parts = sb("parts", [P, 2, 3, 2, S], BF16)
        rest1 = sb("rest1", [P, 2, S])
        q_stack = sb("q_stack", [P, 2, HD, S], BF16)
        k_stack = sb("k_stack", [P, 2, HD, S], BF16)
        neg_max = sb("neg_max", [P, 2, QT, HEADS])
        shift = sb("shift", [P, 2, QT, 2, SHIFT_ROWS, 4], BF16)
        shiftT = sb("shiftT", [16, 2, S], BF16)
        v_aug = sb("v_aug", [P, 2, QT, HEADS, 32])
        probs = sb("probs", [P, 8, QT, S])
        u_sb = sb("u_sb", [P, 4, S])
        den_r = sb("den_r", [P, QT, HEADS])
        ctx_sb = sb("ctx_sb", [P, QT, D])
        ctxT = sb("ctxT", [P, S])
        y_sb = sb("y_sb", [P, QT, D])
        y_st = sb("y_st", [P, QT, 6])
        y_mv = sb("y_mv", [P, QT, 2])
        y_ve = sb("y_ve", [P, QT])
        y_r = sb("y_r", [P, QT])
        yn = sb("yn", [P, QT, D])
        z_st = sb("z_st", [P, QT, 6])
        z_mv = sb("z_mv", [P, QT, 2])
        z_ve = sb("z_ve", [P, 2, QT])
        z_r = sb("z_r", [P, 2, QT])
        z = sb("z", [P, QT, D])
        zn = sb("zn", [P, QT, D])
        znT = sb("znT", [P, S])
        h_st = sb("h_st", [P, QT, 6])
        h_mv = sb("h_mv", [P, QT, 2])
        h_ve = sb("h_ve", [P, QT])
        h_r = sb("h_r", [P, QT])
        rows = sb("rows", [P, 2, QT, TOP, ROW])
        tT = sb("tT", [P, S])
        logits = sb("logits", [P, QT, EXPERTS])
        top8 = sb("top8", [P, QT, 8])
        idx8 = sb("idx8", [P, QT, 8], U32)
        idx_f = sb("idx_f", [P, QT, TOP])
        chosen = sb("chosen", [P, TOP, QT, EXPERTS])
        chosen_b = sb("chosen_b", [P, 2, QT, EXPERTS], BF16)
        before = sb("before", [P, 2, QT, EXPERTS], BF16)
        gap = sb("gap", [P, QT])
        gap_e = sb("gap_e", [P, QT])
        gap_s = sb("gap_s", [P, QT])
        place = sb("place", [P, 16])
        place_c = sb("place_c", [P, TOP, 16])
        slot_f = sb("slot_f", [P, TOP * QT])
        slot = sb("slot", [P, 2, TOP * QT], U32)

        cnt = sb("cnt", [P, EXPERTS])
        tile_gt = sb("tile_gt", [P, EXPERTS, 16])
        n_tiles = sb("n_tiles", [P, EXPERTS])
        tile_lo = sb("tile_lo", [P, EXPERTS, EXPERTS])
        tile_end = sb("tile_end", [P, EXPERTS])
        past = sb("past", [P, TILES, EXPERTS])
        past_n = sb("past_n", [P, TILES, EXPERTS])
        tile_e = sb("tile_e", [P, TILES])
        tile_s = sb("tile_s", [P, TILES])
        tile_w = sb("tile_w", [P, 2, TILES])
        tile_row = sb("tile_row", [P, 2, TILES])
        table = sb("table", [P, 3, TILES], I32)
        pad_f = sb("pad_f", [P, EXPERTS])
        pad_at = sb("pad_at", [P, EXPERTS], I32)
        rows_in = sb("rows_in", [P, 2, ROW])
        w_now = sb("w_now", [P, 2, 2 * INTER])
        rT = sb("rT", [P, 2, P])
        silu = sb("silu", [P, 2, INTER])
        hidT = sb("hidT", [P, 2, INTER])
        dest = sb("dest", [P, 2], U32)
        weight = sb("weight", [P, 2])
        res = sb("res", [P, 2, D])
        ya = sb("ya", [P, 2, TOP, QT, D])
        o1 = sb("o1", [P, 2, QT, D])
        o2 = sb("o2", [P, 2, QT, D])
        o_st = sb("o_st", [P, 2, QT, 6])
        o_mv = sb("o_mv", [P, 2, QT, 2])
        o_ve = sb("o_ve", [P, 2, QT])
        o_r = sb("o_r", [P, 2, QT])
        on = sb("on", [P, 2, QT, D])
        x3 = sb("x3", [P, 2, QT, D])

        ps = [bank(f"ps{i}") for i in range(8)]
        ps_max, ps_exp, ps_pv, ps_a, ps_c = ps[0:2], ps[2:4], ps[4:6], ps[6], ps[7]
        ps_gate, ps_up, ps_rT, ps_res = ps[0:2], ps[2:4], ps[4:6], ps[6:8]

        s_cst, s_wqk, s_wvo, s_wffn = sem("consts_in"), sem("wqk_in"), sem("small_weights_in"), sem("ffn_weights_in")
        s_xin = [sem("x_in_0"), sem("x_in_1"), sem("x_in_rest")]
        s_const_b, s_stack_ones, s_vzero, s_rows0 = sem("bf16_consts"), sem("stack_ones"), sem("v_ones"), sem("rows_cleared")
        s_xst, s_xmv, s_xve, s_xr = sem("x_stats"), sem("x_mean_var"), sem("x_var_eps"), sem("x_rstd")
        s_xn, s_xnT_ps, s_xnT = sem("x_normed"), sem("xT_in_psum"), sem("xT_in_sbuf")
        s_qk_ps, s_hi, s_rest, s_mid, s_lo = sem("qk_in_psum"), sem("high_part"), sem("rest_after_high"), sem("middle_part"), sem("low_part")
        s_stack = [[sem(f"stack_in_{p}{f}") for f in range(2)] for p in range(2)]
        s_v_ps, s_v = sem("v_in_psum"), sem("v_in_sbuf")
        s_smax_ps, s_smax = sem("max_scores_in_psum"), sem("max_found")
        s_sh_hi, s_sh, s_shT_ps, s_shT = sem("shift_high"), sem("shift_low"), sem("shiftT_in_psum"), sem("shiftT_in_sbuf")
        s_shin = [sem("shift_rows_in_0"), sem("shift_rows_in_1")]
        s_sexp_ps, s_exp, s_pv = sem("exp_scores_in_psum"), sem("probs_ready"), sem("pv_group_done")
        s_u = sem("pv_bank_copied")
        s_uT, s_den, s_ctx = sem("ctx_tile_in_psum"), sem("denominators_inverted"), sem("ctx_tile_ready")
        s_ctxT_ps, s_ctxT, s_y_ps, s_y = sem("ctxT_in_psum"), sem("ctxT_in_sbuf"), sem("y_in_psum"), sem("y_in_sbuf")
        s_yst, s_ymv, s_yve, s_yr, s_yn, s_x2 = sem("y_stats"), sem("y_mean_var"), sem("y_var_eps"), sem("y_rstd"), sem("y_normed"), sem("x2_ready")
        s_zst, s_zmv, s_zve, s_zr, s_z, s_zn = sem("x2_stats"), sem("x2_mean_var"), sem("x2_var_eps"), sem("x2_rstd"), sem("z_ready"), sem("z_normed")
        s_znT_ps, s_znT, s_aw_ps, s_h = sem("znT_in_psum"), sem("znT_in_sbuf"), sem("attn_w_in_psum"), sem("h_ready")
        s_hst, s_hmv, s_hve, s_hr, s_hn = sem("h_stats"), sem("h_mean_var"), sem("h_var_eps"), sem("h_rstd"), sem("h_normed")
        s_tT_ps, s_tT, s_lg_ps, s_lg = sem("tT_in_psum"), sem("tT_in_sbuf"), sem("logits_in_psum"), sem("logits_in_sbuf")
        s_top, s_idx, s_idxf, s_oh, s_chb, s_bef = sem("top_values"), sem("top_indices"), sem("indices_as_float"), sem("one_hots"), sem("chosen_bf16"), sem("counts_before")
        s_gap, s_gape, s_gaps, s_w0, s_w1 = sem("logit_gap"), sem("gap_exp"), sem("gap_sum"), sem("weight_0"), sem("weight_1")
        s_pl_ps, s_pl, s_plc, s_sf, s_slot = sem("places_in_psum"), sem("places_in_sbuf"), sem("places_masked"), sem("slots_as_float"), sem("slots_ready")
        s_hn2, s_dst = sem("rows_copied"), sem("destinations_written")
        s_scat = [sem("rows_scattered_0"), sem("rows_scattered_1")]
        s_cnt_ps, s_tab = sem("counts_in_psum"), sem("table_step")
        s_pad = sem("padding_written")
        s_rin = [sem("rows_in_0"), sem("rows_in_1")]
        s_wn, s_rT_ps, s_rT = sem("expert_weights_placed"), sem("rowsT_in_psum"), sem("rowsT_in_sbuf")
        s_gate, s_up, s_silu, s_hid = sem("gate_in_psum"), sem("up_in_psum"), sem("silu_ready"), sem("hidden_ready")
        s_res_ps, s_aux, s_res = sem("result_in_psum"), sem("weight_and_destination"), sem("result_ready")
        s_ysc = [sem("results_scattered_0"), sem("results_scattered_1")]
        s_ya = [sem("results_in_0"), sem("results_in_1")]
        s_o1, s_o2, s_ost, s_omv, s_ove, s_or, s_on, s_x3 = (sem("h_plus_first"), sem("ffn_out"), sem("ffn_stats"), sem("ffn_mean_var"),
                                                            sem("ffn_var_eps"), sem("ffn_rstd"), sem("ffn_normed"), sem("x3_ready"))
        s_out = [sem("out_written_0"), sem("out_written_1")]

        block = ctx.enter_context(nc.Block())

        def tiles_of(b):
            return at(b.n * QT, QT)

        def tile_at(b, t):
            return at(b.n * QT + t)

        def wait(eng, s, value, own=False):
            if not isinstance(value, int) or value > 0:
                eng.wait_ge(s, value)
                if own and not isinstance(value, int):
                    eng.nop(nofuse=True)

        def pipeline(eng, step):
            step(fixed(-1), a=True, m=True, e=False, c=False, first=True)
            step(fixed(0), a=True, m=True, e=True, c=False)
            with eng.Fori(0, (NB - 4) // 2) as i:
                step(Batch(i * 2 + 1, 1, i), a=True, m=True, e=True, c=True)
                step(Batch(i * 2 + 2, 0, i + 1), a=True, m=True, e=True, c=True)
            step(fixed(NB - 3), a=True, m=True, e=True, c=True)
            step(fixed(NB - 2), a=False, m=True, e=True, c=True)
            step(fixed(NB - 1), a=False, m=False, e=True, c=True)
            step(fixed(NB), a=False, m=False, e=False, c=True)

        def tiles(eng, body):
            body(fixed(0), first=True)
            body(fixed(1))
            with eng.Fori(1, TILES // 2 - 1) as i:
                body(Batch(i * 2, 0, i))
                body(Batch(i * 2 + 1, 1, i))
            body(fixed(TILES - 2))
            body(fixed(TILES - 1), last=True)

        def batches(eng, body):
            body(fixed(0))
            body(fixed(1))
            with eng.Fori(1, NB // 2) as i:
                body(Batch(i * 2, 0, i))
                body(Batch(i * 2 + 1, 1, i))

        def at(n, k=1):
            return slice(n, n + k) if isinstance(n, int) else bass.ds(n, k)

        def x_arrived(eng, b):
            if isinstance(b.n, int) and b.n < 2:
                eng.wait_ge(s_xin[b.n], 16)
            else:
                eng.wait_ge(s_xin[2], 16)

        @block.sync
        def _(sp):
            sp.dma_start(x_sb[:, 0:QT, :], x[0].rearrange("(t p) d -> p t d", p=P)).then_inc(s_xin[0], 16)
            sp.dma_start(cst[:, :], consts).then_inc(s_cst, 16)
            sp.dma_start(wqk_sb[:, :, :], wqk).then_inc(s_wqk, 16)
            sp.dma_start(x_sb[:, QT:2 * QT, :], x[1].rearrange("(t p) d -> p t d", p=P)).then_inc(s_xin[1], 16)
            sp.dma_start(wv_sb[:, :], wv).then_inc(s_wvo, 16)
            sp.dma_start(wo_sb[:, :], wo).then_inc(s_wvo, 16)
            sp.dma_start(attn_w_sb[:, :], attn_w).then_inc(s_wvo, 16)
            sp.dma_start(gate_w_sb[:, :], gate_w).then_inc(s_wvo, 16)
            sp.dma_start(norms_sb[:, :], norms).then_inc(s_wvo, 16)
            sp.dma_start(x_sb[:, 2 * QT:NT, :], x[2:NB].rearrange("b (t p) d -> p (b t) d", p=P)).then_inc(s_xin[2], 16)

            def stack(b, f):
                wait(sp, s_lo, b.n + 1, own=True)
                wait(sp, s_sexp_ps, (b.n - 2) * HEADS + 8 * f + 8, own=True)
                for dst, w, runs in ((q_stack, 0, ((0, 3, 0, 0), (3, 2, 1, 0), (5, 1, 2, 0))),
                                     (k_stack, 1, ((0, 3, 0, 1), (3, 2, 0, 1), (5, 1, 0, 1)))):
                    for side in range(2):
                        for r0, nr, part, step in runs:
                            for r in range(r0, r0 + nr):
                                sp.dma_start(
                                    dst[64 * side + HD * r:64 * side + HD * (r + 1), b.parity, 4 * f:4 * f + 4, :],
                                    parts[64 * side + 32 * f:64 * side + 32 * (f + 1), b.parity,
                                          part + step * (r - r0), w, :]
                                ).then_inc(s_stack[b.parity][f], 16)

            def shift_rows(b, f):
                wait(sp, s_shT, 2 * b.n + f + 1, own=True)
                for side in range(2):
                    sp.dma_start(q_stack[64 * side + STACK:64 * side + STACK + SHIFT_ROWS, b.parity, 4 * f:4 * f + 4, :],
                                 shiftT[8 * side:8 * side + 8, f, :]).then_inc(s_shin[f], 16)

            def step(s, a, m, e, c, first=False):
                if first:
                    stack(s.plus(1), 0)
                    stack(s.plus(1), 1)
                if e:
                    shift_rows(s, 1)
                if a:
                    stack(s.plus(2), 0)
                if m:
                    shift_rows(s.plus(1), 0)
                if a:
                    stack(s.plus(2), 1)
                if first:
                    sp.dma_start(gate_up_sb[:, :], gate_up).then_inc(s_wffn, 16)
                    sp.dma_start(down_sb[:, :], down).then_inc(s_wffn, 16)

            sp.wait_ge(s_stack_ones, 2)
            pipeline(sp, step)

            sp.wait_ge(s_tab, TABLE_STEPS)
            for s_ in s_scat:
                sp.wait_ge(s_, NB // 2 * TOP * QT * 16)
            for e_ in range(EXPERTS):
                row = sp.value_load(pad_at[0:1, e_:e_ + 1], min_val=0, max_val=EXPERTS * REGION - P)
                sp.dma_start(xs[bass.ds(row, P), :], cst[:, C_PAD:C_PAD + ROW]).then_inc(s_pad, 16)
            sp.dma_start(xs[EXPERTS * REGION:EXPERTS * REGION + P, :], cst[:, C_PAD:C_PAD + ROW]).then_inc(s_pad, 16)
            sp.wait_ge(s_pad, 16 * (EXPERTS + 1))

            def load_rows(t, first=False, last=False):
                row = sp.value_load(table[0:1, 0, at(t.n)], min_val=0, max_val=EXPERTS * REGION)
                wait(sp, s_rT_ps, t.n - 1, own=True)
                wait(sp, s_aux, t.n - 1, own=True)
                sp.dma_start(rows_in[:, t.parity, :], xs[bass.ds(row, P), :]).then_inc(s_rin[t.parity], 16)

            tiles(sp, load_rows)

            for s_ in s_ysc:
                sp.wait_ge(s_, TILES // 2 * 16)
            ys_v = ys.rearrange("(c b t p) d -> b p c t d", c=TOP, t=QT, p=P)
            out_v = out.rearrange("b (t p) d -> b p t d", p=P)

            def load(n, p):
                for c in range(TOP):
                    sp.dma_start(ya[:, p, c, :, :], ys_v[at(n), :, c, :, :].rearrange("b p t d -> (b p) t d")).then_inc(s_ya[p], 16)

            def store(b):
                wait(sp, s_x3, b.n + 1, own=True)
                sp.dma_start(out_v[at(b.n)].rearrange("b p t d -> (b p) t d"), x3[:, b.parity]).then_inc(s_out[b.parity], 16)

            load(0, 0)
            load(1, 1)
            with sp.Fori(0, NB // 2 - 1) as i:
                for p in range(2):
                    store(Batch(i * 2 + p, p, i))
                    load(i * 2 + (p + 2), p)
            store(fixed(NB - 2))
            store(fixed(NB - 1))
            for p in range(2):
                sp.wait_ge(s_out[p], 16 * (NB // 2))

        @block.tensor
        def _(pe):
            def shift_T(b, f, before_this):
                pe.wait_ge(s_sh, 2 * b.n + f + 1)
                before_this()
                for t in range(QT):
                    last = nc.tensor.transpose(ps_a[0:16, t * 64:t * 64 + 64].bitcast(BF16),
                                               shift[:, f, t].rearrange("p a b c -> p (a b c)"), ident_b[:, :])
                last.then_inc(s_shT_ps, 1)

            def x_T(b, before_this):
                wait(pe, s_xn, QT * b.n + QT)
                before_this()
                for t in range(QT):
                    last = nc.tensor.transpose(ps_a[:, t * P:t * P + P], xn[:, t, :], ident)
                last.then_inc(s_xnT_ps, 1)

            def project_qk(b):
                wait(pe, s_xnT, b.n + 1)
                for w in range(2):
                    last = nc.tensor.matmul(ps_a[:, w * S:w * S + S], wqk_sb[:, w, :], xnT[:, b.parity, :], start=True, stop=True)
                last.then_inc(s_qk_ps, 1)

            def project_v(b, before_this):
                before_this()
                for t in range(QT):
                    last = nc.tensor.matmul(ps_a[:, t * P:t * P + P], xnT[:, b.parity, t * P:t * P + P], wv_sb[:, :], start=True, stop=True)
                last.then_inc(s_v_ps, 1)

            def max_scores(b, h):
                pair, side = h // 2, h % 2
                if h % 8 == 0:
                    pe.wait_ge(s_stack[b.parity][h // 8], 16 * 24 * (b.pair + 1))
                wait(pe, s_smax, b.n * HEADS + h - 1)
                for t in range(QT):
                    last = nc.tensor.matmul(ps_max[h % 2][:, t * S:t * S + S],
                                            q_stack[64 * side:64 * side + STACK, b.parity, pair, t * P:t * P + P],
                                            k_stack[64 * side:64 * side + STACK, b.parity, pair, :], start=True, stop=True)
                last.then_inc(s_smax_ps, 1)

            def exp_scores(b, h):
                pair, side = h // 2, h % 2
                k = STACK + SHIFT_ROWS
                if h % 8 == 0:
                    pe.wait_ge(s_shin[h // 8], 32 * b.n + 32)
                wait(pe, s_exp, b.n * HEADS + h - 1)
                for t in range(QT):
                    last = nc.tensor.matmul(ps_exp[h % 2][:, t * S:t * S + S],
                                            k_stack[64 * side:64 * side + k, b.parity, pair, t * P:t * P + P],
                                            q_stack[64 * side:64 * side + k, b.parity, pair, :], start=True, stop=True)
                last.then_inc(s_sexp_ps, 1)

            def pv(b, g):
                if g == 0:
                    wait(pe, s_v, b.n + 1)
                pe.wait_ge(s_exp, b.n * HEADS + 4 * g + 4)
                if g % 2 == 0:
                    wait(pe, s_u, 2 * b.n - 2 + g // 2 + 1)
                for t in range(QT):
                    for j in range(4):
                        h = 4 * g + j
                        last = nc.tensor.matmul(ps_pv[g // 2][32 * j:32 * j + 32, (g % 2) * S:(g % 2) * S + S],
                                                v_aug[:, b.parity, t, h, :], probs[:, h % 8, t, :],
                                                start=(t == 0), stop=(t == QT - 1))
                last.then_inc(s_pv, 1)

            def ctx_tile(b, t):
                if t == 0:
                    wait(pe, s_u, 2 * b.n + 2)
                    if isinstance(b.n, int):
                        wait(pe, s_pl, b.n)
                else:
                    wait(pe, s_ctx, 2 * b.n + 1)
                for g in range(4):
                    last = nc.tensor.transpose(ps_c[:, g * P:g * P + P], u_sb[:, g, t * P:t * P + P], ident)
                last.then_inc(s_uT, 1)

            def ctx_T(b):
                wait(pe, s_ctx, 2 * b.n + 2)
                for t in range(QT):
                    last = nc.tensor.transpose(ps_c[:, t * P:t * P + P], ctx_sb[:, t, :], ident)
                last.then_inc(s_ctxT_ps, 1)

            def two_tiles(b, ready, value, act, w, n, done):
                wait(pe, ready, value)
                for t in range(QT):
                    last = nc.tensor.matmul(ps_c[:, t * n:t * n + n], act[:, t * P:t * P + P], w, start=True, stop=True)
                last.then_inc(done, 1)

            def zn_T(b):
                wait(pe, s_zn, 2 * b.n + 2)
                for t in range(QT):
                    last = nc.tensor.transpose(ps_c[:, t * P:t * P + P], zn[:, t, :], ident)
                last.then_inc(s_znT_ps, 1)

            def h_T(b):
                wait(pe, s_hn, 2 * b.n + 2)
                for t in range(QT):
                    last = nc.tensor.transpose(ps_c[:, t * P:t * P + P], rows[:, b.parity, t, 0, 0:P], ident)
                last.then_inc(s_tT_ps, 1)

            def places(b):
                wait(pe, s_bef, 2 * b.n + 3)
                nc.tensor.matmul(ps_c[:, 0:16], upper_b[:, :], chosen_b[:, b.parity].rearrange("p t e -> p (t e)"), start=True, stop=False)
                nc.tensor.matmul(ps_c[:, 0:16], ones_b[:, :], before[:, b.parity].rearrange("p t e -> p (t e)"),
                                 start=False, stop=True).then_inc(s_pl_ps, 1)

            def step(s, a, m, e, c, first=False):
                A, M, C = s.plus(2), s.plus(1), s.plus(-1)
                nothing = lambda: None
                if first:
                    x_T(M, nothing)
                    project_qk(M)
                for h in range(HEADS):
                    if h == 0 and e:
                        shift_T(s, 1, lambda: (wait(pe, s_v, s.n + 1), wait(pe, s_shT, 2 * s.n + 1)))
                    if m:
                        max_scores(M, h)
                    if e:
                        exp_scores(s, h)
                    if h == 1 and c:
                        pv(C, 3)
                    if h == 2 and a:
                        x_T(A, (lambda: wait(pe, s_shT, 2 * s.n + 2)) if e else (lambda: wait(pe, s_rest, M.n + 1)))
                    if h == 3 and c:
                        ctx_tile(C, 0)
                    if h == 4 and c:
                        ctx_tile(C, 1)
                    if h == 5 and e:
                        pv(s, 0)
                    if h == 5 and a:
                        project_qk(A)
                    if h == 6 and c:
                        ctx_T(C)
                    if h == 7 and c:
                        two_tiles(C, s_ctxT, C.n + 1, ctxT, wo_sb[:, :], P, s_y_ps)
                    if h == 8 and m:
                        project_v(M, (lambda: wait(pe, s_rest, A.n + 1)) if a else (lambda: wait(pe, s_shT, 2 * s.n + 2)))
                    if h == 9 and e:
                        pv(s, 1)
                    if h == 9 and m:
                        shift_T(M, 0, lambda: wait(pe, s_v, M.n + 1))
                    if h == 11 and c:
                        zn_T(C)
                    if h == 12 and c:
                        two_tiles(C, s_znT, C.n + 1, znT, attn_w_sb[:, :], P, s_aw_ps)
                    if h == 13 and e:
                        pv(s, 2)
                    if h == 14 and c:
                        h_T(C)
                    if h == 15 and c:
                        two_tiles(C, s_tT, C.n + 1, tT, gate_w_sb[:, :], EXPERTS, s_lg_ps)
                        places(C)

            pe.wait_ge(s_cst, 16)
            pe.wait_ge(s_const_b, 3)
            pe.wait_ge(s_wqk, 16)
            pe.wait_ge(s_wvo, 16 * 5)
            pipeline(pe, step)
            pe.wait_ge(s_bef, 2 * NB + 1)
            pe.wait_ge(s_pl, NB)
            nc.tensor.matmul(ps_c[:, 0:EXPERTS], ones_b[:, :], before[:, NB % 2, 0, :], start=True, stop=True).then_inc(s_cnt_ps, 1)

            pe.wait_ge(s_tab, TABLE_STEPS)
            pe.wait_ge(s_wffn, 32)

            def rows_T(t):
                p = t.parity
                wait(pe, s_rin[p], t.pair * 16 + 16)
                wait(pe, s_rT, t.n - 1)
                nc.tensor.transpose(ps_rT[p][:, 0:P], rows_in[:, p, 0:P], ident).then_inc(s_rT_ps, 1)

            def gate_and_up(t):
                p = t.parity
                wait(pe, s_wn, t.n + 1)
                wait(pe, s_rT, t.n + 1)
                wait(pe, s_hid, t.n - 1)
                for half, (bank_, done) in enumerate(((ps_gate, s_gate), (ps_up, s_up))):
                    for k in range(IC):
                        last = nc.tensor.matmul(bank_[p][:, k * P:k * P + P],
                                                w_now[:, p, half * INTER + k * P:half * INTER + k * P + P],
                                                rT[:, p, :], start=True, stop=True)
                    last.then_inc(done, 1)

            def down_product(t):
                p = t.parity
                col = pe.value_load(table[0:1, 2, at(t.n)], min_val=0, max_val=(EXPERTS - 1) * INTER)
                wait(pe, s_hid, t.n + 1)
                wait(pe, s_res, t.n - 1)
                for k in range(IC):
                    last = nc.tensor.matmul(ps_res[p][:, 0:P], hidT[:, p, k * P:k * P + P],
                                            down_sb[:, bass.ds(col + k * P, P)], start=(k == 0), stop=(k == IC - 1))
                last.then_inc(s_res_ps, 1)

            def tile_products(t, first=False, last=False):
                if first:
                    rows_T(t)
                if not last:
                    rows_T(t.plus(1))
                gate_and_up(t)
                if not first:
                    down_product(t.plus(-1))
                if last:
                    down_product(t)

            tiles(pe, tile_products)

        @block.scalar
        def _(act):
            def x_T(b):
                wait(act, s_xnT_ps, b.n + 1)
                nc.scalar.copy(xnT[:, b.parity, :], ps_a[:, 0:S]).then_inc(s_xnT, 1)

            def high_part(b):
                wait(act, s_qk_ps, b.n + 1)
                nc.scalar.copy(parts[:, b.parity, 0, :, :].rearrange("p w t -> p (w t)"), ps_a[:, :]).then_inc(s_hi, 1)

            def v_out(b):
                wait(act, s_v_ps, b.n + 1)
                nc.scalar.copy(v_aug[:, b.parity, :, :, 0:HD],
                               ps_a[:, 0:QT * P].rearrange("p (t h d) -> p t h d", t=QT, d=HD)).then_inc(s_v, 1)

            def exps(b, h):
                pe_group = b.n * 4 + h // 4 - 1
                if h % 4 == 0:
                    wait(act, s_pv, pe_group)
                act.wait_ge(s_sexp_ps, b.n * HEADS + h + 1)
                nc.scalar.activation(probs[:, h % 8, :, :].rearrange("p t s -> p (t s)"), ps_exp[h % 2][:, :], ACT.Exp,
                                     scale=SCALE).then_inc(s_exp, 1)

            def pv_out(b, k):
                wait(act, s_pv, b.n * 4 + 2 * k + 2)
                if k == 0:
                    wait(act, s_uT, 2 * b.n)
                nc.scalar.copy(u_sb[:, 2 * k:2 * k + 2, :].rearrange("p g s -> p (g s)"), ps_pv[k][:, :]).then_inc(s_u, 1)

            def ctx_T(b):
                wait(act, s_ctxT_ps, b.n + 1)
                nc.scalar.copy(ctxT[:, :], ps_c[:, 0:S]).then_inc(s_ctxT, 1)

            def y_out(b):
                wait(act, s_y_ps, b.n + 1)
                nc.scalar.copy(y_sb[:, :, :].rearrange("p t d -> p (t d)"), ps_c[:, 0:S]).then_inc(s_y, 1)

            def affine(b, ready, dst, done, k):
                wait(act, ready, b.n + 1)
                nc.scalar.activation(dst, ps_c[:, 0:S], ACT.Identity, bias=norms_sb[:, k + 1:k + 2],
                                     scale=norms_sb[:, k:k + 1]).then_inc(done, 1)

            def gap_exp(b):
                wait(act, s_gap, b.n + 1)
                nc.scalar.activation(gap_e[:, :], gap[:, :], ACT.Exp).then_inc(s_gape, 1)

            def step(s, a, m, e, c, first=False):
                A, M, C = s.plus(2), s.plus(1), s.plus(-1)
                if first:
                    x_T(M)
                    high_part(M)
                for h in range(HEADS):
                    if e:
                        exps(s, h)
                    if h == 2 and c:
                        pv_out(C, 1)
                    if h == 3 and a:
                        x_T(A)
                    if h == 6 and a:
                        high_part(A)
                    if h == 7 and c:
                        ctx_T(C)
                    if h == 8 and c:
                        y_out(C)
                    if h == 9 and m:
                        v_out(M)
                    if h == 10 and e:
                        pv_out(s, 0)
                    if h == 12 and c:
                        affine(C, s_znT_ps, znT[:, :], s_znT, 0)
                    if h == 15 and c:
                        affine(C, s_tT_ps, tT[:, :], s_tT, 2)
                        gap_exp(C)

            act.wait_ge(s_vzero, 2)
            act.wait_ge(s_wvo, 16 * 5)
            pipeline(act, step)

            def row_T(t):
                wait(act, s_rT_ps, t.n + 1)
                wait(act, s_up, t.n - 1)
                nc.scalar.activation(rT[:, t.parity, :], ps_rT[t.parity][:, 0:P], ACT.Identity, bias=norms_sb[:, 3:4],
                                     scale=norms_sb[:, 2:3]).then_inc(s_rT, 1)

            def silu_of(t, first=False, last=False):
                if first:
                    row_T(t)
                if not last:
                    row_T(t.plus(1))
                wait(act, s_gate, t.n + 1)
                wait(act, s_hid, t.n - 1)
                nc.scalar.activation(silu[:, t.parity, :], ps_gate[t.parity][:, :], ACT.Silu).then_inc(s_silu, 1)

            tiles(act, silu_of)

        @block.vector
        def _(dve):
            def stats(b, src, st, mv, s_st, s_mv):
                for t in range(QT):
                    nc.vector.bn_stats(st[:, t, :], src(t)).then_inc(s_st, 1)
                wait(dve, s_st, 2 * b.n + 2, own=True)
                for t in range(QT):
                    nc.vector.bn_aggr(mv[:, t, :], st[:, t, :]).then_inc(s_mv, 1)

            def normed(b, src, dst, mv, r, s_r, value, done):
                wait(dve, s_r, value)
                for t in range(QT):
                    nc.vector.tensor_scalar(dst(t), src(t), mv[:, t, 0:1], r[:, t:t + 1], ALU.subtract, ALU.mult).then_inc(done, 1)

            def x_stats(b):
                x_arrived(dve, b)
                stats(b, lambda t: x_sb[:, tile_at(b, t), :], x_st, x_mv, s_xst, s_xmv)

            def x_normed(b):
                wait(dve, s_xnT_ps, b.n)
                normed(b, lambda t: x_sb[:, tile_at(b, t), :], lambda t: xn[:, t, :], x_mv, x_r, s_xr, b.n + 1, s_xn)

            def rest_of(b):
                wait(dve, s_hi, b.n + 1)
                wait(dve, s_lo, b.n)
                nc.vector.tensor_tensor(rest1[:, :, :].rearrange("p w t -> p (w t)"), ps_a[:, :],
                                        parts[:, b.parity, 0, :, :].rearrange("p w t -> p (w t)"), ALU.subtract).then_inc(s_rest, 1)

            def take_max(b, h):
                f, pair, side = h // 8, (h % 8) // 2, h % 2
                dve.wait_ge(s_smax_ps, b.n * HEADS + h + 1)
                col = 8 * f + 4 * side + pair
                nc.vector.tensor_reduce(neg_max[:, b.parity, :, col:col + 1],
                                        ps_max[h % 2][:, :].rearrange("p (t k) -> p t k", t=QT), AX.X, ALU.max,
                                        negate=True).then_inc(s_smax, 1)

            def shifts(b, f):
                wait(dve, s_smax, b.n * HEADS + 8 * f + 8)
                if f == 0:
                    wait(dve, s_shT_ps, 2 * b.n - 1)
                src = neg_max[:, b.parity, :, 8 * f:8 * f + 8].rearrange("p t (a c) -> p t a c", a=2)
                nc.vector.tensor_copy(shift[:, f, :, :, 0, :], src).then_inc(s_sh_hi, 1)
                wait(dve, s_sh_hi, 2 * b.n + f + 1)
                nc.vector.tensor_tensor(shift[:, f, :, :, 1, :], src, shift[:, f, :, :, 0, :], ALU.subtract).then_inc(s_sh, 1)

            def shift_out(b, f):
                wait(dve, s_shT_ps, 2 * b.n + f + 1)
                wait(dve, s_shin[f], 32 * b.n)
                nc.vector.tensor_copy(shiftT[:, f, :], ps_a[0:16, 0:128].bitcast(BF16)).then_inc(s_shT, 1)

            def ctx_tile(b, t):
                wait(dve, s_uT, 2 * b.n + t + 1)
                u = ps_c[:, :].rearrange("p (h r) -> p h r", r=32)
                nc.vector.reciprocal(den_r[:, t, :], u[:, :, HD:HD + 1].rearrange("p h r -> p (h r)")).then_inc(s_den, 1)
                wait(dve, s_den, 2 * b.n + t + 1)
                nc.vector.tensor_tensor(ctx_sb[:, t, :].rearrange("p (h d) -> p h d", d=HD), u[:, :, 0:HD],
                                        den_r[:, t, :].unsqueeze(2).to_broadcast([P, HEADS, HD]), ALU.mult).then_inc(s_ctx, 1)

            def h_out(b):
                wait(dve, s_aw_ps, b.n + 1)
                nc.vector.tensor_tensor(h_sb[:, tiles_of(b), :], ps_c[:, 0:S].rearrange("p (t d) -> p t d", t=QT), z[:, :, :],
                                        ALU.add).then_inc(s_h, 1)
                wait(dve, s_h, b.n + 1, own=True)

            def route(b):
                wait(dve, s_lg_ps, b.n + 1)
                nc.vector.tensor_copy(logits[:, :, :].rearrange("p t e -> p (t e)"), ps_c[:, 0:QT * EXPERTS]).then_inc(s_lg, 1)
                wait(dve, s_lg, b.n + 1, own=True)
                for t in range(QT):
                    nc.vector.max(top8[:, t, :], logits[:, t, :]).then_inc(s_top, 1)
                wait(dve, s_top, 2 * b.n + 2, own=True)
                for t in range(QT):
                    nc.vector.max_index(idx8[:, t, :], top8[:, t, :], logits[:, t, :]).then_inc(s_idx, 1)
                nc.vector.tensor_tensor(gap[:, :], top8[:, :, 1], top8[:, :, 0], ALU.subtract).then_inc(s_gap, 1)
                wait(dve, s_idx, 2 * b.n + 2)
                nc.vector.tensor_copy(idx_f[:, :, :], idx8[:, :, 0:TOP]).then_inc(s_idxf, 1)
                wait(dve, s_idxf, b.n + 1)
                for k in range(TOP):
                    nc.vector.tensor_tensor(chosen[:, k, :, :], iota8, idx_f[:, :, k:k + 1].to_broadcast([P, QT, EXPERTS]),
                                            ALU.is_equal).then_inc(s_oh, 1)
                wait(dve, s_oh, 2 * b.n + 2)
                nc.vector.tensor_tensor(chosen_b[:, b.parity], chosen[:, 0], chosen[:, 1], ALU.add).then_inc(s_chb, 1)
                wait(dve, s_chb, b.n + 1)
                nc.vector.tensor_tensor(before[:, b.parity, 1, :], before[:, b.parity, 0, :], chosen_b[:, b.parity, 0, :],
                                        ALU.add).then_inc(s_bef, 1)
                wait(dve, s_bef, 2 * b.n + 2)
                nc.vector.tensor_tensor(before[:, 1 - b.parity, 0, :], before[:, b.parity, 1, :], chosen_b[:, b.parity, 1, :],
                                        ALU.add).then_inc(s_bef, 1)
                wait(dve, s_gape, b.n + 1)
                nc.vector.tensor_scalar(gap_s[:, :], gap_e[:, :], 1.0, None, ALU.add).then_inc(s_gaps, 1)
                wait(dve, s_gaps, b.n + 1)
                nc.vector.reciprocal(rows[:, b.parity, :, 0, P], gap_s[:, :]).then_inc(s_w0, 1)
                wait(dve, s_w0, b.n + 1)
                nc.vector.tensor_tensor(rows[:, b.parity, :, 1, P], gap_e[:, :], rows[:, b.parity, :, 0, P], ALU.mult).then_inc(s_w1, 1)

            def slots(b):
                wait(dve, s_pl_ps, b.n + 1)
                nc.vector.tensor_tensor(place[:, :], ps_c[:, 0:16], region_base, ALU.add).then_inc(s_pl, 1)
                wait(dve, s_pl, b.n + 1)
                nc.vector.tensor_tensor(place_c[:, :, :], chosen[:, :, :, :].rearrange("p c t e -> p c (t e)"),
                                        place[:, :].unsqueeze(1).to_broadcast([P, TOP, 16]), ALU.mult).then_inc(s_plc, 1)
                wait(dve, s_plc, b.n + 1)
                nc.vector.tensor_reduce(slot_f[:, :], place_c[:, :, :].rearrange("p c (t e) -> p (c t) e", e=EXPERTS), AX.X,
                                        ALU.add).then_inc(s_sf, 1)
                wait(dve, s_sf, b.n + 1)
                nc.vector.tensor_copy(slot[:, b.parity, :], slot_f[:, :]).then_inc(s_slot, 1)

            def step(s, a, m, e, c, first=False):
                A, M, C = s.plus(2), s.plus(1), s.plus(-1)
                if first:
                    x_stats(M)
                    x_normed(M)
                    rest_of(M)
                for h in range(HEADS):
                    if h == 0 and e:
                        shifts(s, 1)
                    if m:
                        take_max(M, h)
                    if h == 0 and a:
                        x_stats(A)
                    if h == 1 and e:
                        shift_out(s, 1)
                    if h == 1 and a:
                        x_normed(A)
                    if h == 4 and c:
                        ctx_tile(C, 0)
                    if h == 5 and c:
                        ctx_tile(C, 1)
                    if h == 7 and a:
                        rest_of(A)
                    if h == 7 and m:
                        shifts(M, 0)
                    if h == 9 and c:
                        wait(dve, s_y, C.n + 1, own=True)
                        stats(C, lambda t: y_sb[:, t, :], y_st, y_mv, s_yst, s_ymv)
                        normed(C, lambda t: y_sb[:, t, :], lambda t: yn[:, t, :], y_mv, y_r, s_yr, C.n + 1, s_yn)
                    if h == 10 and m:
                        shift_out(M, 0)
                    if h == 10 and c:
                        wait(dve, s_x2, C.n + 1, own=True)
                        stats(C, lambda t: x2_sb[:, tile_at(C, t), :], z_st, z_mv, s_zst, s_zmv)
                    if h == 11 and c:
                        normed(C, lambda t: x2_sb[:, tile_at(C, t), :], lambda t: zn[:, t, :], z_mv, z_r[:, 1, :], s_zr, C.n + 1, s_zn)
                        normed(C, lambda t: x2_sb[:, tile_at(C, t), :], lambda t: z[:, t, :], z_mv, z_r[:, 0, :], s_zr, C.n + 1, s_z)
                    if h == 13 and c:
                        wait(dve, s_z, 2 * C.n + 2)
                        h_out(C)
                        stats(C, lambda t: h_sb[:, tile_at(C, t), :], h_st, h_mv, s_hst, s_hmv)
                    if h == 14 and c:
                        normed(C, lambda t: h_sb[:, tile_at(C, t), :], lambda t: rows[:, C.parity, t, 0, 0:P], h_mv, h_r, s_hr, C.n + 1, s_hn)
                    if h == 15 and c:
                        route(C)
                        slots(C)

            dve.wait_ge(s_cst, 16)
            nc.vector.tensor_copy(ident_b[:, :], ident).then_inc(s_const_b, 1)
            nc.vector.tensor_copy(upper_b[:, :], cst[:, C_UPPER:C_UPPER + P]).then_inc(s_const_b, 1)
            nc.vector.tensor_copy(ones_b[:, :], cst[:, C_ONES:C_ONES + P]).then_inc(s_const_b, 1)
            nc.vector.memset(before[:, :, :, :], 0.0).then_inc(s_bef, 1)
            dve.wait_ge(s_bef, 1)
            dve.wait_ge(s_rows0, 2)
            pipeline(dve, step)

            steps = [0]

            def link(instruction):
                steps[0] += 1
                instruction.then_inc(s_tab, 1)
                dve.wait_ge(s_tab, steps[0])

            def row_of(column, n):
                return cst[:, column:column + n]

            tri = row_of(C_LOWER, EXPERTS * EXPERTS).rearrange("p (a b) -> p a b", b=EXPERTS)
            dve.wait_ge(s_cnt_ps, 1)
            link(nc.vector.tensor_copy(cnt[:, :], ps_c[:, 0:EXPERTS]))
            link(nc.vector.tensor_tensor(tile_gt[:, :, :], cnt[:, :].unsqueeze(2).to_broadcast([P, EXPERTS, 16]),
                                         row_of(C_STEP, 16).unsqueeze(1).to_broadcast([P, EXPERTS, 16]), ALU.is_gt))
            link(nc.vector.tensor_reduce(n_tiles[:, :], tile_gt[:, :, :], AX.X, ALU.add))
            link(nc.vector.tensor_tensor(tile_lo[:, :, :], n_tiles[:, :].unsqueeze(1).to_broadcast([P, EXPERTS, EXPERTS]), tri, ALU.mult))
            link(nc.vector.tensor_reduce(tile_end[:, :], tile_lo[:, :, :], AX.X, ALU.add))
            link(nc.vector.tensor_tensor(past[:, :, :], row_of(C_TILE, TILES).unsqueeze(2).to_broadcast([P, TILES, EXPERTS]),
                                         tile_end[:, :].unsqueeze(1).to_broadcast([P, TILES, EXPERTS]), ALU.is_ge))
            link(nc.vector.tensor_tensor(past_n[:, :, :], past[:, :, :], n_tiles[:, :].unsqueeze(1).to_broadcast([P, TILES, EXPERTS]),
                                         ALU.mult))
            link(nc.vector.tensor_reduce(tile_e[:, :], past[:, :, :], AX.X, ALU.add))
            link(nc.vector.tensor_reduce(tile_s[:, :], past_n[:, :, :], AX.X, ALU.add))
            link(nc.vector.tensor_tensor(tile_row[:, 0, :], row_of(C_TILE, TILES), tile_s[:, :], ALU.subtract))
            link(nc.vector.tensor_scalar(tile_w[:, 1, :], tile_e[:, :], EXPERTS - 0.5, float(P), ALU.is_lt, ALU.mult))
            link(nc.vector.tensor_tensor(tile_row[:, 1, :], tile_row[:, 0, :], tile_w[:, 1, :], ALU.mult))
            link(nc.vector.scalar_tensor_tensor(table[:, 0, :], tile_e[:, :], float(REGION), tile_row[:, 1, :], ALU.mult, ALU.add))
            link(nc.vector.tensor_scalar(table[:, 1, :], tile_e[:, :], float(EXPERTS - 1), float(2 * INTER), ALU.min, ALU.mult))
            link(nc.vector.tensor_scalar(table[:, 2, :], tile_e[:, :], float(EXPERTS - 1), float(INTER), ALU.min, ALU.mult))
            link(nc.vector.tensor_tensor(pad_at[:, :], cnt[:, :], region_base[:, 0:EXPERTS], ALU.add))
            assert steps[0] == TABLE_STEPS

            def aux(t):
                p = t.parity
                wait(dve, s_rin[p], t.pair * 16 + 16)
                wait(dve, s_ysc[p], t.pair * 16)
                nc.vector.tensor_copy(dest[:, p:p + 1], rows_in[:, p, P + 1:P + 2])
                nc.vector.tensor_copy(weight[:, p:p + 1], rows_in[:, p, P:P + 1]).then_inc(s_aux, 1)

            def hidden(t):
                p = t.parity
                wait(dve, s_silu, t.n + 1)
                wait(dve, s_up, t.n + 1)
                wait(dve, s_res_ps, t.n - 1)
                nc.vector.tensor_tensor(hidT[:, p, :], ps_up[p][:, :], silu[:, p, :], ALU.mult).then_inc(s_hid, 1)

            def result(t):
                p = t.parity
                wait(dve, s_aux, t.n + 1)
                wait(dve, s_res_ps, t.n + 1)
                nc.vector.tensor_scalar(res[:, p, :], ps_res[p][:, 0:P], weight[:, p:p + 1], None, ALU.mult).then_inc(s_res, 1)

            def tile_elementwise(t, first=False, last=False):
                aux(t)
                hidden(t)
                if not first:
                    result(t.plus(-1))
                if last:
                    result(t)

            tiles(dve, tile_elementwise)

            def add_and_norm(b):
                n, p = b.n, b.parity
                dve.wait_ge(s_ya[p], b.pair * 32 + 32)
                nc.vector.tensor_tensor(o1[:, p], ya[:, p, 0], h_sb[:, tiles_of(b), :], ALU.add).then_inc(s_o1, 1)
                wait(dve, s_o1, n + 1)
                nc.vector.tensor_tensor(o2[:, p], ya[:, p, 1], o1[:, p], ALU.add).then_inc(s_o2, 1)
                wait(dve, s_o2, n + 1, own=True)
                for t in range(QT):
                    nc.vector.bn_stats(o_st[:, p, t, :], o2[:, p, t, :]).then_inc(s_ost, 1)
                wait(dve, s_ost, n * 2 + 2, own=True)
                for t in range(QT):
                    nc.vector.bn_aggr(o_mv[:, p, t, :], o_st[:, p, t, :]).then_inc(s_omv, 1)
                wait(dve, s_x3, n - 1)
                wait(dve, s_or, n + 1)
                for t in range(QT):
                    nc.vector.tensor_scalar(on[:, p, t, :], o2[:, p, t, :], o_mv[:, p, t, 0:1], o_r[:, p, t:t + 1],
                                            ALU.subtract, ALU.mult).then_inc(s_on, 1)

            batches(dve, add_and_norm)

        @block.gpsimd
        def _(pool):
            def rstd(b, mv, ve, r, s_mv, s_ve, s_r):
                wait(pool, s_mv, 2 * b.n + 2, own=True)
                nc.gpsimd.tensor_scalar(ve[:, :], mv[:, :, 1], EPS, None, ALU.add).then_inc(s_ve, 1)
                wait(pool, s_ve, b.n + 1, own=True)
                nc.gpsimd.tensor_tensor(r[:, :], ve[:, :], neg_half[:, 0:QT], ALU.pow).then_inc(s_r, 1)

            def lower_parts(b):
                wait(pool, s_rest, b.n + 1, own=True)
                nc.gpsimd.tensor_copy(parts[:, b.parity, 1, :, :], rest1[:, :, :]).then_inc(s_mid, 1)
                wait(pool, s_mid, b.n + 1, own=True)
                nc.gpsimd.tensor_tensor(parts[:, b.parity, 2, :, :], rest1[:, :, :], parts[:, b.parity, 1, :, :],
                                        ALU.subtract).then_inc(s_lo, 1)

            def x2(b):
                wait(pool, s_yn, 2 * b.n + 2, own=True)
                nc.gpsimd.tensor_tensor(x2_sb[:, tiles_of(b), :], yn[:, :, :], x_sb[:, tiles_of(b), :], ALU.add).then_inc(s_x2, 1)

            def z_rstd(b):
                wait(pool, s_zmv, 2 * b.n + 2, own=True)
                nc.gpsimd.tensor_scalar(z_ve[:, 0, :], z_mv[:, :, 1], EPS, None, ALU.add).then_inc(s_zve, 1)
                nc.gpsimd.tensor_scalar(z_ve[:, 1, :], z_mv[:, :, 1], 1.0 + EPS, EPS * EPS, ALU.mult, ALU.add).then_inc(s_zve, 1)
                wait(pool, s_zve, 2 * b.n + 2, own=True)
                nc.gpsimd.tensor_tensor(z_r[:, :, :].rearrange("p a t -> p (a t)"), z_ve[:, :, :].rearrange("p a t -> p (a t)"),
                                        neg_half[:, :], ALU.pow).then_inc(s_zr, 1)

            def copy_rows(b):
                wait(pool, s_hn, 2 * b.n + 2, own=True)
                nc.gpsimd.tensor_copy(rows[:, b.parity, :, 1, 0:P], rows[:, b.parity, :, 0, 0:P]).then_inc(s_hn2, 1)
                at = rows[:, b.parity, :, :, P + 1]
                nc.gpsimd.tensor_scalar(at, at, float(2 * S), None, ALU.add).then_inc(s_dst, 1)

            def scatter(b):
                wait(pool, s_hn2, b.n + 1, own=True)
                wait(pool, s_dst, b.n + 1, own=True)
                wait(pool, s_w1, b.n + 1, own=True)
                wait(pool, s_slot, b.n + 1, own=True)
                for k in range(TOP):
                    for t in range(QT):
                        j = k * QT + t
                        nc.gpsimd.indirect_dma_start(
                            out=xs[:, :], out_offset=bass.IndirectOffsetOnAxis(ap=slot[:, b.parity, j:j + 1], axis=0),
                            in_=rows[:, b.parity, t, k, :], in_offset=None,
                            bounds_check=EXPERTS * REGION - 1, oob_is_err=False).then_inc(s_scat[b.parity], 16)
                wait(pool, s_scat[b.parity], TOP * QT * 16 * (b.pair + 1), own=True)

            def step(s, a, m, e, c, first=False):
                A, M, C = s.plus(2), s.plus(1), s.plus(-1)
                if first:
                    rstd(M, x_mv, x_ve, x_r, s_xmv, s_xve, s_xr)
                    lower_parts(M)
                if a:
                    rstd(A, x_mv, x_ve, x_r, s_xmv, s_xve, s_xr)
                    lower_parts(A)
                if c:
                    rstd(C, y_mv, y_ve, y_r, s_ymv, s_yve, s_yr)
                    x2(C)
                    z_rstd(C)
                    rstd(C, h_mv, h_ve, h_r, s_hmv, s_hve, s_hr)
                    copy_rows(C)
                    scatter(C)

            nc.gpsimd.memset(neg_half[:, :], -0.5).then_inc(s_stack_ones, 1)
            nc.gpsimd.memset(q_stack[:, :, :, :], 1.0)
            nc.gpsimd.memset(k_stack[:, :, :, :], 1.0).then_inc(s_stack_ones, 1)
            nc.gpsimd.memset(v_aug[:, :, :, :, :], 0.0).then_inc(s_vzero, 1)
            pool.wait_ge(s_vzero, 1)
            nc.gpsimd.memset(v_aug[:, :, :, :, HD:HD + 1], 1.0).then_inc(s_vzero, 1)
            nc.gpsimd.memset(rows[:, :, :, :, :], 0.0).then_inc(s_rows0, 1)
            pool.wait_ge(s_rows0, 1)
            pool.wait_ge(s_cst, 16)
            nc.gpsimd.tensor_copy(rows[:, :, :, :, P + 1], cst[:, C_DEST:C_DEST + 8].rearrange("p (a t c) -> p a t c", a=2, t=QT)
                                  ).then_inc(s_rows0, 1)
            pool.wait_ge(s_rows0, 2)
            pool.wait_ge(s_stack_ones, 2)
            pipeline(pool, step)

            pool.wait_ge(s_tab, TABLE_STEPS)
            pool.wait_ge(s_wffn, 32)

            def place_weights(t):
                col = pool.value_load(table[0:1, 1, at(t.n)], min_val=0, max_val=(EXPERTS - 1) * 2 * INTER)
                wait(pool, s_up, t.n - 1, own=True)
                nc.gpsimd.tensor_copy(w_now[:, t.parity, :], gate_up_sb[:, bass.ds(col, 2 * INTER)]).then_inc(s_wn, 1)

            def scatter_results(t):
                p = t.parity
                wait(pool, s_res, t.n + 1, own=True)
                nc.gpsimd.indirect_dma_start(
                    out=ys[:, :], out_offset=bass.IndirectOffsetOnAxis(ap=dest[:, p:p + 1], axis=0),
                    in_=res[:, p, :], in_offset=None,
                    bounds_check=TOP * TOKENS - 1, oob_is_err=False).then_inc(s_ysc[p], 16)

            def tile_moves(t, first=False, last=False):
                place_weights(t)
                if not first:
                    scatter_results(t.plus(-1))
                if last:
                    scatter_results(t)

            tiles(pool, tile_moves)

            def finish(b):
                n, p = b.n, b.parity
                wait(pool, s_omv, n * 2 + 2, own=True)
                nc.gpsimd.tensor_scalar(o_ve[:, p, :], o_mv[:, p, :, 1], EPS, None, ALU.add).then_inc(s_ove, 1)
                wait(pool, s_ove, n + 1, own=True)
                nc.gpsimd.tensor_tensor(o_r[:, p, :], o_ve[:, p, :], neg_half[:, 0:QT], ALU.pow).then_inc(s_or, 1)
                wait(pool, s_on, n * 2 + 2, own=True)
                wait(pool, s_out[p], b.pair * 16, own=True)
                nc.gpsimd.tensor_tensor(x3[:, p], on[:, p], x2_sb[:, tiles_of(b), :], ALU.add).then_inc(s_x3, 1)

            batches(pool, finish)


def constants(np, tokens, batch, region):
    c = np.zeros((P, C_END), np.float32)
    c[:, C_IDENT:C_IDENT + P] = np.eye(P)
    c[:, C_UPPER:C_UPPER + P] = np.triu(np.ones((P, P)), 1)
    c[:, C_ONES:C_ONES + P] = 1.0
    c[:, C_IOTA:C_IOTA + 16] = np.tile(np.arange(EXPERTS), 2)
    c[:, C_REGION:C_REGION + 16] = np.tile(np.arange(EXPERTS) * region, 2)
    for parity in range(2):
        for t in range(2):
            for k in range(TOP):
                c[:, C_DEST + parity * 4 + t * 2 + k] = k * tokens + (parity - 2) * batch + t * P + np.arange(P)
    c[:, C_LOWER:C_LOWER + 64] = np.tril(np.ones((EXPERTS, EXPERTS))).reshape(-1)
    c[:, C_STEP:C_STEP + 16] = np.arange(16) * P
    c[:, C_TILE:C_TILE + C_PAD - C_TILE] = np.arange(C_PAD - C_TILE)
    c[:, C_PAD + P + 1] = TOP * tokens
    return c


def layouts(np, v):
    d = P
    heads = lambda w: w.reshape(HD, 2, HD, d).transpose(3, 1, 0, 2)
    def halves(w):
        a = heads(w)
        return a.reshape(d, 2, 2, 4, HD).transpose(0, 1, 2, 4, 3).reshape(d, d)
    wqk = np.stack([halves(v["L0_attn_w_q"]), halves(v["L0_attn_w_k"])], axis=1)
    gate = v["L0_ffn_gate_proj"].transpose(2, 0, 1)
    up = v["L0_ffn_up_proj"].transpose(2, 0, 1)
    gate_up = np.stack([gate, up], axis=2).reshape(d, -1)
    down = v["L0_ffn_down_proj"].transpose(0, 2, 1)
    down = down.reshape(EXPERTS, -1, P, d).transpose(2, 0, 1, 3).reshape(P, -1)
    norms = np.stack([v["L0_ffn_ln1_g"], v["L0_ffn_ln1_b"], v["L0_ffn_ln2_g"], v["L0_ffn_ln2_b"]], axis=1)
    x = v["L0_attn_hidden_state"]
    tokens = x.shape[0] * x.shape[1]
    return {
        "x": x, "wqk": wqk, "wv": v["L0_attn_w_v"].T, "wo": v["L0_attn_w_o"].T, "attn_w": v["L0_ffn_attn_w"].T,
        "gate_w": v["L0_ffn_gate_w"].T, "norms": norms, "gate_up": gate_up, "down": down,
        "consts": constants(np, tokens, x.shape[1], tokens + P),
    }


def kernel(**inputs):
    import numpy as np
    import concourse.bacc as bacc
    from concourse.bass_utils import run_bass_kernel_spmd

    nc = bacc.Bacc("TRN2", target_bir_lowering=False, num_devices=1)
    arrays, args = {}, []
    for name, a in layouts(np, {k: np.asarray(a) for k, a in inputs.items()}).items():
        a = np.ascontiguousarray(a)
        arrays[f"{name}_dram"] = a
        args.append(nc.dram_tensor(f"{name}_dram", a.shape, F32, kind="ExternalInput").ap())
    out = nc.dram_tensor("out_dram", inputs["L0_attn_hidden_state"].shape, F32, kind="ExternalOutput").ap()
    block_kernel(nc, *args, out)
    r = run_bass_kernel_spmd(nc, [arrays], core_ids=[0])
    return r.results[0]["out_dram"]
```

```python
from contextlib import ExitStack

import concourse.bass as bass
from concourse import mybir

P = 128
F32 = mybir.dt.float32
BF16 = mybir.dt.bfloat16
U32 = mybir.dt.uint32
I32 = mybir.dt.int32
ALU = mybir.AluOpType
ACT = mybir.ActivationFunctionType
AX = mybir.AxisListType

EPS = 1e-5
HEADS = 16
HD = 8
PARTS = 3
STACK = PARTS * PARTS * HD
SHIFT_ROWS = 2
EXPERTS = 8
TOP = 2
RING = 4
ROW = 132
C_IDENT, C_UPPER, C_ONES, C_IOTA, C_REGION, C_DEST = 0, 128, 256, 384, 400, 416
C_LOWER, C_STEP, C_TILE, C_PAD, C_END = 424, 488, 504, 544, 676


class Batch:

    def __init__(self, n, parity, pair):
        self.n, self.parity, self.pair = n, parity, pair

    def plus(self, d):
        p = self.parity + d
        return Batch(self.n + d, p % 2, self.pair + p // 2)


def fixed(n):
    return Batch(n, n % 2, n // 2)


class Tile:

    def __init__(self, n, slot, round_):
        self.n, self.slot, self.parity, self.round = n, slot, slot % 2, round_

    def plus(self, d):
        s = self.slot + d
        return Tile(self.n + d, s % RING, self.round + s // RING)


def fixed_tile(n):
    return Tile(n, n % RING, n // RING)


def block_kernel(nc, x, wqk, wv, wo, attn_w, gate_w, norms, gate_up, down, consts, out):
    NB, S, D = x.shape
    QT = S // P
    NT = NB * QT
    TOKENS = NB * S
    INTER = down.shape[1] // EXPERTS
    IC = INTER // P
    REGION = TOKENS + P
    TILES = -(-(TOP * TOKENS + EXPERTS * (P - 1)) // P)
    TILES += -TILES % RING
    SCALE = 1.0 / float(D) ** 0.5
    SCATTER = TOP * QT * 16
    TABLE_STEPS = 16
    assert D == P and QT == 2 and HEADS * HD == D

    xs = nc.dram_tensor("routed_rows", [EXPERTS * REGION + P, ROW], F32, kind="Internal").ap()
    parts_dram = nc.dram_tensor("qk_parts", [2, 2, 2, PARTS, P // 2, S], BF16, kind="Internal").ap()
    ys = nc.dram_tensor("routed_results", [TOP * TOKENS, D], F32, kind="Internal").ap()

    ctx = ExitStack()
    with ctx:
        def sb(name, shape, dt=F32):
            return ctx.enter_context(nc.sbuf_tensor(name, shape, dt))

        def bank(name):
            return ctx.enter_context(nc.psum_tensor(name, [P, 512], F32))

        def sem(name):
            return ctx.enter_context(nc.semaphore(name))

        cst = sb("cst", [P, C_END])
        ident = cst[:, C_IDENT:C_IDENT + P]
        iota8 = cst[:, C_IOTA:C_IOTA + 16].rearrange("p (t e) -> p t e", e=EXPERTS)
        region_base = cst[:, C_REGION:C_REGION + 16]
        ident_b = sb("ident_b", [P, P], BF16)
        upper_b = sb("upper_b", [P, P], BF16)
        ones_b = sb("ones_b", [P, P], BF16)
        neg_half = sb("neg_half", [P, NT])
        neg_mean = sb("neg_mean", [P, NT])
        neg_mean_y, neg_mean_z, neg_mean_h = sb("neg_mean_y", [P, QT]), sb("neg_mean_z", [P, QT]), sb("neg_mean_h", [P, QT])
        wqk_sb = sb("wqk_sb", [P, 2, P])
        wv_sb = sb("wv_sb", [P, P])
        wo_sb = sb("wo_sb", [P, P])
        attn_w_sb = sb("attn_w_sb", [P, P])
        gate_w_sb = sb("gate_w_sb", [P, EXPERTS])
        norms_sb = sb("norms_sb", [P, 4])

        x_sb = sb("x_sb", [P, NT, D])
        x2_sb = sb("x2_sb", [P, NT, D])
        h_sb = sb("h_sb", [P, NT, D])

        x_st = sb("x_st", [P, NT, 6])
        x_mv = sb("x_mv", [P, NT, 2])
        x_ve = sb("x_ve", [P, NT])
        x_rn = sb("x_rn", [P, 2, NT])
        x_now = sb("x_now", [P, 2, 2, QT])
        xn = sb("xn", [P, QT, D])
        xnT = sb("xnT", [P, 2, S])
        parts = sb("parts", [P, 2, 2, PARTS, S], BF16)
        rest1 = sb("rest1", [P, 2, S])
        stacks = sb("stacks", [P, 2, 2, HEADS, S], BF16)
        q_stack, k_stack = stacks[:, 0], stacks[:, 1]
        neg_max = sb("neg_max", [P, 2, QT, HEADS])
        shift = sb("shift", [P, 2, QT, SHIFT_ROWS, HD], BF16)
        shiftT = sb("shiftT", [16, 2, S], BF16)
        v_aug = sb("v_aug", [P, 2, QT, HEADS, 32])
        probs = sb("probs", [P, 8, QT, S])
        u_sb = sb("u_sb", [P, 4, S])
        den_r = sb("den_r", [P, QT, HEADS])
        ctx_sb = sb("ctx_sb", [P, QT, D])
        ctxT = sb("ctxT", [P, S])
        y_sb = sb("y_sb", [P, QT, D])
        y_st = sb("y_st", [P, QT, 6])
        y_mv = sb("y_mv", [P, QT, 2])
        y_ve = sb("y_ve", [P, QT])
        y_r = sb("y_r", [P, QT])
        y_nb = sb("y_nb", [P, QT])
        yn = sb("yn", [P, QT, D])
        z_st = sb("z_st", [P, QT, 6])
        z_mv = sb("z_mv", [P, QT, 2])
        z_ve = sb("z_ve", [P, 2, QT])
        z_r = sb("z_r", [P, 2, QT])
        z_nb = sb("z_nb", [P, QT])
        z = sb("z", [P, QT, D])
        zn = sb("zn", [P, QT, D])
        znT = sb("znT", [P, S])
        h_st = sb("h_st", [P, QT, 6])
        h_mv = sb("h_mv", [P, QT, 2])
        h_ve = sb("h_ve", [P, QT])
        h_r = sb("h_r", [P, QT])
        h_nb = sb("h_nb", [P, QT])
        rows = sb("rows", [P, 2, QT, TOP, ROW])
        tT = sb("tT", [P, S])
        logits = sb("logits", [P, QT, EXPERTS])
        top8 = sb("top8", [P, QT, 8])
        idx8 = sb("idx8", [P, QT, 8], U32)
        idx_f = sb("idx_f", [P, QT, TOP])
        chosen = sb("chosen", [P, TOP, QT, EXPERTS])
        chosen_b = sb("chosen_b", [P, 2, QT, EXPERTS], BF16)
        before = sb("before", [P, 2, QT, EXPERTS], BF16)
        gap = sb("gap", [P, QT])
        gap_e = sb("gap_e", [P, QT])
        gap_s = sb("gap_s", [P, QT])
        place = sb("place", [P, 16])
        place_c = sb("place_c", [P, TOP, 16])
        slot_f = sb("slot_f", [P, TOP * QT])
        slot = sb("slot", [P, 2, TOP * QT], U32)

        gate_up_sb = stacks[:, :, :, :, :].rearrange("p w a h s -> p (w a h s)").bitcast(F32)
        down_sb = sb("down_sb", [P, EXPERTS * INTER])
        cnt = sb("cnt", [P, EXPERTS])
        tile_gt = sb("tile_gt", [P, EXPERTS, 16])
        n_tiles = sb("n_tiles", [P, EXPERTS])
        tile_lo = sb("tile_lo", [P, EXPERTS, EXPERTS])
        tile_end = sb("tile_end", [P, EXPERTS])
        past = sb("past", [P, TILES, EXPERTS])
        past_n = sb("past_n", [P, TILES, EXPERTS])
        tile_e = sb("tile_e", [P, TILES])
        tile_s = sb("tile_s", [P, TILES])
        tile_w = sb("tile_w", [P, 2, TILES])
        tile_row = sb("tile_row", [P, 2, TILES])
        table = sb("table", [P, 3, TILES], I32)
        pad_f = sb("pad_f", [P, EXPERTS])
        pad_at = sb("pad_at", [P, EXPERTS], I32)
        rows_in = sb("rows_in", [P, RING, ROW])
        w_now = sb("w_now", [P, 2, 2 * INTER])
        rT = sb("rT", [P, 2, P])
        silu = sb("silu", [P, 2, INTER])
        hidT = sb("hidT", [P, 2, INTER])
        dest = sb("dest", [P, RING], U32)
        weight = sb("weight", [P, RING])
        res = sb("res", [P, RING, D])
        ya = sb("ya", [P, 2, TOP, QT, D])
        o1 = sb("o1", [P, 2, QT, D])
        o2 = sb("o2", [P, 2, QT, D])
        o_st = sb("o_st", [P, 2, QT, 6])
        o_mv = sb("o_mv", [P, 2, QT, 2])
        o_ve = sb("o_ve", [P, 2, QT])
        o_r = sb("o_r", [P, 2, QT])
        on = sb("on", [P, 2, QT, D])
        x3 = sb("x3", [P, 2, QT, D])

        ps = [bank(f"ps{i}") for i in range(8)]
        ps_max, ps_exp, ps_pv, ps_a, ps_c, ps_d = ps[0:2], ps[2:4], ps[4], ps[5], ps[6], ps[7]
        ps_gate, ps_up, ps_rT, ps_res = ps[0:2], ps[2:4], ps[4:6], ps[6:8]

        s_cst, s_wqk, s_wvo, s_wffn = sem("consts_in"), sem("wqk_in"), sem("small_weights_in"), sem("ffn_weights_in")
        s_xin = [sem("x_in_0"), sem("x_in_1"), sem("x_in_rest")]
        s_const_b, s_stack_ones, s_vzero, s_rows0 = sem("bf16_consts"), sem("stack_ones"), sem("v_ones"), sem("rows_cleared")
        s_xst, s_xmv, s_xve, s_xr = sem("x_stats"), sem("x_mean_var"), sem("x_var_eps"), sem("x_rstd")
        s_xnb, s_xnow, s_ynb, s_znb, s_hnb = sem("x_bias"), sem("x_scales_at_hand"), sem("y_bias"), sem("z_bias"), sem("h_bias")
        s_xn, s_xnT_ps, s_xnT = sem("x_normed"), sem("xT_in_psum"), sem("xT_in_sbuf")
        s_qk_ps, s_hi, s_rest, s_mid, s_lo = sem("qk_in_psum"), sem("high_part"), sem("rest_after_high"), sem("middle_part"), sem("low_part")
        s_parts = [sem("parts_in_dram_0"), sem("parts_in_dram_1")]
        s_stack = [[sem(f"stack_in_{p}{f}") for f in range(2)] for p in range(2)]
        s_v_ps, s_v = sem("v_in_psum"), sem("v_in_sbuf")
        s_smax_ps, s_smax = sem("max_scores_in_psum"), sem("max_found")
        s_sh_hi, s_sh, s_shT_ps, s_shT = sem("shift_high"), sem("shift_low"), sem("shiftT_in_psum"), sem("shiftT_in_sbuf")
        s_shin = [sem("shift_rows_in_0"), sem("shift_rows_in_1")]
        s_sexp_ps, s_exp, s_pv = sem("exp_scores_in_psum"), sem("probs_ready"), sem("pv_group_done")
        s_u = sem("pv_bank_copied")
        s_uT, s_den, s_ctx = sem("ctx_tile_in_psum"), sem("denominators_inverted"), sem("ctx_tile_ready")
        s_ctxT_ps, s_ctxT, s_y_ps, s_y = sem("ctxT_in_psum"), sem("ctxT_in_sbuf"), sem("y_in_psum"), sem("y_in_sbuf")
        s_yst, s_ymv, s_yve, s_yr, s_yn, s_x2 = sem("y_stats"), sem("y_mean_var"), sem("y_var_eps"), sem("y_rstd"), sem("y_normed"), sem("x2_ready")
        s_zst, s_zmv, s_zve, s_zr, s_z, s_zn = sem("x2_stats"), sem("x2_mean_var"), sem("x2_var_eps"), sem("x2_rstd"), sem("z_ready"), sem("z_normed")
        s_znT_ps, s_znT, s_aw_ps, s_h = sem("znT_in_psum"), sem("znT_in_sbuf"), sem("attn_w_in_psum"), sem("h_ready")
        s_hst, s_hmv, s_hve, s_hr, s_hn = sem("h_stats"), sem("h_mean_var"), sem("h_var_eps"), sem("h_rstd"), sem("h_normed")
        s_tT_ps, s_tT, s_lg_ps, s_lg = sem("tT_in_psum"), sem("tT_in_sbuf"), sem("logits_in_psum"), sem("logits_in_sbuf")
        s_top, s_idx, s_idxf, s_oh, s_chb, s_bef = sem("top_values"), sem("top_indices"), sem("indices_as_float"), sem("one_hots"), sem("chosen_bf16"), sem("counts_before")
        s_gap, s_gape, s_gaps, s_w0, s_w1 = sem("logit_gap"), sem("gap_exp"), sem("gap_sum"), sem("weight_0"), sem("weight_1")
        s_pl_ps, s_pl, s_plc, s_sf, s_slot = sem("places_in_psum"), sem("places_in_sbuf"), sem("places_masked"), sem("slots_as_float"), sem("slots_ready")
        s_hn2, s_dst = sem("rows_copied"), sem("destinations_written")
        s_scat = [sem("rows_scattered_0"), sem("rows_scattered_1")]
        s_cnt_ps, s_tab = sem("counts_in_psum"), sem("table_step")
        s_pad = sem("padding_written")
        s_rin = [sem(f"rows_in_{i}") for i in range(RING)]
        s_wn, s_rT_ps, s_rT = sem("expert_weights_placed"), sem("rowsT_in_psum"), sem("rowsT_in_sbuf")
        s_gate, s_up, s_silu, s_hid = sem("gate_in_psum"), sem("up_in_psum"), sem("silu_ready"), sem("hidden_ready")
        s_res_ps, s_aux, s_res = sem("result_in_psum"), sem("weight_and_destination"), sem("result_ready")
        s_ysc = [sem(f"results_scattered_{i}") for i in range(RING)]
        s_ya = [sem("results_in_0"), sem("results_in_1")]
        s_o1, s_o2, s_ost, s_omv, s_ove, s_or, s_on, s_x3 = (sem("h_plus_first"), sem("ffn_out"), sem("ffn_stats"), sem("ffn_mean_var"),
                                                            sem("ffn_var_eps"), sem("ffn_rstd"), sem("ffn_normed"), sem("x3_ready"))
        s_out = [sem("out_written_0"), sem("out_written_1")]

        block = ctx.enter_context(nc.Block())

        def tiles_of(b):
            return at(b.n * QT, QT)

        def tile_at(b, t):
            return at(b.n * QT + t)

        def scattered(b):
            return SCATTER * (b.pair + 1) + 16 * b.parity

        def wait(eng, s, value, own=False):
            if not isinstance(value, int) or value > 0:
                eng.wait_ge(s, value)
                if own and not isinstance(value, int):
                    eng.nop(nofuse=True)

        def pipeline(eng, step):
            step(fixed(-1), a=True, m=True, e=False, c=False, d=False, first=True)
            step(fixed(0), a=True, m=True, e=True, c=False, d=False)
            step(fixed(1), a=True, m=True, e=True, c=True, d=False)
            with eng.Fori(0, (NB - 4) // 2) as i:
                step(Batch(i * 2 + 2, 0, i + 1), a=True, m=True, e=True, c=True, d=True)
                step(Batch(i * 2 + 3, 1, i + 1), a=True, m=True, e=True, c=True, d=True)
            step(fixed(NB - 2), a=False, m=True, e=True, c=True, d=True)
            step(fixed(NB - 1), a=False, m=False, e=True, c=True, d=True)
            step(fixed(NB), a=False, m=False, e=False, c=True, d=True)
            step(fixed(NB + 1), a=False, m=False, e=False, c=False, d=True)

        def tiles(eng, body):
            for n in range(RING):
                body(fixed_tile(n), first=n == 0)
            with eng.Fori(1, TILES // RING - 1) as i:
                for slot in range(RING):
                    body(Tile(i * RING + slot, slot, i))
            for n in range(TILES - RING, TILES):
                body(fixed_tile(n), last=n == TILES - 1)

        def batches(eng, body):
            body(fixed(0))
            body(fixed(1))
            with eng.Fori(1, NB // 2) as i:
                body(Batch(i * 2, 0, i))
                body(Batch(i * 2 + 1, 1, i))

        def at(n, k=1):
            return slice(n, n + k) if isinstance(n, int) else bass.ds(n, k)

        @block.sync
        def _(sp):
            sp.dma_start(x_sb[:, 0:QT, :], x[0].rearrange("(t p) d -> p t d", p=P)).then_inc(s_xin[0], 16)
            sp.dma_start(cst[:, :], consts).then_inc(s_cst, 16)
            sp.dma_start(wqk_sb[:, :, :], wqk).then_inc(s_wqk, 16)
            sp.dma_start(x_sb[:, QT:2 * QT, :], x[1].rearrange("(t p) d -> p t d", p=P)).then_inc(s_xin[1], 16)
            sp.dma_start(wv_sb[:, :], wv).then_inc(s_wvo, 16)
            sp.dma_start(wo_sb[:, :], wo).then_inc(s_wvo, 16)
            sp.dma_start(attn_w_sb[:, :], attn_w).then_inc(s_wvo, 16)
            sp.dma_start(gate_w_sb[:, :], gate_w).then_inc(s_wvo, 16)
            sp.dma_start(norms_sb[:, :], norms).then_inc(s_wvo, 16)
            sp.dma_start(x_sb[:, 2 * QT:NT, :], x[2:NB].rearrange("b (t p) d -> p (b t) d", p=P)).then_inc(s_xin[2], 16)

            def send_parts(b):
                wait(sp, s_lo, b.n + 1, own=True)
                for f in range(2):
                    sp.dma_start(parts_dram[b.parity, f].rearrange("w i c t -> c (w i) t"),
                                 parts[64 * f:64 * f + 64, b.parity].rearrange("c w i t -> c (w i) t")).then_inc(s_parts[f], 16)

            def stack(b, f):
                wait(sp, s_parts[f], 16 * (b.n + 1), own=True)
                wait(sp, s_sexp_ps, (b.n - 2) * HEADS + HD * f + HD, own=True)
                k_parts = parts_dram[b.parity, f, 1].rearrange("i (d s) t -> (i d) (s t)", s=HD)
                sp.dma_start(k_stack[0:STACK, b.parity, HD * f:HD * f + HD, :],
                             k_parts.unsqueeze(0).to_broadcast([PARTS, PARTS * HD, HD * S])).then_inc(s_stack[b.parity][f], 16)
                for i in range(PARTS):
                    q_part = parts_dram[b.parity, f, 0, i].rearrange("(d s) t -> d (s t)", s=HD)
                    sp.dma_start(q_stack[24 * i:24 * i + 24, b.parity, HD * f:HD * f + HD, :],
                                 q_part.unsqueeze(0).to_broadcast([PARTS, HD, HD * S])).then_inc(s_stack[b.parity][f], 16)

            def shift_rows(b, f):
                wait(sp, s_shT, 2 * b.n + f + 1, own=True)
                sp.dma_start(q_stack[STACK:STACK + SHIFT_ROWS, b.parity, HD * f:HD * f + HD, :], shiftT[:, f, :]
                             ).then_inc(s_shin[f], 16)

            def step(s, a, m, e, c, d, first=False):
                if first:
                    send_parts(s.plus(1))
                    stack(s.plus(1), 0)
                    stack(s.plus(1), 1)
                if e:
                    shift_rows(s, 1)
                if a:
                    send_parts(s.plus(2))
                    stack(s.plus(2), 0)
                if m:
                    shift_rows(s.plus(1), 0)
                if a:
                    stack(s.plus(2), 1)
                if first:
                    sp.dma_start(down_sb[:, :], down).then_inc(s_wffn, 16)
                if not m and e:
                    sp.wait_ge(s_sexp_ps, NB * HEADS)
                    sp.dma_start(gate_up_sb, gate_up).then_inc(s_wffn, 16)

            sp.wait_ge(s_stack_ones, 3)
            pipeline(sp, step)

            sp.wait_ge(s_tab, TABLE_STEPS)
            for p in range(2):
                sp.wait_ge(s_scat[p], scattered(fixed(NB - 2 + p)))
            for e_ in range(EXPERTS):
                row = sp.value_load(pad_at[0:1, e_:e_ + 1], min_val=0, max_val=EXPERTS * REGION - P)
                sp.dma_start(xs[bass.ds(row, P), :], cst[:, C_PAD:C_PAD + ROW]).then_inc(s_pad, 16)
            sp.wait_ge(s_pad, 16 * EXPERTS)

            def load_rows(t, first=False, last=False):
                row = sp.value_load(table[0:1, 0, at(t.n)], min_val=0, max_val=EXPERTS * REGION)
                wait(sp, s_rT_ps, t.n - RING + 1, own=True)
                wait(sp, s_aux, t.n - RING + 1, own=True)
                sp.dma_start(rows_in[:, t.slot, :], xs[bass.ds(row, P), :]).then_inc(s_rin[t.slot], 16)

            tiles(sp, load_rows)

            for s_ in s_ysc:
                sp.wait_ge(s_, TILES // RING * 16)
            ys_v = ys.rearrange("(c b t p) d -> b p c t d", c=TOP, t=QT, p=P)
            out_v = out.rearrange("b (t p) d -> b p t d", p=P)

            def load(n, p):
                for c in range(TOP):
                    sp.dma_start(ya[:, p, c, :, :], ys_v[at(n), :, c, :, :].rearrange("b p t d -> (b p) t d")).then_inc(s_ya[p], 16)

            def store(b):
                wait(sp, s_x3, b.n + 1, own=True)
                sp.dma_start(out_v[at(b.n)].rearrange("b p t d -> (b p) t d"), x3[:, b.parity]).then_inc(s_out[b.parity], 16)

            load(0, 0)
            load(1, 1)
            with sp.Fori(0, NB // 2 - 1) as i:
                for p in range(2):
                    store(Batch(i * 2 + p, p, i))
                    load(i * 2 + (p + 2), p)
            store(fixed(NB - 2))
            store(fixed(NB - 1))
            for p in range(2):
                sp.wait_ge(s_out[p], 16 * (NB // 2))

        @block.tensor
        def _(pe):
            def shift_T(b, f, before_this):
                pe.wait_ge(s_sh, 2 * b.n + f + 1)
                before_this()
                for t in range(QT):
                    last = nc.tensor.transpose(ps_a[0:16, t * 64:t * 64 + 64].bitcast(BF16),
                                               shift[:, f, t].rearrange("p a b -> p (a b)"), ident_b[:, :])
                last.then_inc(s_shT_ps, 1)

            def x_T(b, before_this):
                wait(pe, s_xn, QT * b.n + QT)
                before_this()
                for t in range(QT):
                    last = nc.tensor.transpose(ps_a[:, t * P:t * P + P], xn[:, t, :], ident)
                last.then_inc(s_xnT_ps, 1)

            def project_qk(b):
                wait(pe, s_xnT, b.n + 1)
                for w in range(2):
                    last = nc.tensor.matmul(ps_a[:, w * S:w * S + S], wqk_sb[:, w, :], xnT[:, b.parity, :], start=True, stop=True)
                last.then_inc(s_qk_ps, 1)

            def project_v(b, before_this):
                before_this()
                for t in range(QT):
                    last = nc.tensor.matmul(ps_a[:, t * P:t * P + P], xnT[:, b.parity, t * P:t * P + P], wv_sb[:, :], start=True, stop=True)
                last.then_inc(s_v_ps, 1)

            def max_scores(b, h):
                if h % 8 == 0:
                    pe.wait_ge(s_stack[b.parity][h // 8], 16 * 4 * (b.pair + 1))
                wait(pe, s_smax, b.n * HEADS + h - 1)
                for t in range(QT):
                    last = nc.tensor.matmul(ps_max[h % 2][:, t * S:t * S + S], q_stack[0:STACK, b.parity, h, t * P:t * P + P],
                                            k_stack[0:STACK, b.parity, h, :], start=True, stop=True)
                last.then_inc(s_smax_ps, 1)

            def exp_scores(b, h):
                if h % 8 == 0:
                    pe.wait_ge(s_shin[h // 8], 16 * b.n + 16)
                wait(pe, s_exp, b.n * HEADS + h - 1)
                for t in range(QT):
                    last = nc.tensor.matmul(ps_exp[h % 2][:, t * S:t * S + S], k_stack[:, b.parity, h, t * P:t * P + P],
                                            q_stack[:, b.parity, h, :], start=True, stop=True)
                last.then_inc(s_sexp_ps, 1)

            def pv(b, g):
                if g == 0:
                    wait(pe, s_v, b.n + 1)
                pe.wait_ge(s_exp, b.n * HEADS + 4 * g + 4)
                if g % 2 == 0:
                    wait(pe, s_u, 2 * b.n + g // 2)
                for t in range(QT):
                    for j in range(4):
                        h = 4 * g + j
                        last = nc.tensor.matmul(ps_pv[32 * j:32 * j + 32, (g % 2) * S:(g % 2) * S + S],
                                                v_aug[:, b.parity, t, h, :], probs[:, h % 8, t, :],
                                                start=(t == 0), stop=(t == QT - 1))
                last.then_inc(s_pv, 1)

            def ctx_tile(b, t):
                for g in range(4):
                    last = nc.tensor.transpose(ps_c[:, g * P:g * P + P], u_sb[:, g, t * P:t * P + P], ident)
                last.then_inc(s_uT, 1)

            def ctx_T(b):
                wait(pe, s_ctx, 2 * b.n + 2)
                for t in range(QT):
                    last = nc.tensor.transpose(ps_c[:, t * P:t * P + P], ctx_sb[:, t, :], ident)
                last.then_inc(s_ctxT_ps, 1)

            def two_tiles(b, bank_, ready, value, act, w, n, done):
                wait(pe, ready, value)
                for t in range(QT):
                    last = nc.tensor.matmul(bank_[:, t * n:t * n + n], act[:, t * P:t * P + P], w, start=True, stop=True)
                last.then_inc(done, 1)

            def zn_T(b):
                wait(pe, s_zn, 2 * b.n + 2)
                for t in range(QT):
                    last = nc.tensor.transpose(ps_d[:, t * P:t * P + P], zn[:, t, :], ident)
                last.then_inc(s_znT_ps, 1)

            def h_T(b):
                wait(pe, s_hn, 2 * b.n + 2)
                for t in range(QT):
                    last = nc.tensor.transpose(ps_d[:, t * P:t * P + P], rows[:, b.parity, t, 0, 0:P], ident)
                last.then_inc(s_tT_ps, 1)

            def places(b):
                wait(pe, s_bef, 2 * b.n + 3)
                nc.tensor.matmul(ps_d[:, 0:16], upper_b[:, :], chosen_b[:, b.parity].rearrange("p t e -> p (t e)"), start=True, stop=False)
                nc.tensor.matmul(ps_d[:, 0:16], ones_b[:, :], before[:, b.parity].rearrange("p t e -> p (t e)"),
                                 start=False, stop=True).then_inc(s_pl_ps, 1)

            def step(s, a, m, e, c, d, first=False):
                A, M, C, D_ = s.plus(2), s.plus(1), s.plus(-1), s.plus(-2)
                nothing = lambda: None
                if first:
                    x_T(M, nothing)
                    project_qk(M)
                for h in range(HEADS):
                    if m:
                        max_scores(M, h)
                    if e:
                        exp_scores(s, h)
                    if h == 1 and c:
                        pv(C, 3)
                    if h == 1 and e:
                        shift_T(s, 1, lambda: (wait(pe, s_v, s.n + 1), wait(pe, s_shT, 2 * s.n + 1)))
                    if h == 2 and d:
                        if not m:
                            wait(pe, s_pl, D_.n)
                        zn_T(D_)
                    if h == 3 and c:
                        wait(pe, s_y, C.n)
                        wait(pe, s_u, 2 * C.n + 2)
                        ctx_tile(C, 0)
                    if h == 3 and a:
                        x_T(A, (lambda: wait(pe, s_shT, 2 * s.n + 2)) if e else (lambda: wait(pe, s_rest, M.n + 1)))
                    if h == 4 and d:
                        two_tiles(D_, ps_d, s_znT, D_.n + 1, znT, attn_w_sb[:, :], P, s_aw_ps)
                    if h == 5 and e:
                        pv(s, 0)
                    if h == 5 and c:
                        wait(pe, s_ctx, 2 * C.n + 1)
                        ctx_tile(C, 1)
                    if h == 5 and a:
                        project_qk(A)
                    if h == 7 and c:
                        ctx_T(C)
                    if h == 8 and m:
                        project_v(M, (lambda: wait(pe, s_rest, A.n + 1)) if a else (lambda: wait(pe, s_shT, 2 * s.n + 2)))
                    if h == 8 and d:
                        h_T(D_)
                    if h == 9 and c:
                        two_tiles(C, ps_c, s_ctxT, C.n + 1, ctxT, wo_sb[:, :], P, s_y_ps)
                    if h == 9 and e:
                        pv(s, 1)
                    if h == 10 and m:
                        shift_T(M, 0, lambda: wait(pe, s_v, M.n + 1))
                    if h == 10 and d:
                        two_tiles(D_, ps_d, s_tT, D_.n + 1, tT, gate_w_sb[:, :], EXPERTS, s_lg_ps)
                    if h == 12 and d:
                        wait(pe, s_lg, D_.n + 1)
                        places(D_)
                    if h == 13 and e:
                        pv(s, 2)

            pe.wait_ge(s_cst, 16)
            pe.wait_ge(s_const_b, 3)
            pe.wait_ge(s_wqk, 16)
            pe.wait_ge(s_wvo, 16 * 5)
            pipeline(pe, step)
            pe.wait_ge(s_bef, 2 * NB + 1)
            pe.wait_ge(s_pl, NB)
            nc.tensor.matmul(ps_c[:, 0:EXPERTS], ones_b[:, :], before[:, NB % 2, 0, :], start=True, stop=True).then_inc(s_cnt_ps, 1)

            pe.wait_ge(s_tab, TABLE_STEPS)
            pe.wait_ge(s_wffn, 32)

            def rows_T(t):
                p = t.parity
                wait(pe, s_rin[t.slot], t.round * 16 + 16)
                wait(pe, s_rT, t.n - 1)
                nc.tensor.transpose(ps_rT[p][:, 0:P], rows_in[:, t.slot, 0:P], ident).then_inc(s_rT_ps, 1)

            def gate_and_up(t):
                p = t.parity
                wait(pe, s_wn, t.n + 1)
                wait(pe, s_rT, t.n + 1)
                wait(pe, s_hid, t.n - 1)
                for half, (bank_, done) in enumerate(((ps_gate, s_gate), (ps_up, s_up))):
                    for k in range(IC):
                        last = nc.tensor.matmul(bank_[p][:, k * P:k * P + P],
                                                w_now[:, p, half * INTER + k * P:half * INTER + k * P + P],
                                                rT[:, p, :], start=True, stop=True)
                    last.then_inc(done, 1)

            def down_product(t):
                p = t.parity
                col = pe.value_load(table[0:1, 2, at(t.n)], min_val=0, max_val=(EXPERTS - 1) * INTER)
                wait(pe, s_hid, t.n + 1)
                wait(pe, s_res, t.n - 1)
                for k in range(IC):
                    last = nc.tensor.matmul(ps_res[p][:, 0:P], hidT[:, p, k * P:k * P + P],
                                            down_sb[:, bass.ds(col + k * P, P)], start=(k == 0), stop=(k == IC - 1))
                last.then_inc(s_res_ps, 1)

            def tile_products(t, first=False, last=False):
                if first:
                    rows_T(t)
                if not last:
                    rows_T(t.plus(1))
                gate_and_up(t)
                if not first:
                    down_product(t.plus(-1))
                if last:
                    down_product(t)

            tiles(pe, tile_products)

        @block.scalar
        def _(act):
            def x_T(b):
                wait(act, s_xnT_ps, b.n + 1)
                nc.scalar.copy(xnT[:, b.parity, :], ps_a[:, 0:S]).then_inc(s_xnT, 1)

            def high_part(b):
                wait(act, s_qk_ps, b.n + 1)
                nc.scalar.copy(parts[:, b.parity, :, 0, :], ps_a[:, :].rearrange("p (w t) -> p w t", w=2)).then_inc(s_hi, 1)

            def middle_part(b):
                wait(act, s_rest, b.n + 1)
                nc.scalar.copy(parts[:, b.parity, :, 1, :], rest1[:, :, :]).then_inc(s_mid, 1)

            def normed(src, dst, r, nb, done):
                for t in range(QT):
                    nc.scalar.activation(dst(t), src(t), ACT.Identity, bias=nb(t), scale=r(t)).then_inc(done, 1)

            def x_normed(b):
                wait(act, s_xnow, b.n + 1)
                wait(act, s_xnT_ps, b.n)
                now = x_now[:, b.parity]
                normed(lambda t: x_sb[:, tile_at(b, t), :], lambda t: xn[:, t, :],
                       lambda t: now[:, 0, t:t + 1], lambda t: now[:, 1, t:t + 1], s_xn)

            def y_normed(b):
                wait(act, s_ynb, b.n + 1)
                wait(act, s_y, b.n + 1)
                normed(lambda t: y_sb[:, t, :], lambda t: yn[:, t, :], lambda t: y_r[:, t:t + 1], lambda t: y_nb[:, t:t + 1], s_yn)

            def z_of(b):
                wait(act, s_znb, b.n + 1)
                normed(lambda t: x2_sb[:, tile_at(b, t), :], lambda t: z[:, t, :],
                       lambda t: z_r[:, 0, t:t + 1], lambda t: z_nb[:, t:t + 1], s_z)

            def h_normed(b):
                wait(act, s_hnb, b.n + 1)
                normed(lambda t: h_sb[:, tile_at(b, t), :], lambda t: rows[:, b.parity, t, 0, 0:P],
                       lambda t: h_r[:, t:t + 1], lambda t: h_nb[:, t:t + 1], s_hn)

            def v_out(b):
                wait(act, s_v_ps, b.n + 1)
                nc.scalar.copy(v_aug[:, b.parity, :, :, 0:HD],
                               ps_a[:, 0:QT * P].rearrange("p (t h d) -> p t h d", t=QT, d=HD)).then_inc(s_v, 1)

            def exps(b, h):
                pe_group = b.n * 4 + h // 4 - 1
                if h % 4 == 0:
                    wait(act, s_pv, pe_group)
                act.wait_ge(s_sexp_ps, b.n * HEADS + h + 1)
                nc.scalar.activation(probs[:, h % 8, :, :].rearrange("p t s -> p (t s)"), ps_exp[h % 2][:, :], ACT.Exp,
                                     scale=SCALE).then_inc(s_exp, 1)

            def pv_out(b, k):
                wait(act, s_pv, b.n * 4 + 2 * k + 2)
                if k == 0:
                    wait(act, s_uT, 2 * b.n)
                nc.scalar.copy(u_sb[:, 2 * k:2 * k + 2, :].rearrange("p g s -> p (g s)"), ps_pv[:, :]).then_inc(s_u, 1)

            def ctx_T(b):
                wait(act, s_ctxT_ps, b.n + 1)
                nc.scalar.copy(ctxT[:, :], ps_c[:, 0:S]).then_inc(s_ctxT, 1)

            def y_out(b):
                wait(act, s_y_ps, b.n + 1)
                nc.scalar.copy(y_sb[:, :, :].rearrange("p t d -> p (t d)"), ps_c[:, 0:S]).then_inc(s_y, 1)

            def affine(b, ready, dst, done, k):
                wait(act, ready, b.n + 1)
                nc.scalar.activation(dst, ps_d[:, 0:S], ACT.Identity, bias=norms_sb[:, k + 1:k + 2],
                                     scale=norms_sb[:, k:k + 1]).then_inc(done, 1)

            def gap_exp(b):
                wait(act, s_gap, b.n + 1)
                nc.scalar.activation(gap_e[:, :], gap[:, :], ACT.Exp).then_inc(s_gape, 1)

            def step(s, a, m, e, c, d, first=False):
                A, M, C, D_ = s.plus(2), s.plus(1), s.plus(-1), s.plus(-2)
                if first:
                    x_normed(M)
                    x_T(M)
                    high_part(M)
                    middle_part(M)
                for h in range(HEADS):
                    if e:
                        exps(s, h)
                    if h == 0 and d:
                        z_of(D_)
                    if h == 1 and a:
                        x_normed(A)
                    if h == 1 and c:
                        pv_out(C, 1)
                    if h == 2 and d:
                        affine(D_, s_znT_ps, znT[:, :], s_znT, 0)
                    if h == 3 and a:
                        x_T(A)
                    if h == 5 and a:
                        high_part(A)
                    if h == 6 and d:
                        h_normed(D_)
                    if h == 7 and a:
                        middle_part(A)
                    if h == 7 and c:
                        ctx_T(C)
                    if h == 8 and m:
                        v_out(M)
                    if h == 8 and d:
                        affine(D_, s_tT_ps, tT[:, :], s_tT, 2)
                    if h == 9 and c:
                        y_out(C)
                    if h == 9 and e:
                        pv_out(s, 0)
                    if h == 11 and d:
                        gap_exp(D_)
                    if h == 12 and c:
                        y_normed(C)

            act.wait_ge(s_vzero, 2)
            act.wait_ge(s_wvo, 16 * 5)
            pipeline(act, step)

            def row_T(t):
                wait(act, s_rT_ps, t.n + 1)
                wait(act, s_up, t.n - 1)
                nc.scalar.activation(rT[:, t.parity, :], ps_rT[t.parity][:, 0:P], ACT.Identity, bias=norms_sb[:, 3:4],
                                     scale=norms_sb[:, 2:3]).then_inc(s_rT, 1)

            def silu_of(t, first=False, last=False):
                if first:
                    row_T(t)
                if not last:
                    row_T(t.plus(1))
                wait(act, s_gate, t.n + 1)
                wait(act, s_hid, t.n - 1)
                nc.scalar.activation(silu[:, t.parity, :], ps_gate[t.parity][:, :], ACT.Silu).then_inc(s_silu, 1)

            tiles(act, silu_of)

        @block.vector
        def _(dve):
            def stats(b, src, st, mv, s_st, s_mv):
                for t in range(QT):
                    nc.vector.bn_stats(st[:, t, :], src(t)).then_inc(s_st, 1)
                wait(dve, s_st, 2 * b.n + 2, own=True)
                for t in range(QT):
                    nc.vector.bn_aggr(mv[:, t, :], st[:, t, :]).then_inc(s_mv, 1)

            def x_stats(first, last):
                for t in range(first, last):
                    nc.vector.bn_stats(x_st[:, t, :], x_sb[:, t, :]).then_inc(s_xst, 1)
                dve.wait_ge(s_xst, last)
                for t in range(first, last):
                    nc.vector.bn_aggr(x_mv[:, t, :], x_st[:, t, :]).then_inc(s_xmv, 1)

            def x_scales(b):
                dve.wait_ge(s_xnb, min(b.n + 1, 3) if isinstance(b.n, int) else 3)
                nc.vector.tensor_copy(x_now[:, b.parity], x_rn[:, :, tiles_of(b)]).then_inc(s_xnow, 1)

            def zn_of(b):
                wait(dve, s_zr, b.n + 1)
                for t in range(QT):
                    nc.vector.tensor_scalar(zn[:, t, :], x2_sb[:, tile_at(b, t), :], z_mv[:, t, 0:1], z_r[:, 1, t:t + 1],
                                            ALU.subtract, ALU.mult).then_inc(s_zn, 1)

            def rest_of(b):
                wait(dve, s_hi, b.n + 1)
                wait(dve, s_lo, b.n)
                nc.vector.tensor_tensor(rest1[:, :, :], ps_a[:, :].rearrange("p (w t) -> p w t", w=2), parts[:, b.parity, :, 0, :],
                                        ALU.subtract).then_inc(s_rest, 1)

            def take_max(b, h):
                dve.wait_ge(s_smax_ps, b.n * HEADS + h + 1)
                nc.vector.tensor_reduce(neg_max[:, b.parity, :, h:h + 1],
                                        ps_max[h % 2][:, :].rearrange("p (t k) -> p t k", t=QT), AX.X, ALU.max,
                                        negate=True).then_inc(s_smax, 1)

            def shifts(b, f):
                wait(dve, s_smax, b.n * HEADS + 8 * f + 8)
                if f == 0:
                    wait(dve, s_shT_ps, 2 * b.n - 1)
                src = neg_max[:, b.parity, :, 8 * f:8 * f + 8]
                nc.vector.tensor_copy(shift[:, f, :, 0, :], src).then_inc(s_sh_hi, 1)
                wait(dve, s_sh_hi, 2 * b.n + f + 1)
                nc.vector.tensor_tensor(shift[:, f, :, 1, :], src, shift[:, f, :, 0, :], ALU.subtract).then_inc(s_sh, 1)

            def shift_out(b, f):
                wait(dve, s_shT_ps, 2 * b.n + f + 1)
                wait(dve, s_shin[f], 16 * b.n)
                nc.vector.tensor_copy(shiftT[:, f, :], ps_a[0:16, 0:128].bitcast(BF16)).then_inc(s_shT, 1)

            def ctx_tile(b, t):
                wait(dve, s_uT, 2 * b.n + t + 1)
                u = ps_c[:, :].rearrange("p (h r) -> p h r", r=32)
                nc.vector.reciprocal(den_r[:, t, :], u[:, :, HD:HD + 1].rearrange("p h r -> p (h r)")).then_inc(s_den, 1)
                wait(dve, s_den, 2 * b.n + t + 1)
                nc.vector.tensor_tensor(ctx_sb[:, t, :].rearrange("p (h d) -> p h d", d=HD), u[:, :, 0:HD],
                                        den_r[:, t, :].unsqueeze(2).to_broadcast([P, HEADS, HD]), ALU.mult).then_inc(s_ctx, 1)

            def h_out(b):
                wait(dve, s_aw_ps, b.n + 1)
                nc.vector.tensor_tensor(h_sb[:, tiles_of(b), :], ps_d[:, 0:S].rearrange("p (t d) -> p t d", t=QT), z[:, :, :],
                                        ALU.add).then_inc(s_h, 1)
                wait(dve, s_h, b.n + 1, own=True)

            def route(b):
                wait(dve, s_lg_ps, b.n + 1)
                nc.vector.tensor_copy(logits[:, :, :].rearrange("p t e -> p (t e)"), ps_d[:, 0:QT * EXPERTS]).then_inc(s_lg, 1)
                wait(dve, s_lg, b.n + 1, own=True)
                for t in range(QT):
                    nc.vector.max(top8[:, t, :], logits[:, t, :]).then_inc(s_top, 1)
                wait(dve, s_top, 2 * b.n + 2, own=True)
                for t in range(QT):
                    nc.vector.max_index(idx8[:, t, :], top8[:, t, :], logits[:, t, :]).then_inc(s_idx, 1)
                nc.vector.tensor_tensor(gap[:, :], top8[:, :, 1], top8[:, :, 0], ALU.subtract).then_inc(s_gap, 1)
                wait(dve, s_idx, 2 * b.n + 2)
                nc.vector.tensor_copy(idx_f[:, :, :], idx8[:, :, 0:TOP]).then_inc(s_idxf, 1)
                wait(dve, s_idxf, b.n + 1)
                for k in range(TOP):
                    nc.vector.tensor_tensor(chosen[:, k, :, :], iota8, idx_f[:, :, k:k + 1].to_broadcast([P, QT, EXPERTS]),
                                            ALU.is_equal).then_inc(s_oh, 1)
                wait(dve, s_oh, 2 * b.n + 2)
                nc.vector.tensor_tensor(chosen_b[:, b.parity], chosen[:, 0], chosen[:, 1], ALU.add).then_inc(s_chb, 1)
                wait(dve, s_chb, b.n + 1)
                nc.vector.tensor_tensor(before[:, b.parity, 1, :], before[:, b.parity, 0, :], chosen_b[:, b.parity, 0, :],
                                        ALU.add).then_inc(s_bef, 1)
                wait(dve, s_bef, 2 * b.n + 2)
                nc.vector.tensor_tensor(before[:, 1 - b.parity, 0, :], before[:, b.parity, 1, :], chosen_b[:, b.parity, 1, :],
                                        ALU.add).then_inc(s_bef, 1)
                wait(dve, s_gape, b.n + 1)
                nc.vector.tensor_scalar(gap_s[:, :], gap_e[:, :], 1.0, None, ALU.add).then_inc(s_gaps, 1)
                wait(dve, s_gaps, b.n + 1)
                nc.vector.reciprocal(rows[:, b.parity, :, 0, P], gap_s[:, :]).then_inc(s_w0, 1)
                wait(dve, s_w0, b.n + 1)
                nc.vector.tensor_tensor(rows[:, b.parity, :, 1, P], gap_e[:, :], rows[:, b.parity, :, 0, P], ALU.mult).then_inc(s_w1, 1)

            def slots(b):
                wait(dve, s_pl_ps, b.n + 1)
                nc.vector.tensor_tensor(place[:, :], ps_d[:, 0:16], region_base, ALU.add).then_inc(s_pl, 1)
                wait(dve, s_pl, b.n + 1)
                nc.vector.tensor_tensor(place_c[:, :, :], chosen[:, :, :, :].rearrange("p c t e -> p c (t e)"),
                                        place[:, :].unsqueeze(1).to_broadcast([P, TOP, 16]), ALU.mult).then_inc(s_plc, 1)
                wait(dve, s_plc, b.n + 1)
                nc.vector.tensor_reduce(slot_f[:, :], place_c[:, :, :].rearrange("p c (t e) -> p (c t) e", e=EXPERTS), AX.X,
                                        ALU.add).then_inc(s_sf, 1)
                wait(dve, s_sf, b.n + 1)
                nc.vector.tensor_copy(slot[:, b.parity, :], slot_f[:, :]).then_inc(s_slot, 1)

            def step(s, a, m, e, c, d, first=False):
                A, M, C, D_ = s.plus(2), s.plus(1), s.plus(-1), s.plus(-2)
                if first:
                    x_scales(M)
                    x_scales(A)
                    rest_of(M)
                    dve.wait_ge(s_xin[2], 16)
                    x_stats(2 * QT, NT)
                for h in range(HEADS):
                    if h == 0 and e:
                        shifts(s, 1)
                    if h == 0 and a and not first:
                        x_scales(A)
                    if h == 0 and d:
                        zn_of(D_)
                    if m:
                        take_max(M, h)
                    if h == 1 and e:
                        shift_out(s, 1)
                    if h == 3 and c:
                        ctx_tile(C, 0)
                    if h == 4 and d:
                        wait(dve, s_z, 2 * D_.n + 2)
                        h_out(D_)
                        stats(D_, lambda t: h_sb[:, tile_at(D_, t), :], h_st, h_mv, s_hst, s_hmv)
                    if h == 5 and c:
                        ctx_tile(C, 1)
                    if h == 6 and a:
                        rest_of(A)
                    if h == 7 and m:
                        shifts(M, 0)
                    if h == 10 and c:
                        wait(dve, s_y, C.n + 1, own=True)
                        stats(C, lambda t: y_sb[:, t, :], y_st, y_mv, s_yst, s_ymv)
                    if h == 10 and m:
                        shift_out(M, 0)
                    if h == 10 and d:
                        route(D_)
                    if h == 12 and d:
                        slots(D_)
                    if h == 14 and c:
                        wait(dve, s_x2, C.n + 1, own=True)
                        stats(C, lambda t: x2_sb[:, tile_at(C, t), :], z_st, z_mv, s_zst, s_zmv)

            dve.wait_ge(s_cst, 16)
            nc.vector.tensor_copy(ident_b[:, :], ident).then_inc(s_const_b, 1)
            nc.vector.tensor_copy(upper_b[:, :], cst[:, C_UPPER:C_UPPER + P]).then_inc(s_const_b, 1)
            nc.vector.tensor_copy(ones_b[:, :], cst[:, C_ONES:C_ONES + P]).then_inc(s_const_b, 1)
            nc.vector.memset(before[:, :, :, :], 0.0).then_inc(s_bef, 1)
            dve.wait_ge(s_bef, 1)
            for b in range(2):
                dve.wait_ge(s_xin[b], 16)
                x_stats(b * QT, b * QT + QT)
            pipeline(dve, step)

            steps = [0]

            def link(instruction):
                steps[0] += 1
                instruction.then_inc(s_tab, 1)
                dve.wait_ge(s_tab, steps[0])

            def row_of(column, n):
                return cst[:, column:column + n]

            tri = row_of(C_LOWER, EXPERTS * EXPERTS).rearrange("p (a b) -> p a b", b=EXPERTS)
            dve.wait_ge(s_cnt_ps, 1)
            link(nc.vector.tensor_copy(cnt[:, :], ps_c[:, 0:EXPERTS]))
            link(nc.vector.tensor_tensor(tile_gt[:, :, :], cnt[:, :].unsqueeze(2).to_broadcast([P, EXPERTS, 16]),
                                         row_of(C_STEP, 16).unsqueeze(1).to_broadcast([P, EXPERTS, 16]), ALU.is_gt))
            link(nc.vector.tensor_reduce(n_tiles[:, :], tile_gt[:, :, :], AX.X, ALU.add))
            link(nc.vector.tensor_tensor(tile_lo[:, :, :], n_tiles[:, :].unsqueeze(1).to_broadcast([P, EXPERTS, EXPERTS]), tri, ALU.mult))
            link(nc.vector.tensor_reduce(tile_end[:, :], tile_lo[:, :, :], AX.X, ALU.add))
            link(nc.vector.tensor_tensor(past[:, :, :], row_of(C_TILE, TILES).unsqueeze(2).to_broadcast([P, TILES, EXPERTS]),
                                         tile_end[:, :].unsqueeze(1).to_broadcast([P, TILES, EXPERTS]), ALU.is_ge))
            link(nc.vector.tensor_tensor(past_n[:, :, :], past[:, :, :], n_tiles[:, :].unsqueeze(1).to_broadcast([P, TILES, EXPERTS]),
                                         ALU.mult))
            link(nc.vector.tensor_reduce(tile_e[:, :], past[:, :, :], AX.X, ALU.add))
            link(nc.vector.tensor_reduce(tile_s[:, :], past_n[:, :, :], AX.X, ALU.add))
            link(nc.vector.tensor_tensor(tile_row[:, 0, :], row_of(C_TILE, TILES), tile_s[:, :], ALU.subtract))
            link(nc.vector.tensor_scalar(tile_w[:, 1, :], tile_e[:, :], EXPERTS - 0.5, float(P), ALU.is_lt, ALU.mult))
            link(nc.vector.tensor_tensor(tile_row[:, 1, :], tile_row[:, 0, :], tile_w[:, 1, :], ALU.mult))
            link(nc.vector.scalar_tensor_tensor(table[:, 0, :], tile_e[:, :], float(REGION), tile_row[:, 1, :], ALU.mult, ALU.add))
            link(nc.vector.tensor_scalar(table[:, 1, :], tile_e[:, :], float(EXPERTS - 1), float(2 * INTER), ALU.min, ALU.mult))
            link(nc.vector.tensor_scalar(table[:, 2, :], tile_e[:, :], float(EXPERTS - 1), float(INTER), ALU.min, ALU.mult))
            link(nc.vector.tensor_tensor(pad_at[:, :], cnt[:, :], region_base[:, 0:EXPERTS], ALU.add))
            assert steps[0] == TABLE_STEPS

            dve.wait_ge(s_wffn, 32)

            def aux(t):
                p = t.slot
                wait(dve, s_rin[p], t.round * 16 + 16)
                wait(dve, s_ysc[p], t.round * 16)
                nc.vector.tensor_copy(dest[:, p:p + 1], rows_in[:, p, P + 1:P + 2])
                nc.vector.tensor_copy(weight[:, p:p + 1], rows_in[:, p, P:P + 1]).then_inc(s_aux, 1)

            def hidden(t):
                p = t.parity
                wait(dve, s_silu, t.n + 1)
                wait(dve, s_up, t.n + 1)
                wait(dve, s_res_ps, t.n - 1)
                nc.vector.tensor_tensor(hidT[:, p, :], ps_up[p][:, :], silu[:, p, :], ALU.mult).then_inc(s_hid, 1)

            def result(t):
                p = t.slot
                wait(dve, s_aux, t.n + 1)
                wait(dve, s_res_ps, t.n + 1)
                nc.vector.tensor_scalar(res[:, p, :], ps_res[t.parity][:, 0:P], weight[:, p:p + 1], None, ALU.mult).then_inc(s_res, 1)

            def place_weights(t):
                col = dve.value_load(table[0:1, 1, at(t.n)], min_val=0, max_val=(EXPERTS - 1) * 2 * INTER)
                wait(dve, s_up, t.n - 1)
                nc.vector.tensor_copy(w_now[:, t.parity, :], gate_up_sb[:, bass.ds(col, 2 * INTER)]).then_inc(s_wn, 1)

            def tile_elementwise(t, first=False, last=False):
                if first:
                    place_weights(t)
                if not last:
                    place_weights(t.plus(1))
                aux(t)
                hidden(t)
                if not first:
                    result(t.plus(-1))
                if last:
                    result(t)

            tiles(dve, tile_elementwise)

            def add_and_norm(b):
                n, p = b.n, b.parity
                dve.wait_ge(s_ya[p], b.pair * 32 + 32)
                nc.vector.tensor_tensor(o1[:, p], ya[:, p, 0], h_sb[:, tiles_of(b), :], ALU.add).then_inc(s_o1, 1)
                wait(dve, s_o1, n + 1)
                nc.vector.tensor_tensor(o2[:, p], ya[:, p, 1], o1[:, p], ALU.add).then_inc(s_o2, 1)
                wait(dve, s_o2, n + 1, own=True)
                for t in range(QT):
                    nc.vector.bn_stats(o_st[:, p, t, :], o2[:, p, t, :]).then_inc(s_ost, 1)
                wait(dve, s_ost, n * 2 + 2, own=True)
                for t in range(QT):
                    nc.vector.bn_aggr(o_mv[:, p, t, :], o_st[:, p, t, :]).then_inc(s_omv, 1)
                wait(dve, s_x3, n - 1)
                wait(dve, s_or, n + 1)
                for t in range(QT):
                    nc.vector.tensor_scalar(on[:, p, t, :], o2[:, p, t, :], o_mv[:, p, t, 0:1], o_r[:, p, t:t + 1],
                                            ALU.subtract, ALU.mult).then_inc(s_on, 1)

            batches(dve, add_and_norm)

        @block.gpsimd
        def _(pool):
            def rstd(b, mv, ve, nm, r, nb, s_mv, s_ve, s_r, s_nb):
                wait(pool, s_mv, 2 * b.n + 2, own=True)
                nc.gpsimd.tensor_scalar(ve[:, :], mv[:, :, 1], EPS, None, ALU.add).then_inc(s_ve, 1)
                nc.gpsimd.tensor_scalar(nm[:, :], mv[:, :, 0], -1.0, None, ALU.mult).then_inc(s_ve, 1)
                wait(pool, s_ve, 2 * b.n + 2, own=True)
                nc.gpsimd.tensor_tensor(r[:, :], ve[:, :], neg_half[:, 0:QT], ALU.pow).then_inc(s_r, 1)
                wait(pool, s_r, b.n + 1, own=True)
                nc.gpsimd.tensor_tensor(nb[:, :], nm[:, :], r[:, :], ALU.mult).then_inc(s_nb, 1)

            def low_part(b):
                wait(pool, s_mid, b.n + 1, own=True)
                nc.gpsimd.tensor_tensor(parts[:, b.parity, :, 2, :], rest1[:, :, :], parts[:, b.parity, :, 1, :],
                                        ALU.subtract).then_inc(s_lo, 1)

            def x_rstd(first, last, count):
                pool.wait_ge(s_xmv, last)
                nc.gpsimd.tensor_scalar(x_ve[:, first:last], x_mv[:, first:last, 1], EPS, None, ALU.add).then_inc(s_xve, 1)
                nc.gpsimd.tensor_scalar(neg_mean[:, first:last], x_mv[:, first:last, 0], -1.0, None, ALU.mult).then_inc(s_xve, 1)
                pool.wait_ge(s_xve, 2 * count)
                nc.gpsimd.tensor_tensor(x_rn[:, 0, first:last], x_ve[:, first:last], neg_half[:, 0:last - first], ALU.pow).then_inc(s_xr, 1)
                pool.wait_ge(s_xr, count)
                nc.gpsimd.tensor_tensor(x_rn[:, 1, first:last], neg_mean[:, first:last], x_rn[:, 0, first:last],
                                        ALU.mult).then_inc(s_xnb, 1)

            def x2(b):
                wait(pool, s_yn, 2 * b.n + 2, own=True)
                nc.gpsimd.tensor_tensor(x2_sb[:, tiles_of(b), :], yn[:, :, :], x_sb[:, tiles_of(b), :], ALU.add).then_inc(s_x2, 1)

            def z_rstd(b):
                wait(pool, s_zmv, 2 * b.n + 2, own=True)
                nc.gpsimd.tensor_scalar(z_ve[:, 0, :], z_mv[:, :, 1], EPS, None, ALU.add).then_inc(s_zve, 1)
                nc.gpsimd.tensor_scalar(z_ve[:, 1, :], z_mv[:, :, 1], 1.0 + EPS, EPS * EPS, ALU.mult, ALU.add).then_inc(s_zve, 1)
                nc.gpsimd.tensor_scalar(neg_mean_z[:, :], z_mv[:, :, 0], -1.0, None, ALU.mult).then_inc(s_zve, 1)
                wait(pool, s_zve, 3 * b.n + 3, own=True)
                nc.gpsimd.tensor_tensor(z_r[:, :, :].rearrange("p a t -> p (a t)"), z_ve[:, :, :].rearrange("p a t -> p (a t)"),
                                        neg_half[:, 0:2 * QT], ALU.pow).then_inc(s_zr, 1)
                wait(pool, s_zr, b.n + 1, own=True)
                nc.gpsimd.tensor_tensor(z_nb[:, :], neg_mean_z[:, :], z_r[:, 0, :], ALU.mult).then_inc(s_znb, 1)

            def copy_rows(b):
                wait(pool, s_hn, 2 * b.n + 2, own=True)
                nc.gpsimd.tensor_copy(rows[:, b.parity, :, 1, 0:P], rows[:, b.parity, :, 0, 0:P]).then_inc(s_hn2, 1)
                at = rows[:, b.parity, :, :, P + 1]
                nc.gpsimd.tensor_scalar(at, at, float(2 * S), None, ALU.add).then_inc(s_dst, 1)

            def scatter(b):
                wait(pool, s_hn2, b.n + 1, own=True)
                wait(pool, s_dst, b.n + 1, own=True)
                wait(pool, s_w1, b.n + 1, own=True)
                wait(pool, s_slot, b.n + 1, own=True)
                for k in range(TOP):
                    for t in range(QT):
                        j = k * QT + t
                        nc.gpsimd.indirect_dma_start(
                            out=xs[:, :], out_offset=bass.IndirectOffsetOnAxis(ap=slot[:, b.parity, j:j + 1], axis=0),
                            in_=rows[:, b.parity, t, k, :], in_offset=None,
                            bounds_check=EXPERTS * REGION - 1, oob_is_err=False).then_inc(s_scat[b.parity], 16)

            def step(s, a, m, e, c, d, first=False):
                C, D_ = s.plus(-1), s.plus(-2)
                if first:
                    low_part(s.plus(1))
                    x_rstd(2 * QT, NT, 3)
                if d:
                    prev = D_.plus(-1)
                    if not isinstance(prev.n, int) or prev.n >= 0:
                        wait(pool, s_scat[prev.parity], scattered(prev), own=True)
                    rstd(D_, h_mv, h_ve, neg_mean_h, h_r, h_nb, s_hmv, s_hve, s_hr, s_hnb)
                    copy_rows(D_)
                if a:
                    low_part(s.plus(2))
                if c:
                    rstd(C, y_mv, y_ve, neg_mean_y, y_r, y_nb, s_ymv, s_yve, s_yr, s_ynb)
                    x2(C)
                    z_rstd(C)
                if d:
                    scatter(D_)

            nc.gpsimd.memset(neg_half[:, :], -0.5).then_inc(s_stack_ones, 1)
            pool.wait_ge(s_stack_ones, 1)
            x_rstd(0, QT, 1)
            x_rstd(QT, 2 * QT, 2)
            nc.gpsimd.memset(q_stack, 0.0).then_inc(s_stack_ones, 1)
            nc.gpsimd.memset(k_stack, 1.0).then_inc(s_stack_ones, 1)
            nc.gpsimd.memset(v_aug[:, :, :, :, :], 0.0).then_inc(s_vzero, 1)
            pool.wait_ge(s_vzero, 1)
            nc.gpsimd.memset(v_aug[:, :, :, :, HD:HD + 1], 1.0).then_inc(s_vzero, 1)
            nc.gpsimd.memset(rows[:, :, :, :, :], 0.0).then_inc(s_rows0, 1)
            pool.wait_ge(s_rows0, 1)
            pool.wait_ge(s_cst, 16)
            nc.gpsimd.tensor_copy(rows[:, :, :, :, P + 1], cst[:, C_DEST:C_DEST + 8].rearrange("p (a t c) -> p a t c", a=2, t=QT)
                                  ).then_inc(s_rows0, 1)
            pool.wait_ge(s_rows0, 2)
            nc.gpsimd.dma_start(xs[EXPERTS * REGION:EXPERTS * REGION + P, :], cst[:, C_PAD:C_PAD + ROW]).then_inc(s_scat[1], 16)
            pipeline(pool, step)

            pool.wait_ge(s_tab, TABLE_STEPS)

            def scatter_results(t):
                p = t.slot
                wait(pool, s_res, t.n + 1, own=True)
                nc.gpsimd.indirect_dma_start(
                    out=ys[:, :], out_offset=bass.IndirectOffsetOnAxis(ap=dest[:, p:p + 1], axis=0),
                    in_=res[:, p, :], in_offset=None,
                    bounds_check=TOP * TOKENS - 1, oob_is_err=False).then_inc(s_ysc[p], 16)

            def tile_moves(t, first=False, last=False):
                if not first:
                    scatter_results(t.plus(-1))
                if last:
                    scatter_results(t)

            tiles(pool, tile_moves)

            def finish(b):
                n, p = b.n, b.parity
                wait(pool, s_omv, n * 2 + 2, own=True)
                nc.gpsimd.tensor_scalar(o_ve[:, p, :], o_mv[:, p, :, 1], EPS, None, ALU.add).then_inc(s_ove, 1)
                wait(pool, s_ove, n + 1, own=True)
                nc.gpsimd.tensor_tensor(o_r[:, p, :], o_ve[:, p, :], neg_half[:, 0:QT], ALU.pow).then_inc(s_or, 1)
                wait(pool, s_on, n * 2 + 2, own=True)
                wait(pool, s_out[p], b.pair * 16, own=True)
                nc.gpsimd.tensor_tensor(x3[:, p], on[:, p], x2_sb[:, tiles_of(b), :], ALU.add).then_inc(s_x3, 1)

            batches(pool, finish)


def constants(np, tokens, batch, region):
    c = np.zeros((P, C_END), np.float32)
    c[:, C_IDENT:C_IDENT + P] = np.eye(P)
    c[:, C_UPPER:C_UPPER + P] = np.triu(np.ones((P, P)), 1)
    c[:, C_ONES:C_ONES + P] = 1.0
    c[:, C_IOTA:C_IOTA + 16] = np.tile(np.arange(EXPERTS), 2)
    c[:, C_REGION:C_REGION + 16] = np.tile(np.arange(EXPERTS) * region, 2)
    for parity in range(2):
        for t in range(2):
            for k in range(TOP):
                c[:, C_DEST + parity * 4 + t * 2 + k] = k * tokens + (parity - 2) * batch + t * P + np.arange(P)
    c[:, C_LOWER:C_LOWER + 64] = np.tril(np.ones((EXPERTS, EXPERTS))).reshape(-1)
    c[:, C_STEP:C_STEP + 16] = np.arange(16) * P
    c[:, C_TILE:C_TILE + C_PAD - C_TILE] = np.arange(C_PAD - C_TILE)
    c[:, C_PAD + P + 1] = TOP * tokens
    return c


def layouts(np, v):
    d = P
    def halves(w):
        return w.reshape(2, HD, HD, d).transpose(3, 0, 2, 1).reshape(d, d)
    wqk = np.stack([halves(v["L0_attn_w_q"]), halves(v["L0_attn_w_k"])], axis=1)
    gate = v["L0_ffn_gate_proj"].transpose(2, 0, 1)
    up = v["L0_ffn_up_proj"].transpose(2, 0, 1)
    gate_up = np.stack([gate, up], axis=2).reshape(d, -1)
    down = v["L0_ffn_down_proj"].transpose(0, 2, 1)
    down = down.reshape(EXPERTS, -1, P, d).transpose(2, 0, 1, 3).reshape(P, -1)
    norms = np.stack([v["L0_ffn_ln1_g"], v["L0_ffn_ln1_b"], v["L0_ffn_ln2_g"], v["L0_ffn_ln2_b"]], axis=1)
    x = v["L0_attn_hidden_state"]
    tokens = x.shape[0] * x.shape[1]
    return {
        "x": x, "wqk": wqk, "wv": v["L0_attn_w_v"].T, "wo": v["L0_attn_w_o"].T, "attn_w": v["L0_ffn_attn_w"].T,
        "gate_w": v["L0_ffn_gate_w"].T, "norms": norms, "gate_up": gate_up, "down": down,
        "consts": constants(np, tokens, x.shape[1], tokens + P),
    }


def kernel(**inputs):
    import numpy as np
    import concourse.bacc as bacc
    from concourse.bass_utils import run_bass_kernel_spmd

    nc = bacc.Bacc("TRN2", target_bir_lowering=False, num_devices=1)
    arrays, args = {}, []
    for name, a in layouts(np, {k: np.asarray(a) for k, a in inputs.items()}).items():
        a = np.ascontiguousarray(a)
        arrays[f"{name}_dram"] = a
        args.append(nc.dram_tensor(f"{name}_dram", a.shape, F32, kind="ExternalInput").ap())
    out = nc.dram_tensor("out_dram", inputs["L0_attn_hidden_state"].shape, F32, kind="ExternalOutput").ap()
    block_kernel(nc, *args, out)
    r = run_bass_kernel_spmd(nc, [arrays], core_ids=[0])
    return r.results[0]["out_dram"]
```

```python
from contextlib import ExitStack

import concourse.bass as bass
from concourse import mybir

P = 128
F32 = mybir.dt.float32
BF16 = mybir.dt.bfloat16
U32 = mybir.dt.uint32
I32 = mybir.dt.int32
ALU = mybir.AluOpType
ACT = mybir.ActivationFunctionType
AX = mybir.AxisListType

EPS = 1e-5
HEADS = 16
HD = 8
TWO_ONES = 1.0019378662109375
PARTS = 3
STACK = PARTS * PARTS * HD
SHIFT_ROWS = 2
EXPERTS = 8
TOP = 2
LAG = 2
RING = 4
ROW = 132
C_IDENT, C_UPPER, C_ONES, C_IOTA, C_REGION, C_DEST = 0, 128, 256, 384, 400, 416
C_LOWER, C_STEP, C_TILE, C_PAD, C_SHARE, C_END = 424, 488, 504, 544, 676, 684


class Batch:

    def __init__(self, n, parity, pair):
        self.n, self.parity, self.pair = n, parity, pair

    def plus(self, d):
        p = self.parity + d
        return Batch(self.n + d, p % 2, self.pair + p // 2)


def fixed(n):
    return Batch(n, n % 2, n // 2)


class Tile:

    def __init__(self, n, slot, round_):
        self.n, self.slot, self.parity, self.round = n, slot, slot % 2, round_

    def plus(self, d):
        s = self.slot + d
        return Tile(self.n + d, s % RING, self.round + s // RING)


def fixed_tile(n):
    return Tile(n, n % RING, n // RING)


def block_kernel(nc, x, wqk, wv, wo, attn_w, gate_w, norms, gate_up, down, consts, out):
    NB, S, D = x.shape
    QT = S // P
    NT = NB * QT
    TOKENS = NB * S
    INTER = down.shape[1] // EXPERTS
    IC = INTER // P
    REGION = TOKENS + P
    TILES = (TOP * TOKENS + EXPERTS * (P - 1)) // P
    ROUNDS = -(-TILES // RING)
    SCALE = 1.0 / float(D) ** 0.5
    SCATTER = TOP * QT * 16
    TABLE_STEPS = 15
    assert D == P and QT == 2 and HEADS * HD == D and (EXPERTS - 1) * (REGION // P) + NT <= 256

    xs = nc.dram_tensor("routed_rows", [EXPERTS * REGION + P, ROW], F32, kind="Internal").ap()
    parts_dram = nc.dram_tensor("qk_parts", [2, 2, 2, PARTS, P // 2, S], BF16, kind="Internal").ap()
    ys = nc.dram_tensor("routed_results", [TOP * TOKENS, D], F32, kind="Internal").ap()

    ctx = ExitStack()
    with ctx:
        def sb(name, shape, dt=F32):
            return ctx.enter_context(nc.sbuf_tensor(name, shape, dt))

        def bank(name):
            return ctx.enter_context(nc.psum_tensor(name, [P, 512], F32))

        def sem(name):
            return ctx.enter_context(nc.semaphore(name))

        cst = sb("cst", [P, C_END])
        ident = cst[:, C_IDENT:C_IDENT + P]
        iota8 = cst[:, C_IOTA:C_IOTA + 16].rearrange("p (t e) -> p t e", e=EXPERTS)
        region_base = cst[:, C_REGION:C_REGION + 16]
        ident_b = sb("ident_b", [P, P], BF16)
        upper_b = sb("upper_b", [P, P], BF16)
        ones_b = sb("ones_b", [P, P], BF16)
        neg_half = sb("neg_half", [P, NT])
        table_loaded = sb("table_loaded", [P, 2])
        neg_one = sb("neg_one", [P, QT])
        neg_mean = sb("neg_mean", [P, NT])
        neg_mean_y, neg_mean_h = sb("neg_mean_y", [P, QT]), sb("neg_mean_h", [P, QT])
        wqk_sb = sb("wqk_sb", [P, 2, P])
        wv_sb = sb("wv_sb", [P, P])
        wo_sb = sb("wo_sb", [P, P])
        attn_w_sb = sb("attn_w_sb", [P, P])
        gate_w_sb = sb("gate_w_sb", [P, EXPERTS])
        norms_sb = sb("norms_sb", [P, 4])

        x_sb = sb("x_sb", [P, NT, D])
        x2_sb = sb("x2_sb", [P, NT, D])
        h_sb = sb("h_sb", [P, NT, D])

        x_st = sb("x_st", [P, NT, 6])
        x_mv = sb("x_mv", [P, NT, 2])
        x_ve = sb("x_ve", [P, NT])
        x_rn = sb("x_rn", [P, 2, NT])
        x_now = sb("x_now", [P, 2, 2, QT])
        xn = sb("xn", [P, QT, D])
        xnT = sb("xnT", [P, 2, S])
        parts = sb("parts", [P, 2, 2, PARTS, S], BF16)
        rest1 = sb("rest1", [P, 2, S])
        stacks = sb("stacks", [P, 2, 2, HEADS, S], BF16)
        q_stack, k_stack = stacks[:, 0], stacks[:, 1]
        neg_max = sb("neg_max", [P, 2, QT, HEADS])
        shift = sb("shift", [P, 2, QT, SHIFT_ROWS, HD], BF16)
        shiftT = sb("shiftT", [16, 2, S], BF16)
        v_aug = sb("v_aug", [P, 2, QT, HEADS, 32])
        probs = sb("probs", [P, 8, QT, S])
        u_sb = sb("u_sb", [P, 4, S])
        den_r = sb("den_r", [P, QT, HEADS])
        ctx_sb = sb("ctx_sb", [P, QT, D])
        ctxT = sb("ctxT", [P, S])
        y_st = sb("y_st", [P, QT, 6])
        y_mv = sb("y_mv", [P, QT, 2])
        y_ve = sb("y_ve", [P, QT])
        y_r = sb("y_r", [P, QT])
        y_nb = sb("y_nb", [P, QT])
        yn = sb("yn", [P, QT, D])
        z_st = sb("z_st", [P, QT, 6])
        z_mv = sb("z_mv", [P, QT, 2])
        z_ve = sb("z_ve", [P, 2, QT])
        z_r = sb("z_r", [P, 2, QT])
        z_std = sb("z_std", [P, QT])
        z_ratio = sb("z_ratio", [P, QT])
        zn = sb("zn", [P, QT, D])
        znT = sb("znT", [P, S])
        h_st = sb("h_st", [P, QT, 6])
        h_mv = sb("h_mv", [P, QT, 2])
        h_ve = sb("h_ve", [P, QT])
        h_r = sb("h_r", [P, QT])
        h_nb = sb("h_nb", [P, QT])
        rows = sb("rows", [P, 2, QT, TOP, ROW])
        tT = sb("tT", [P, S])
        top8 = sb("top8", [P, QT, 8])
        idx8 = sb("idx8", [P, QT, 8], U32)
        chosen = sb("chosen", [P, TOP, QT, EXPERTS])
        chosen_b = sb("chosen_b", [P, 2, QT, EXPERTS], BF16)
        in_batch = sb("in_batch", [P, EXPERTS], BF16)
        before = sb("before", [P, 2, EXPERTS], BF16)
        gap = sb("gap", [P, QT])
        gap_e = sb("gap_e", [P, QT])
        gap_s = sb("gap_s", [P, QT])
        place_c = sb("place_c", [P, TOP, 16])
        slot = sb("slot", [P, 2, TOP * QT], U32)

        gate_up_sb = sb("gate_up_sb", [P, EXPERTS * 2 * INTER])
        down_sb = sb("down_sb", [P, EXPERTS * INTER])
        cnt = sb("cnt", [P, EXPERTS])
        tile_gt = sb("tile_gt", [P, EXPERTS, 16])
        n_tiles = sb("n_tiles", [P, EXPERTS])
        tile_lo = sb("tile_lo", [P, EXPERTS, EXPERTS])
        tile_end = sb("tile_end", [P, EXPERTS])
        past = sb("past", [P, TILES, EXPERTS])
        past_n = sb("past_n", [P, TILES, EXPERTS])
        tile_e = sb("tile_e", [P, TILES])
        tile_s = sb("tile_s", [P, TILES])
        tile_w = sb("tile_w", [P, 2, TILES])
        tile_row = sb("tile_row", [P, 2, TILES])
        table = sb("table", [P, 3, TILES], I32)
        pad_f = sb("pad_f", [P, EXPERTS])
        pad_at = sb("pad_at", [P, EXPERTS], I32)
        rows_in = sb("rows_in", [P, RING, ROW])
        w_now = sb("w_now", [P, 2, 2 * INTER])
        rT = sb("rT", [P, 2, P])
        silu = sb("silu", [P, 2, INTER])
        hidT = sb("hidT", [P, 2, INTER])
        dest = sb("dest", [P, RING], U32)
        weight = sb("weight", [P, RING])
        res = sb("res", [P, RING, D])
        room = stacks[:, :, :, :, :].rearrange("p w a h s -> p (w a h s)").bitcast(F32)
        ya = room[:, 0:TOP * NT * D].rearrange("p (c t d) -> p c t d", c=TOP, d=D)
        o1 = on = room[:, TOP * NT * D:(TOP + 1) * NT * D].rearrange("p (t d) -> p t d", d=D)
        o2 = x3 = room[:, (TOP + 1) * NT * D:(TOP + 2) * NT * D].rearrange("p (t d) -> p t d", d=D)
        o_st = sb("o_st", [P, NT, 6])
        o_mv = sb("o_mv", [P, NT, 2])
        o_ve = sb("o_ve", [P, NT])
        neg_mean_o = sb("neg_mean_o", [P, NT])
        o_r = sb("o_r", [P, NT])
        o_nb = sb("o_nb", [P, NT])

        ps = [bank(f"ps{i}") for i in range(8)]
        ps_max, ps_exp, ps_pv, ps_a, ps_c, ps_d = ps[0:2], ps[2:4], ps[4], ps[5], ps[6], ps[7]
        ps_gate, ps_up, ps_rT, ps_res = ps[0:2], ps[2:4], ps[4:6], ps[6:8]

        s_cst, s_wqk, s_wvo, s_wffn = sem("consts_in"), sem("wqk_in"), sem("small_weights_in"), sem("ffn_weights_in")
        s_xin = [sem("x_in_0"), sem("x_in_1"), sem("x_in_rest")]
        s_ones_1 = sem("stack_ones_odd")
        s_const_b, s_stack_ones, s_vzero, s_rows0 = sem("bf16_consts"), sem("stack_ones"), sem("v_ones"), sem("rows_cleared")
        s_xst, s_xmv, s_xve, s_xr = sem("x_stats"), sem("x_mean_var"), sem("x_var_eps"), sem("x_rstd")
        s_half = sem("exponents_ready")
        s_xnb, s_xnow, s_ynb, s_znb, s_hnb = sem("x_bias"), sem("x_scales_at_hand"), sem("y_bias"), sem("z_std_and_ratio"), sem("h_bias")
        s_xn, s_xnT_ps, s_xnT = sem("x_normed"), sem("xT_in_psum"), sem("xT_in_sbuf")
        s_qk_ps, s_hi, s_rest, s_mid, s_lo = sem("qk_in_psum"), sem("high_part"), sem("rest_after_high"), sem("middle_part"), sem("low_part")
        s_parts = [sem("parts_in_dram_0"), sem("parts_in_dram_1")]
        s_stack = [[sem(f"stack_in_{p}{f}") for f in range(2)] for p in range(2)]
        s_v_ps, s_v = sem("v_in_psum"), sem("v_in_sbuf")
        s_smax_ps, s_smax = sem("max_scores_in_psum"), sem("max_found")
        s_sh_hi, s_sh, s_shT_ps, s_shT = sem("shift_high"), sem("shift_low"), sem("shiftT_in_psum"), sem("shiftT_in_sbuf")
        s_shin = [sem("shift_rows_in_0"), sem("shift_rows_in_1")]
        s_sexp_ps, s_exp, s_pv = sem("exp_scores_in_psum"), sem("probs_ready"), sem("pv_group_done")
        s_u = sem("pv_bank_copied")
        s_uT, s_den, s_ctx = sem("ctx_tile_in_psum"), sem("denominators_inverted"), sem("ctx_tile_ready")
        s_ctxT_ps, s_ctxT, s_y_ps = sem("ctxT_in_psum"), sem("ctxT_in_sbuf"), sem("y_in_psum")
        s_yst, s_ymv, s_yve, s_yr, s_yn, s_x2 = sem("y_stats"), sem("y_mean_var"), sem("y_var_eps"), sem("y_rstd"), sem("y_normed"), sem("x2_ready")
        s_zst, s_zmv, s_zve, s_zr, s_zn = sem("x2_stats"), sem("x2_mean_var"), sem("x2_var_eps"), sem("x2_rstd"), sem("z_normed")
        s_znT_ps, s_znT, s_aw_ps, s_h = sem("znT_in_psum"), sem("znT_in_sbuf"), sem("attn_w_in_psum"), sem("h_ready")
        s_hst, s_hmv, s_hve, s_hr, s_hn = sem("h_stats"), sem("h_mean_var"), sem("h_var_eps"), sem("h_rstd"), sem("h_normed")
        s_tT_ps, s_tT, s_lg_ps = sem("tT_in_psum"), sem("tT_in_sbuf"), sem("logits_in_psum")
        s_top, s_idx, s_oh, s_chb, s_inb, s_bef = sem("top_values"), sem("top_indices"), sem("one_hots"), sem("chosen_bf16"), sem("batch_counted"), sem("counts_before")
        s_gap, s_gape, s_gaps, s_w0, s_w1 = sem("logit_gap"), sem("gap_exp"), sem("gap_sum"), sem("weight_0"), sem("weight_1")
        s_pl_ps, s_pl, s_slot = sem("places_in_psum"), sem("chosen_places_in_sbuf"), sem("slots_ready")
        s_hn2, s_dst = sem("rows_copied"), sem("destinations_written")
        s_scat = [sem("rows_scattered_0"), sem("rows_scattered_1")]
        s_cnt_ps, s_tab = sem("counts_in_psum"), sem("table_step")
        s_pad_at, s_pad = sem("ends_of_filled_rows"), sem("padding_written")
        s_rin = [sem(f"rows_in_{i}") for i in range(RING)]
        s_wn, s_rT_ps, s_rT = sem("expert_weights_placed"), sem("rowsT_in_psum"), sem("rowsT_in_sbuf")
        s_gate, s_up, s_silu, s_hid = sem("gate_in_psum"), sem("up_in_psum"), sem("silu_ready"), sem("hidden_ready")
        s_res_ps, s_aux, s_res = sem("result_in_psum"), sem("weight_and_destination"), sem("result_ready")
        s_ysc = [sem(f"results_scattered_{i}") for i in range(RING)]
        s_ya = [sem(f"results_in_{i}") for i in range(NB // 2)]
        s_o1, s_o2, s_ost, s_omv, s_ove, s_or, s_on, s_x3 = (sem("h_plus_first"), sem("ffn_out"), sem("ffn_stats"), sem("ffn_mean_var"),
                                                            sem("ffn_var_eps"), sem("ffn_rstd"), sem("ffn_normed"), [sem("x3_ready_even"), sem("x3_ready_odd")])
        s_onb, s_out = sem("ffn_bias"), sem("out_written")

        block = ctx.enter_context(nc.Block())

        def k_ones(parity):
            return stacks[:, 1, parity].rearrange("p h s -> p (h s)").bitcast(F32)

        def tiles_of(b):
            return at(b.n * QT, QT)

        UT = 2 * QT

        UNITS = NT // UT

        def unit(u):
            return slice(u * UT, u * UT + UT)

        def tile_at(b, t):
            return at(b.n * QT + t)

        def scattered(b):
            return SCATTER * (b.pair + 1) + 16

        def wait(eng, s, value, own=False):
            if not isinstance(value, int) or value > 0:
                eng.wait_ge(s, value)
                if own and not isinstance(value, int):
                    eng.nop(nofuse=True)

        def pipeline(eng, step):
            step(fixed(-1), a=True, m=True, e=False, c=False, d=False, first=True)
            step(fixed(0), a=True, m=True, e=True, c=False, d=False)
            step(fixed(1), a=True, m=True, e=True, c=True, d=False)
            with eng.Fori(0, (NB - 4) // 2) as i:
                step(Batch(i * 2 + 2, 0, i + 1), a=True, m=True, e=True, c=True, d=True)
                step(Batch(i * 2 + 3, 1, i + 1), a=True, m=True, e=True, c=True, d=True)
            step(fixed(NB - 2), a=False, m=True, e=True, c=True, d=True)
            step(fixed(NB - 1), a=False, m=False, e=True, c=True, d=True)
            step(fixed(NB), a=False, m=False, e=False, c=True, d=True)
            step(fixed(NB + 1), a=False, m=False, e=False, c=False, d=True)

        def max_turn(s, m, e, h):
            if h < LAG:
                return (s, HEADS - LAG + h) if e else None
            return (s.plus(1), h - LAG) if m else None

        def write_padding(eng, experts):
            eng.wait_ge(s_pad_at, 1)
            for e in experts:
                row = eng.value_load(pad_at[0:1, e:e + 1], min_val=0, max_val=EXPERTS * REGION - P)
                eng.dma_start(xs[bass.ds(row, P), :], cst[:, C_PAD:C_PAD + ROW]).then_inc(s_pad, 16)

        def tiles(eng, body):
            for n in range(RING):
                body(fixed_tile(n), first=n == 0)
            with eng.Fori(1, ROUNDS - 1) as i:
                for slot in range(RING):
                    body(Tile(i * RING + slot, slot, i))
            for n in range((ROUNDS - 1) * RING, TILES):
                body(fixed_tile(n), last=n == TILES - 1)

        def at(n, k=1):
            return slice(n, n + k) if isinstance(n, int) else bass.ds(n, k)

        @block.sync
        def _(sp):
            sp.dma_start(x_sb[:, 0:QT, :], x[0].rearrange("(t p) d -> p t d", p=P)).then_inc(s_xin[0], 16)
            sp.dma_start(cst[:, :], consts).then_inc(s_cst, 16)
            sp.dma_start(wqk_sb[:, :, :], wqk).then_inc(s_wqk, 16)
            sp.dma_start(x_sb[:, QT:2 * QT, :], x[1].rearrange("(t p) d -> p t d", p=P)).then_inc(s_xin[1], 16)
            sp.dma_start(wv_sb[:, :], wv).then_inc(s_wvo, 16)
            sp.dma_start(wo_sb[:, :], wo).then_inc(s_wvo, 16)
            sp.dma_start(attn_w_sb[:, :], attn_w).then_inc(s_wvo, 16)
            sp.dma_start(gate_w_sb[:, :], gate_w).then_inc(s_wvo, 16)
            sp.dma_start(norms_sb[:, :], norms).then_inc(s_wvo, 16)
            sp.dma_start(x_sb[:, 2 * QT:NT, :], x[2:NB].rearrange("b (t p) d -> p (b t) d", p=P)).then_inc(s_xin[2], 16)

            def send_parts(b):
                wait(sp, s_lo, b.n + 1, own=True)
                for f in range(2):
                    sp.dma_start(parts_dram[b.parity, f].rearrange("w i c t -> c (w i) t"),
                                 parts[64 * f:64 * f + 64, b.parity].rearrange("c w i t -> c (w i) t")).then_inc(s_parts[f], 16)

            def stack(b, f, between=lambda: None):
                wait(sp, s_parts[f], 16 * (b.n + 1), own=True)
                wait(sp, s_sexp_ps, (b.n - 2) * HEADS + HD * f + HD, own=True)
                k_parts = parts_dram[b.parity, f, 1].rearrange("i (d s) t -> (i d) (s t)", s=HD)
                sp.dma_start(k_stack[0:STACK, b.parity, HD * f:HD * f + HD, :],
                             k_parts.unsqueeze(0).to_broadcast([PARTS, PARTS * HD, HD * S])).then_inc(s_stack[b.parity][f], 16)
                for i in range(PARTS):
                    if i == 1:
                        between()
                    q_part = parts_dram[b.parity, f, 0, i].rearrange("(d s) t -> d (s t)", s=HD)
                    sp.dma_start(q_stack[24 * i:24 * i + 24, b.parity, HD * f:HD * f + HD, :],
                                 q_part.unsqueeze(0).to_broadcast([PARTS, HD, HD * S])).then_inc(s_stack[b.parity][f], 16)

            def shift_rows(b, f):
                wait(sp, s_shT, 2 * b.n + f + 1, own=True)
                sp.dma_start(q_stack[STACK:STACK + SHIFT_ROWS, b.parity, HD * f:HD * f + HD, :], shiftT[:, f, :]
                             ).then_inc(s_shin[f], 16)

            def step(s, a, m, e, c, d, first=False):
                if first:
                    for b in (s.plus(1), s.plus(2)):
                        send_parts(b)
                        if b.parity == 1:
                            sp.wait_ge(s_ones_1, 1)
                        stack(b, 0)
                        stack(b, 1)
                    shift_rows(s.plus(1), 0)
                    return
                if e:
                    shift_rows(s, 1)
                    for w_sb, w in ((gate_up_sb, gate_up), (down_sb, down)):
                        share = w.shape[1] // NB
                        cols = slice(s.n * share, s.n * share + share) if isinstance(s.n, int) else bass.ds(s.n * share, share)
                        sp.dma_start(w_sb[:, cols], w[:, cols]).then_inc(s_wffn, 16)
                if a:
                    send_parts(s.plus(2))
                    stack(s.plus(2), 0, between=lambda: shift_rows(s.plus(1), 0))
                elif m:
                    shift_rows(s.plus(1), 0)
                if a:
                    stack(s.plus(2), 1)

            sp.wait_ge(s_stack_ones, 2)
            pipeline(sp, step)

            write_padding(sp, range(0, EXPERTS, 2))
            sp.wait_ge(s_pad, 16 * EXPERTS)
            for p in range(2):
                sp.wait_ge(s_scat[p], scattered(fixed(NB - 2 + p)))
            sp.wait_ge(s_tab, TABLE_STEPS)

            def load_rows(t, first=False, last=False):
                row = sp.value_load(table[0:1, 0, at(t.n)], min_val=0, max_val=EXPERTS * REGION)
                wait(sp, s_rT_ps, t.n - RING + 1, own=True)
                wait(sp, s_aux, t.n - RING + 1, own=True)
                sp.dma_start(rows_in[:, t.slot, :], xs[bass.ds(row, P), :]).then_inc(s_rin[t.slot], 16)

            tiles(sp, load_rows)

            for slot_ in range(RING):
                sp.wait_ge(s_ysc[slot_], len(range(slot_, TILES, RING)) * 16)
            ys_v = ys.rearrange("(c t p) d -> p c t d", c=TOP, p=P)
            out_v = out.rearrange("b (t p) d -> p (b t) d", p=P)

            for u in range(UNITS):
                for c in range(TOP):
                    sp.dma_start(ya[:, c, unit(u), :], ys_v[:, c, unit(u), :]).then_inc(s_ya[u], 16)
            for k in range(NB):
                sp.wait_ge(s_x3[k % 2], k // 2 + 1)
                sp.dma_start(out_v[:, k * QT:k * QT + QT, :], x3[:, k * QT:k * QT + QT, :]).then_inc(s_out, 16)
            sp.wait_ge(s_out, 16 * NB)

        @block.tensor
        def _(pe):
            def shift_T(b, f, before_this):
                pe.wait_ge(s_sh, 2 * b.n + f + 1)
                before_this()
                for t in range(QT):
                    last = nc.tensor.transpose(ps_a[0:16, t * 64:t * 64 + 64].bitcast(BF16),
                                               shift[:, f, t].rearrange("p a b -> p (a b)"), ident_b[:, :])
                last.then_inc(s_shT_ps, 1)

            def x_T(b, before_this):
                wait(pe, s_xn, QT * b.n + QT)
                before_this()
                for t in range(QT):
                    last = nc.tensor.transpose(ps_a[:, t * P:t * P + P], xn[:, t, :], ident)
                last.then_inc(s_xnT_ps, 1)

            def project_qk(b):
                wait(pe, s_xnT, b.n + 1)
                for w in range(2):
                    last = nc.tensor.matmul(ps_a[:, w * S:w * S + S], wqk_sb[:, w, :], xnT[:, b.parity, :], start=True, stop=True)
                last.then_inc(s_qk_ps, 1)

            def project_v(b, before_this):
                before_this()
                for t in range(QT):
                    last = nc.tensor.matmul(ps_a[:, t * P:t * P + P], xnT[:, b.parity, t * P:t * P + P], wv_sb[:, :], start=True, stop=True)
                last.then_inc(s_v_ps, 1)

            def max_scores(b, h):
                if h % 8 == 0:
                    pe.wait_ge(s_stack[b.parity][h // 8], 16 * 4 * (b.pair + 1))
                wait(pe, s_smax, b.n * HEADS + h - 1)
                for t in range(QT):
                    last = nc.tensor.matmul(ps_max[h % 2][:, t * S:t * S + S], q_stack[0:STACK, b.parity, h, t * P:t * P + P],
                                            k_stack[0:STACK, b.parity, h, :], start=True, stop=True)
                last.then_inc(s_smax_ps, 1)

            def exp_scores(b, h):
                if h % 8 == 0:
                    pe.wait_ge(s_shin[h // 8], 16 * b.n + 16)
                wait(pe, s_exp, b.n * HEADS + h - 1)
                for t in range(QT):
                    last = nc.tensor.matmul(ps_exp[h % 2][:, t * S:t * S + S], k_stack[:, b.parity, h, t * P:t * P + P],
                                            q_stack[:, b.parity, h, :], start=True, stop=True)
                last.then_inc(s_sexp_ps, 1)

            def pv(b, g, t):
                if t == 0:
                    if g == 0:
                        wait(pe, s_v, b.n + 1)
                    pe.wait_ge(s_exp, b.n * HEADS + 4 * g + 4)
                    if g % 2 == 0:
                        wait(pe, s_u, 2 * b.n + g // 2)
                for j in range(4):
                    h = 4 * g + j
                    last = nc.tensor.matmul(ps_pv[32 * j:32 * j + 32, (g % 2) * S:(g % 2) * S + S],
                                            v_aug[:, b.parity, t, h, :], probs[:, h % 8, t, :],
                                            start=(t == 0), stop=(t == QT - 1))
                if t == QT - 1:
                    last.then_inc(s_pv, 1)

            def ctx_tile(b, t):
                for g in range(4):
                    last = nc.tensor.transpose(ps_c[:, g * P:g * P + P], u_sb[:, g, t * P:t * P + P], ident)
                last.then_inc(s_uT, 1)

            def ctx_T(b):
                wait(pe, s_ctx, 2 * b.n + 2)
                for t in range(QT):
                    last = nc.tensor.transpose(ps_c[:, t * P:t * P + P], ctx_sb[:, t, :], ident)
                last.then_inc(s_ctxT_ps, 1)

            def two_tiles(b, bank_, ready, value, act, w, n, done):
                wait(pe, ready, value)
                for t in range(QT):
                    last = nc.tensor.matmul(bank_[:, t * n:t * n + n], act[:, t * P:t * P + P], w, start=True, stop=True)
                last.then_inc(done, 1)

            def zn_T(b):
                wait(pe, s_zn, 2 * b.n + 2)
                for t in range(QT):
                    last = nc.tensor.transpose(ps_d[:, t * P:t * P + P], zn[:, t, :], ident)
                last.then_inc(s_znT_ps, 1)

            def h_T(b):
                wait(pe, s_hn, 2 * b.n + 2)
                for t in range(QT):
                    last = nc.tensor.transpose(ps_d[:, t * P:t * P + P], rows[:, b.parity, t, 0, 0:P], ident)
                last.then_inc(s_tT_ps, 1)

            def places(b):
                wait(pe, s_chb, b.n + 1)
                wait(pe, s_bef, b.n)
                nc.tensor.matmul(ps_d[:, 0:16], upper_b[:, :], chosen_b[:, b.parity].rearrange("p t e -> p (t e)"), start=True, stop=False)
                nc.tensor.matmul(ps_d[:, EXPERTS:16], ones_b[:, :], chosen_b[:, b.parity, 0, :], start=False, stop=False)
                for t in range(QT):
                    last = nc.tensor.matmul(ps_d[:, t * EXPERTS:t * EXPERTS + EXPERTS], ones_b[:, :], before[:, b.parity, :],
                                            start=False, stop=t == QT - 1)
                last.then_inc(s_pl_ps, 1)

            def step(s, a, m, e, c, d, first=False):
                A, M, C, D_ = s.plus(2), s.plus(1), s.plus(-1), s.plus(-2)
                nothing = lambda: None
                if first:
                    x_T(M, nothing)
                    project_qk(M)
                    x_T(A, lambda: wait(pe, s_rest, M.n + 1))
                    project_qk(A)
                for h in range(HEADS):
                    turn = max_turn(s, m, e, h)
                    if turn:
                        max_scores(*turn)
                    if e:
                        exp_scores(s, h)
                    if h == 0 and c:
                        pv(C, 3, 0)
                    if h == 0 and c:
                        pv(C, 3, 1)
                    if h == 2 and a and e:
                        x_T(A, lambda: wait(pe, s_v, s.n + 1))
                    if h == 2 and d:
                        if not m:
                            wait(pe, s_pl, D_.n)
                        zn_T(D_)
                    if h == 2 and c:
                        wait(pe, s_yn, 2 * C.n)
                        wait(pe, s_u, 2 * C.n + 2)
                        ctx_tile(C, 0)
                    if h == 3 and e:
                        shift_T(s, 1, (lambda: wait(pe, s_xnT, A.n + 1)) if a else (lambda: wait(pe, s_v, s.n + 1)))
                    if h == 4 and d:
                        two_tiles(D_, ps_d, s_znT, D_.n + 1, znT, attn_w_sb[:, :], P, s_aw_ps)
                    if h == 4 and c:
                        wait(pe, s_ctx, 2 * C.n + 1)
                        ctx_tile(C, 1)
                    if h == 5 and a and e:
                        wait(pe, s_shT, 2 * s.n + 2)
                        project_qk(A)
                    if h == 6 and c:
                        ctx_T(C)
                    if h == 7 and e:
                        pv(s, 0, 0)
                    if h == 7 and e:
                        pv(s, 0, 1)
                    if h == 8 and c:
                        two_tiles(C, ps_c, s_ctxT, C.n + 1, ctxT, wo_sb[:, :], P, s_y_ps)
                    if h == 8 and e:
                        pv(s, 1, 0)
                    if h == 9 and d:
                        h_T(D_)
                    if h == 9 and e:
                        pv(s, 1, 1)
                    if h == 10 and m:
                        shift_T(M, 0, (lambda: wait(pe, s_rest, A.n + 1)) if a else (lambda: wait(pe, s_shT, 2 * s.n + 2)))
                    if h == 11 and d:
                        two_tiles(D_, ps_d, s_tT, D_.n + 1, tT, gate_w_sb[:, :], EXPERTS, s_lg_ps)
                    if h == 12 and e:
                        pv(s, 2, 0)
                    if h == 14 and m:
                        project_v(M, lambda: wait(pe, s_shT, 2 * M.n + 1))
                    if h == 14 and e:
                        pv(s, 2, 1)
                    if h == 15 and d:
                        places(D_)

            pe.wait_ge(s_cst, 16)
            pe.wait_ge(s_const_b, 4)
            pe.wait_ge(s_wqk, 16)
            pe.wait_ge(s_wvo, 16 * 5)
            pipeline(pe, step)
            pe.wait_ge(s_bef, NB)
            pe.wait_ge(s_pl, NB)
            nc.tensor.matmul(ps_c[:, 0:EXPERTS], ones_b[:, :], before[:, NB % 2, :], start=True, stop=True).then_inc(s_cnt_ps, 1)

            pe.wait_ge(s_tab, TABLE_STEPS)
            pe.wait_ge(s_wffn, 32 * NB)

            def rows_T(t):
                p = t.parity
                wait(pe, s_rin[t.slot], t.round * 16 + 16)
                wait(pe, s_rT, t.n - 1)
                nc.tensor.transpose(ps_rT[p][:, 0:P], rows_in[:, t.slot, 0:P], ident).then_inc(s_rT_ps, 1)

            def gate_and_up(t):
                p = t.parity
                wait(pe, s_wn, t.n + 1)
                wait(pe, s_rT, t.n + 1)
                wait(pe, s_hid, t.n - 1)
                for half, (bank_, done) in enumerate(((ps_gate, s_gate), (ps_up, s_up))):
                    for k in range(IC):
                        last = nc.tensor.matmul(bank_[p][:, k * P:k * P + P],
                                                w_now[:, p, half * INTER + k * P:half * INTER + k * P + P],
                                                rT[:, p, :], start=True, stop=True)
                    last.then_inc(done, 1)

            def down_product(t):
                p = t.parity
                col = pe.value_load(table[0:1, 2, at(t.n)], min_val=0, max_val=(EXPERTS - 1) * INTER)
                wait(pe, s_hid, t.n + 1)
                wait(pe, s_res, t.n - 1)
                for k in range(IC):
                    last = nc.tensor.matmul(ps_res[p][:, 0:P], hidT[:, p, k * P:k * P + P],
                                            down_sb[:, bass.ds(col + k * P, P)], start=(k == 0), stop=(k == IC - 1))
                last.then_inc(s_res_ps, 1)

            def tile_products(t, first=False, last=False):
                if first:
                    rows_T(t)
                if not last:
                    rows_T(t.plus(1))
                gate_and_up(t)
                if not first:
                    down_product(t.plus(-1))
                if last:
                    down_product(t)

            tiles(pe, tile_products)

        @block.scalar
        def _(act):
            def x_T(b):
                wait(act, s_xnT_ps, b.n + 1)
                nc.scalar.copy(xnT[:, b.parity, :], ps_a[:, 0:S]).then_inc(s_xnT, 1)

            def high_part(b):
                wait(act, s_qk_ps, b.n + 1)
                nc.scalar.copy(parts[:, b.parity, :, 0, :], ps_a[:, :].rearrange("p (w t) -> p w t", w=2)).then_inc(s_hi, 1)

            def middle_part(b):
                wait(act, s_rest, b.n + 1)
                nc.scalar.copy(parts[:, b.parity, :, 1, :], rest1[:, :, :]).then_inc(s_mid, 1)

            def normed(src, dst, r, nb, done):
                for t in range(QT):
                    nc.scalar.activation(dst(t), src(t), ACT.Identity, bias=nb(t), scale=r(t)).then_inc(done, 1)

            def x_normed(b):
                wait(act, s_xnow, b.n + 1)
                wait(act, s_xnT_ps, b.n)
                now = x_now[:, b.parity]
                normed(lambda t: x_sb[:, tile_at(b, t), :], lambda t: xn[:, t, :],
                       lambda t: now[:, 0, t:t + 1], lambda t: now[:, 1, t:t + 1], s_xn)

            def y_normed(b):
                wait(act, s_ynb, b.n + 1)
                normed(lambda t: ps_c[:, t * P:t * P + P], lambda t: yn[:, t, :], lambda t: y_r[:, t:t + 1], lambda t: y_nb[:, t:t + 1], s_yn)

            def h_normed(b):
                wait(act, s_hnb, b.n + 1)
                normed(lambda t: h_sb[:, tile_at(b, t), :], lambda t: rows[:, b.parity, t, 0, 0:P],
                       lambda t: h_r[:, t:t + 1], lambda t: h_nb[:, t:t + 1], s_hn)

            def v_out(b):
                wait(act, s_v_ps, b.n + 1)
                nc.scalar.copy(v_aug[:, b.parity, :, :, 0:HD],
                               ps_a[:, 0:QT * P].rearrange("p (t h d) -> p t h d", t=QT, d=HD)).then_inc(s_v, 1)

            def exps(b, h):
                pe_group = b.n * 4 + h // 4 - 1
                if h % 4 == 0:
                    wait(act, s_pv, pe_group)
                act.wait_ge(s_sexp_ps, b.n * HEADS + h + 1)
                nc.scalar.activation(probs[:, h % 8, :, :].rearrange("p t s -> p (t s)"), ps_exp[h % 2][:, :], ACT.Exp,
                                     scale=SCALE).then_inc(s_exp, 1)

            def pv_out(b, k):
                wait(act, s_pv, b.n * 4 + 2 * k + 2)
                if k == 0:
                    wait(act, s_uT, 2 * b.n)
                nc.scalar.copy(u_sb[:, 2 * k:2 * k + 2, :].rearrange("p g s -> p (g s)"), ps_pv[:, :]).then_inc(s_u, 1)

            def ctx_T(b):
                wait(act, s_ctxT_ps, b.n + 1)
                nc.scalar.copy(ctxT[:, :], ps_c[:, 0:S]).then_inc(s_ctxT, 1)

            def affine(b, ready, dst, done, k):
                wait(act, ready, b.n + 1)
                nc.scalar.activation(dst, ps_d[:, 0:S], ACT.Identity, bias=norms_sb[:, k + 1:k + 2],
                                     scale=norms_sb[:, k:k + 1]).then_inc(done, 1)

            def shift_out(b, f):
                wait(act, s_shT_ps, 2 * b.n + f + 1)
                wait(act, s_shin[f], 16 * b.n)
                nc.scalar.copy(shiftT[:, f, :], ps_a[0:16, 0:128].bitcast(BF16)).then_inc(s_shT, 1)

            def gap_exp(b):
                wait(act, s_gap, b.n + 1)
                nc.scalar.activation(gap_e[:, :], gap[:, :], ACT.Exp).then_inc(s_gape, 1)

            def step(s, a, m, e, c, d, first=False):
                A, M, C, D_ = s.plus(2), s.plus(1), s.plus(-1), s.plus(-2)
                if first:
                    x_normed(M)
                    x_T(M)
                    x_normed(A)
                    high_part(M)
                    middle_part(M)
                    x_T(A)
                    high_part(A)
                    middle_part(A)
                    act.wait_ge(s_vzero, 2)
                    act.wait_ge(s_wvo, 16 * 5)
                for h in range(HEADS):
                    if e:
                        exps(s, h)
                    if h == 0 and a and e:
                        x_normed(A)
                    if h == 0 and c:
                        pv_out(C, 1)
                    if h == 1 and a and e:
                        x_T(A)
                    if h == 2 and d:
                        affine(D_, s_znT_ps, znT[:, :], s_znT, 0)
                    if h == 3 and e:
                        shift_out(s, 1)
                    if h == 5 and a and e:
                        high_part(A)
                    if h == 7 and c:
                        ctx_T(C)
                    if h == 7 and a and e:
                        middle_part(A)
                    if h == 8 and d:
                        h_normed(D_)
                    if h == 9 and d:
                        affine(D_, s_tT_ps, tT[:, :], s_tT, 2)
                    if h == 9 and e:
                        pv_out(s, 0)
                    if h == 11 and c:
                        y_normed(C)
                    if h == 12 and m:
                        shift_out(M, 0)
                    if h == 15 and d:
                        gap_exp(D_)
                    if h == 15 and m:
                        v_out(M)

            act.wait_ge(s_half, 1)
            nc.scalar.activation(table_loaded[:, 0:1], neg_half[:, 0:1], ACT.Exp)
            pipeline(act, step)

            write_padding(act, range(1, EXPERTS, 2))
            nc.scalar.activation(table_loaded[:, 1:2], neg_half[:, 0:1], ACT.Silu)

            def row_T(t):
                wait(act, s_rT_ps, t.n + 1)
                wait(act, s_up, t.n - 1)
                nc.scalar.activation(rT[:, t.parity, :], ps_rT[t.parity][:, 0:P], ACT.Identity, bias=norms_sb[:, 3:4],
                                     scale=norms_sb[:, 2:3]).then_inc(s_rT, 1)

            def silu_of(t, first=False, last=False):
                if first:
                    row_T(t)
                if not last:
                    row_T(t.plus(1))
                wait(act, s_gate, t.n + 1)
                wait(act, s_hid, t.n - 1)
                nc.scalar.activation(silu[:, t.parity, :], ps_gate[t.parity][:, :], ACT.Silu).then_inc(s_silu, 1)

            tiles(act, silu_of)

            for u in range(UNITS):
                act.wait_ge(s_onb, u + 1)
                for t in range(u * UT, u * UT + UT):
                    nc.scalar.activation(on[:, t, :], o2[:, t, :], ACT.Identity, bias=o_nb[:, t:t + 1],
                                         scale=o_r[:, t:t + 1]).then_inc(s_on, 1)

        @block.vector
        def _(dve):
            def stats(src, st, s_st):
                for t in range(QT):
                    nc.vector.bn_stats(st[:, t, :], src(t)).then_inc(s_st, 1)

            def mean_var(b, st, mv, s_st, s_mv):
                wait(dve, s_st, 2 * b.n + 2, own=True)
                for t in range(QT):
                    nc.vector.bn_aggr(mv[:, t, :], st[:, t, :]).then_inc(s_mv, 1)

            def x_stats(first, last):
                for t in range(first, last):
                    nc.vector.bn_stats(x_st[:, t, :], x_sb[:, t, :]).then_inc(s_xst, 1)
                dve.wait_ge(s_xst, last)
                for t in range(first, last):
                    nc.vector.bn_aggr(x_mv[:, t, :], x_st[:, t, :]).then_inc(s_xmv, 1)

            def x_scales(b):
                dve.wait_ge(s_xnb, min(b.n + 1, 3) if isinstance(b.n, int) else 3)
                nc.vector.tensor_copy(x_now[:, b.parity], x_rn[:, :, tiles_of(b)]).then_inc(s_xnow, 1)

            def zn_of(b):
                wait(dve, s_zr, b.n + 1)
                for t in range(QT):
                    nc.vector.tensor_scalar(zn[:, t, :], x2_sb[:, tile_at(b, t), :], z_mv[:, t, 0:1], z_r[:, 1, t:t + 1],
                                            ALU.subtract, ALU.mult).then_inc(s_zn, 1)

            def rest_of(b):
                wait(dve, s_hi, b.n + 1)
                wait(dve, s_lo, b.n)
                nc.vector.tensor_tensor(rest1[:, :, :], ps_a[:, :].rearrange("p (w t) -> p w t", w=2), parts[:, b.parity, :, 0, :],
                                        ALU.subtract).then_inc(s_rest, 1)

            def take_max(b, h):
                dve.wait_ge(s_smax_ps, b.n * HEADS + h + 1)
                nc.vector.tensor_reduce(neg_max[:, b.parity, :, h:h + 1],
                                        ps_max[h % 2][:, :].rearrange("p (t k) -> p t k", t=QT), AX.X, ALU.max,
                                        negate=True).then_inc(s_smax, 1)

            def shift_high(b, f):
                wait(dve, s_smax, b.n * HEADS + 8 * f + 8)
                if f == 0:
                    wait(dve, s_shT_ps, 2 * b.n - 1)
                nc.vector.tensor_copy(shift[:, f, :, 0, :], neg_max[:, b.parity, :, 8 * f:8 * f + 8]).then_inc(s_sh_hi, 1)

            def shift_low(b, f):
                wait(dve, s_sh_hi, 2 * b.n + f + 1)
                nc.vector.tensor_tensor(shift[:, f, :, 1, :], neg_max[:, b.parity, :, 8 * f:8 * f + 8], shift[:, f, :, 0, :],
                                        ALU.subtract).then_inc(s_sh, 1)

            def ctx_tile(b, t):
                wait(dve, s_uT, 2 * b.n + t + 1)
                u = ps_c[:, :].rearrange("p (h r) -> p h r", r=32)
                nc.vector.reciprocal(den_r[:, t, :], u[:, :, HD:HD + 1].rearrange("p h r -> p (h r)")).then_inc(s_den, 1)
                wait(dve, s_den, 2 * b.n + t + 1)
                nc.vector.tensor_tensor(ctx_sb[:, t, :].rearrange("p (h d) -> p h d", d=HD), u[:, :, 0:HD],
                                        den_r[:, t, :].unsqueeze(2).to_broadcast([P, HEADS, HD]), ALU.mult).then_inc(s_ctx, 1)

            def h_out(b):
                wait(dve, s_aw_ps, b.n + 1)
                wait(dve, s_znb, 2 * b.n + 2)
                for t in range(QT):
                    nc.vector.scalar_tensor_tensor(h_sb[:, tile_at(b, t), :], zn[:, t, :], z_ratio[:, t:t + 1],
                                                   ps_d[:, t * P:t * P + P], ALU.mult, ALU.add).then_inc(s_h, 1)

            def top_two(b):
                wait(dve, s_lg_ps, b.n + 1, own=True)
                lg = ps_d[:, 0:QT * EXPERTS].rearrange("p (t e) -> p t e", e=EXPERTS)
                for t in range(QT):
                    nc.vector.max(top8[:, t, :], lg[:, t, :]).then_inc(s_top, 1)
                wait(dve, s_top, 2 * b.n + 2, own=True)
                for t in range(QT):
                    nc.vector.max_index(idx8[:, t, :], top8[:, t, :], lg[:, t, :]).then_inc(s_idx, 1)
                nc.vector.tensor_tensor(gap[:, :], top8[:, :, 1], top8[:, :, 0], ALU.subtract).then_inc(s_gap, 1)

            def one_hots(b):
                wait(dve, s_idx, 2 * b.n + 2)
                nc.vector.tensor_tensor(chosen[:, :, :, :], iota8.unsqueeze(1).to_broadcast([P, TOP, QT, EXPERTS]),
                                        idx8[:, :, 0:TOP].rearrange("p t k -> p k t").unsqueeze(3).to_broadcast([P, TOP, QT, EXPERTS]),
                                        ALU.is_equal).then_inc(s_oh, 1)

            def both_choices(b):
                wait(dve, s_oh, b.n + 1)
                nc.vector.tensor_tensor(chosen_b[:, b.parity], chosen[:, 0], chosen[:, 1], ALU.add).then_inc(s_chb, 1)

            def slots(b):
                wait(dve, s_pl_ps, b.n + 1)
                nc.vector.tensor_tensor(place_c[:, :, :], chosen[:, :, :, :].rearrange("p c t e -> p c (t e)"),
                                        ps_d[:, 0:16].unsqueeze(1).to_broadcast([P, TOP, 16]), ALU.mult).then_inc(s_pl, 1)
                wait(dve, s_pl, b.n + 1)
                with nc.allow_low_precision(reason="the sum is a whole number below 2 ** 24"):
                    nc.vector.tensor_reduce(slot[:, b.parity, :], place_c[:, :, :].rearrange("p c (t e) -> p (c t) e", e=EXPERTS),
                                            AX.X, ALU.add).then_inc(s_slot, 1)
            def step(s, a, m, e, c, d, first=False):
                A, M, C, D_ = s.plus(2), s.plus(1), s.plus(-1), s.plus(-2)
                if first:
                    rest_of(M)
                    nc.vector.memset(k_ones(1), TWO_ONES).then_inc(s_ones_1, 1)
                    rest_of(A)
                    dve.wait_ge(s_xin[2], 16)
                    x_stats(2 * QT, NT)
                for h in range(HEADS):
                    if h == 0 and a and not first:
                        x_scales(A)
                    turn = max_turn(s, m, e, h)
                    if turn:
                        take_max(*turn)
                    if h == 0 and d:
                        zn_of(D_)
                    if h == 2 and e:
                        shift_high(s, 1)
                    if h == 2 and e:
                        shift_low(s, 1)
                    if h == 2 and c:
                        ctx_tile(C, 0)
                    if h == 4 and d:
                        h_out(D_)
                    if h == 4 and c:
                        ctx_tile(C, 1)
                    if h == 5 and d:
                        wait(dve, s_h, 2 * D_.n + 2, own=True)
                        stats(lambda t: h_sb[:, tile_at(D_, t), :], h_st, s_hst)
                    if h == 5 and d:
                        mean_var(D_, h_st, h_mv, s_hst, s_hmv)
                    if h == 6 and a and e:
                        rest_of(A)
                    if h == 8 and c:
                        wait(dve, s_y_ps, C.n + 1, own=True)
                        stats(lambda t: ps_c[:, t * P:t * P + P], y_st, s_yst)
                    if h == 9 and m:
                        shift_high(M, 0)
                    if h == 9 and m:
                        shift_low(M, 0)
                    if h == 9 and c:
                        mean_var(C, y_st, y_mv, s_yst, s_ymv)
                    if h == 11 and d:
                        top_two(D_)
                    if h == 13 and d:
                        one_hots(D_)
                    if h == 13 and c:
                        wait(dve, s_x2, C.n + 1, own=True)
                        stats(lambda t: x2_sb[:, tile_at(C, t), :], z_st, s_zst)
                    if h == 13 and c:
                        mean_var(C, z_st, z_mv, s_zst, s_zmv)
                    if h == 14 and d:
                        both_choices(D_)
                    if h == 15 and d:
                        slots(D_)

            dve.wait_ge(s_cst, 16)
            nc.vector.tensor_copy(ident_b[:, :], ident).then_inc(s_const_b, 1)
            nc.vector.tensor_copy(upper_b[:, :], cst[:, C_UPPER:C_UPPER + P]).then_inc(s_const_b, 1)
            nc.vector.tensor_copy(ones_b[:, :], cst[:, C_ONES:C_ONES + P]).then_inc(s_const_b, 1)
            nc.vector.tensor_copy(before[:, 0, :], cst[:, C_SHARE:C_END]).then_inc(s_const_b, 1)
            for b in range(2):
                dve.wait_ge(s_xin[b], 16)
                x_stats(b * QT, b * QT + QT)
            for b in range(2):
                x_scales(fixed(b))
            nc.vector.memset(k_ones(0), TWO_ONES).then_inc(s_stack_ones, 1)
            pipeline(dve, step)

            steps = [0]

            def link(instruction):
                steps[0] += 1
                instruction.then_inc(s_tab, 1)
                dve.wait_ge(s_tab, steps[0])

            def row_of(column, n):
                return cst[:, column:column + n]

            tri = row_of(C_LOWER, EXPERTS * EXPERTS).rearrange("p (a b) -> p a b", b=EXPERTS)
            dve.wait_ge(s_cnt_ps, 1)
            nc.vector.tensor_copy(pad_at[:, :], ps_c[:, 0:EXPERTS]).then_inc(s_pad_at, 1)
            link(nc.vector.tensor_tensor(cnt[:, :], ps_c[:, 0:EXPERTS], region_base[:, 0:EXPERTS], ALU.subtract))
            link(nc.vector.tensor_tensor(tile_gt[:, :, :], cnt[:, :].unsqueeze(2).to_broadcast([P, EXPERTS, 16]),
                                         row_of(C_STEP, 16).unsqueeze(1).to_broadcast([P, EXPERTS, 16]), ALU.is_gt))
            link(nc.vector.tensor_reduce(n_tiles[:, :], tile_gt[:, :, :], AX.X, ALU.add))
            link(nc.vector.tensor_tensor(tile_lo[:, :, :], n_tiles[:, :].unsqueeze(1).to_broadcast([P, EXPERTS, EXPERTS]), tri, ALU.mult))
            link(nc.vector.tensor_reduce(tile_end[:, :], tile_lo[:, :, :], AX.X, ALU.add))
            link(nc.vector.tensor_tensor(past[:, :, :], row_of(C_TILE, TILES).unsqueeze(2).to_broadcast([P, TILES, EXPERTS]),
                                         tile_end[:, :].unsqueeze(1).to_broadcast([P, TILES, EXPERTS]), ALU.is_ge))
            link(nc.vector.tensor_tensor(past_n[:, :, :], past[:, :, :], n_tiles[:, :].unsqueeze(1).to_broadcast([P, TILES, EXPERTS]),
                                         ALU.mult))
            link(nc.vector.tensor_reduce(tile_e[:, :], past[:, :, :], AX.X, ALU.add))
            link(nc.vector.tensor_reduce(tile_s[:, :], past_n[:, :, :], AX.X, ALU.add))
            link(nc.vector.tensor_tensor(tile_row[:, 0, :], row_of(C_TILE, TILES), tile_s[:, :], ALU.subtract))
            link(nc.vector.tensor_scalar(tile_w[:, 1, :], tile_e[:, :], EXPERTS - 0.5, float(P), ALU.is_lt, ALU.mult))
            link(nc.vector.tensor_tensor(tile_row[:, 1, :], tile_row[:, 0, :], tile_w[:, 1, :], ALU.mult))
            link(nc.vector.scalar_tensor_tensor(table[:, 0, :], tile_e[:, :], float(REGION), tile_row[:, 1, :], ALU.mult, ALU.add))
            link(nc.vector.tensor_scalar(table[:, 1, :], tile_e[:, :], float(EXPERTS - 1), float(2 * INTER), ALU.min, ALU.mult))
            link(nc.vector.tensor_scalar(table[:, 2, :], tile_e[:, :], float(EXPERTS - 1), float(INTER), ALU.min, ALU.mult))
            assert steps[0] == TABLE_STEPS

            dve.wait_ge(s_wffn, 32 * NB)

            def aux(t):
                p = t.slot
                wait(dve, s_rin[p], t.round * 16 + 16)
                wait(dve, s_ysc[p], t.round * 16)
                nc.vector.tensor_copy(dest[:, p:p + 1], rows_in[:, p, P + 1:P + 2])
                nc.vector.tensor_copy(weight[:, p:p + 1], rows_in[:, p, P:P + 1]).then_inc(s_aux, 1)

            def hidden(t):
                p = t.parity
                wait(dve, s_silu, t.n + 1)
                wait(dve, s_up, t.n + 1)
                wait(dve, s_res_ps, t.n - 1)
                nc.vector.tensor_tensor(hidT[:, p, :], ps_up[p][:, :], silu[:, p, :], ALU.mult).then_inc(s_hid, 1)

            def result(t):
                p = t.slot
                wait(dve, s_aux, t.n + 1)
                wait(dve, s_res_ps, t.n + 1)
                nc.vector.tensor_scalar(res[:, p, :], ps_res[t.parity][:, 0:P], weight[:, p:p + 1], None, ALU.mult).then_inc(s_res, 1)

            def place_weights(t):
                col = dve.value_load(table[0:1, 1, at(t.n)], min_val=0, max_val=(EXPERTS - 1) * 2 * INTER)
                wait(dve, s_up, t.n - 1)
                nc.vector.tensor_copy(w_now[:, t.parity, :], gate_up_sb[:, bass.ds(col, 2 * INTER)]).then_inc(s_wn, 1)

            def tile_elementwise(t, first=False, last=False):
                if first:
                    place_weights(t)
                if not last:
                    place_weights(t.plus(1))
                aux(t)
                hidden(t)
                if not first:
                    result(t.plus(-1))
                if last:
                    result(t)

            tiles(dve, tile_elementwise)

            def add_first(u):
                dve.wait_ge(s_ya[u], 32)
                nc.vector.tensor_tensor(o1[:, unit(u), :], ya[:, 0, unit(u), :], h_sb[:, unit(u), :], ALU.add).then_inc(s_o1, 1)

            def odd_x3(u):
                dve.wait_ge(s_on, u * UT + UT)
                tiles_ = slice(u * UT + QT, u * UT + UT)
                nc.vector.tensor_tensor(x3[:, tiles_, :], on[:, tiles_, :], x2_sb[:, tiles_, :], ALU.add).then_inc(s_x3[1], 1)

            add_first(0)
            for u in range(UNITS):
                if u + 1 < UNITS:
                    add_first(u + 1)
                dve.wait_ge(s_o1, u + 1)
                nc.vector.tensor_tensor(o2[:, unit(u), :], ya[:, 1, unit(u), :], o1[:, unit(u), :], ALU.add).then_inc(s_o2, 1)
                dve.wait_ge(s_o2, u + 1)
                for t in range(u * UT, u * UT + UT):
                    nc.vector.bn_stats(o_st[:, t, :], o2[:, t, :]).then_inc(s_ost, 1)
                dve.wait_ge(s_ost, u * UT + UT)
                for t in range(u * UT, u * UT + UT):
                    nc.vector.bn_aggr(o_mv[:, t, :], o_st[:, t, :]).then_inc(s_omv, 1)
                if u > 0:
                    odd_x3(u - 1)
            odd_x3(UNITS - 1)

        @block.gpsimd
        def _(pool):
            def rstd(b, mv, ve, nm, r, nb, s_mv, s_ve, s_r, s_nb):
                wait(pool, s_mv, 2 * b.n + 2, own=True)
                nc.gpsimd.tensor_scalar(ve[:, :], mv[:, :, 1], EPS, None, ALU.add).then_inc(s_ve, 1)
                nc.gpsimd.tensor_scalar(nm[:, :], mv[:, :, 0], -1.0, None, ALU.mult).then_inc(s_ve, 1)
                wait(pool, s_ve, 2 * b.n + 2, own=True)
                nc.gpsimd.tensor_tensor(r[:, :], ve[:, :], neg_half[:, 0:QT], ALU.pow).then_inc(s_r, 1)
                wait(pool, s_r, b.n + 1, own=True)
                nc.gpsimd.tensor_tensor(nb[:, :], nm[:, :], r[:, :], ALU.mult).then_inc(s_nb, 1)

            def low_part(b):
                wait(pool, s_mid, b.n + 1, own=True)
                nc.gpsimd.tensor_tensor(parts[:, b.parity, :, 2, :], rest1[:, :, :], parts[:, b.parity, :, 1, :],
                                        ALU.subtract).then_inc(s_lo, 1)

            def x_rstd(first, last, count):
                pool.wait_ge(s_xmv, last)
                nc.gpsimd.tensor_scalar(x_ve[:, first:last], x_mv[:, first:last, 1], EPS, None, ALU.add).then_inc(s_xve, 1)
                nc.gpsimd.tensor_scalar(neg_mean[:, first:last], x_mv[:, first:last, 0], -1.0, None, ALU.mult).then_inc(s_xve, 1)
                pool.wait_ge(s_xve, 2 * count)
                nc.gpsimd.tensor_tensor(x_rn[:, 0, first:last], x_ve[:, first:last], neg_half[:, 0:last - first], ALU.pow).then_inc(s_xr, 1)
                pool.wait_ge(s_xr, count)
                nc.gpsimd.tensor_tensor(x_rn[:, 1, first:last], neg_mean[:, first:last], x_rn[:, 0, first:last],
                                        ALU.mult).then_inc(s_xnb, 1)

            def x2(b):
                wait(pool, s_yn, 2 * b.n + 2, own=True)
                nc.gpsimd.tensor_tensor(x2_sb[:, tiles_of(b), :], yn[:, :, :], x_sb[:, tiles_of(b), :], ALU.add).then_inc(s_x2, 1)

            def z_rstd(b):
                wait(pool, s_zmv, 2 * b.n + 2, own=True)
                nc.gpsimd.tensor_scalar(z_ve[:, 0, :], z_mv[:, :, 1], EPS, None, ALU.add).then_inc(s_zve, 1)
                nc.gpsimd.tensor_scalar(z_ve[:, 1, :], z_mv[:, :, 1], 1.0 + EPS, EPS * EPS, ALU.mult, ALU.add).then_inc(s_zve, 1)
                wait(pool, s_zve, 2 * b.n + 2, own=True)
                nc.gpsimd.tensor_tensor(z_r[:, :, :].rearrange("p a t -> p (a t)"), z_ve[:, :, :].rearrange("p a t -> p (a t)"),
                                        neg_half[:, 0:2 * QT], ALU.pow).then_inc(s_zr, 1)
                wait(pool, s_zr, b.n + 1, own=True)
                nc.gpsimd.tensor_tensor(z_std[:, :], z_ve[:, 1, :], z_r[:, 1, :], ALU.mult).then_inc(s_znb, 1)
                wait(pool, s_znb, 2 * b.n + 1, own=True)
                nc.gpsimd.tensor_tensor(z_ratio[:, :], z_std[:, :], z_r[:, 0, :], ALU.mult).then_inc(s_znb, 1)

            def copy_rows(b):
                wait(pool, s_hn, 2 * b.n + 2, own=True)
                nc.gpsimd.tensor_scalar(rows[:, b.parity, :, 1, 0:P], rows[:, b.parity, :, 0, 0:P], 1.0, 0.0, ALU.mult, ALU.add).then_inc(s_hn2, 1)
                at = rows[:, b.parity, :, :, P + 1]
                nc.gpsimd.tensor_scalar(at, at, float(2 * S), None, ALU.add).then_inc(s_dst, 1)

            def weights(b):
                wait(pool, s_gape, b.n + 1, own=True)
                nc.gpsimd.tensor_scalar(gap_s[:, :], gap_e[:, :], 1.0, None, ALU.add).then_inc(s_gaps, 1)
                wait(pool, s_gaps, b.n + 1, own=True)
                nc.gpsimd.tensor_tensor(rows[:, b.parity, :, 0, P], gap_s[:, :], neg_one[:, :], ALU.pow).then_inc(s_w0, 1)
                wait(pool, s_w0, b.n + 1, own=True)
                nc.gpsimd.tensor_tensor(rows[:, b.parity, :, 1, P], gap_e[:, :], rows[:, b.parity, :, 0, P], ALU.mult).then_inc(s_w1, 1)

            def counts(b):
                wait(pool, s_pl_ps, b.n + 1, own=True)
                nc.gpsimd.tensor_tensor(in_batch[:, :], chosen_b[:, b.parity, 0, :], chosen_b[:, b.parity, 1, :], ALU.add).then_inc(s_inb, 1)
                wait(pool, s_inb, b.n + 1, own=True)
                nc.gpsimd.tensor_tensor(before[:, 1 - b.parity, :], before[:, b.parity, :], in_batch[:, :], ALU.add).then_inc(s_bef, 1)

            def scatter(b, first, last):
                if first == 0:
                    wait(pool, s_hn2, b.n + 1, own=True)
                    wait(pool, s_dst, b.n + 1, own=True)
                    wait(pool, s_w1, b.n + 1, own=True)
                    wait(pool, s_slot, b.n + 1, own=True)
                for j in range(first, last):
                    k, t = j // QT, j % QT
                    nc.gpsimd.indirect_dma_start(
                        out=xs[:, :], out_offset=bass.IndirectOffsetOnAxis(ap=slot[:, b.parity, j:j + 1], axis=0),
                        in_=rows[:, b.parity, t, k, :], in_offset=None,
                        bounds_check=EXPERTS * REGION - 1, oob_is_err=False).then_inc(s_scat[b.parity], 16)

            def step(s, a, m, e, c, d, first=False):
                C, D_ = s.plus(-1), s.plus(-2)
                if first:
                    low_part(s.plus(1))
                    low_part(s.plus(2))
                    nc.gpsimd.memset(neg_one[:, :], -1.0)
                    nc.gpsimd.memset(v_aug[:, :, :, :, :], 0.0).then_inc(s_vzero, 1)
                    pool.wait_ge(s_vzero, 1)
                    nc.gpsimd.memset(v_aug[:, :, :, :, HD:HD + 1], 1.0).then_inc(s_vzero, 1)
                    nc.gpsimd.memset(rows[:, :, :, :, :], 0.0).then_inc(s_rows0, 1)
                    pool.wait_ge(s_rows0, 1)
                    pool.wait_ge(s_cst, 16)
                    nc.gpsimd.tensor_copy(rows[:, :, :, :, P + 1], cst[:, C_DEST:C_DEST + 8].rearrange("p (a t c) -> p a t c", a=2, t=QT)
                                          ).then_inc(s_rows0, 1)
                    pool.wait_ge(s_rows0, 2)
                    for p in range(2):
                        first_row = EXPERTS * REGION + p * P // 2
                        nc.gpsimd.dma_start(xs[first_row:first_row + P // 2, :], cst[0:P // 2, C_PAD:C_PAD + ROW]).then_inc(s_scat[p], 16)
                    x_rstd(2 * QT, NT, 3)
                tail = not e and not first
                if d:
                    wait(pool, s_scat[D_.parity], scattered(D_.plus(-2)), own=True)
                    rstd(D_, h_mv, h_ve, neg_mean_h, h_r, h_nb, s_hmv, s_hve, s_hr, s_hnb)
                if a and e:
                    low_part(s.plus(2))
                if c:
                    rstd(C, y_mv, y_ve, neg_mean_y, y_r, y_nb, s_ymv, s_yve, s_yr, s_ynb)
                if d and not tail:
                    copy_rows(D_)
                if tail and c:
                    scatter(D_.plus(-1), 0, 1)
                if c:
                    x2(C)
                if tail and c:
                    scatter(D_.plus(-1), 1, 2)
                if c:
                    z_rstd(C)
                if tail and c:
                    scatter(D_.plus(-1), 2, 4)
                if tail and not c:
                    scatter(D_.plus(-1), 0, 4)
                if d and tail:
                    copy_rows(D_)
                if d:
                    weights(D_)
                if d:
                    counts(D_)
                if d and m:
                    scatter(D_, 0, 4)
                if tail and c:
                    scatter(D_, 0, 0)
                if tail and not c:
                    scatter(D_, 0, 4)

            nc.gpsimd.memset(neg_half[:, :], -0.5).then_inc(s_half, 1)
            pool.wait_ge(s_half, 1)
            x_rstd(0, QT, 1)
            x_rstd(QT, 2 * QT, 2)
            nc.gpsimd.memset(stacks[:, 0].rearrange("p a h s -> p (a h s)").bitcast(F32), 0.0).then_inc(s_stack_ones, 1)
            pipeline(pool, step)

            pool.wait_ge(s_tab, TABLE_STEPS)

            def scatter_results(t):
                p = t.slot
                wait(pool, s_res, t.n + 1, own=True)
                nc.gpsimd.indirect_dma_start(
                    out=ys[:, :], out_offset=bass.IndirectOffsetOnAxis(ap=dest[:, p:p + 1], axis=0),
                    in_=res[:, p, :], in_offset=None,
                    bounds_check=TOP * TOKENS - 1, oob_is_err=False).then_inc(s_ysc[p], 16)

            def tile_moves(t, first=False, last=False):
                if not first:
                    scatter_results(t.plus(-1))
                if last:
                    scatter_results(t)

            tiles(pool, tile_moves)

            def even_x3(u):
                pool.wait_ge(s_on, u * UT + QT)
                tiles_ = slice(u * UT, u * UT + QT)
                nc.gpsimd.tensor_tensor(x3[:, tiles_, :], on[:, tiles_, :], x2_sb[:, tiles_, :], ALU.add).then_inc(s_x3[0], 1)

            for u in range(UNITS):
                pool.wait_ge(s_omv, u * UT + UT)
                nc.gpsimd.tensor_scalar(o_ve[:, unit(u)], o_mv[:, unit(u), 1], EPS, None, ALU.add).then_inc(s_ove, 1)
                nc.gpsimd.tensor_scalar(neg_mean_o[:, unit(u)], o_mv[:, unit(u), 0], -1.0, None, ALU.mult).then_inc(s_ove, 1)
                pool.wait_ge(s_ove, 2 * u + 2)
                nc.gpsimd.tensor_tensor(o_r[:, unit(u)], o_ve[:, unit(u)], neg_half[:, 0:UT], ALU.pow).then_inc(s_or, 1)
                pool.wait_ge(s_or, u + 1)
                nc.gpsimd.tensor_tensor(o_nb[:, unit(u)], neg_mean_o[:, unit(u)], o_r[:, unit(u)], ALU.mult).then_inc(s_onb, 1)
                if u > 0:
                    even_x3(u - 1)
            even_x3(UNITS - 1)


def constants(np, tokens, batch, region):
    c = np.zeros((P, C_END), np.float32)
    c[:, C_IDENT:C_IDENT + P] = np.eye(P)
    c[:, C_UPPER:C_UPPER + P] = np.triu(np.ones((P, P)), 1)
    c[:, C_ONES:C_ONES + P] = 1.0
    c[:, C_IOTA:C_IOTA + 16] = np.tile(np.arange(EXPERTS), 2)
    c[:, C_REGION:C_REGION + 16] = np.tile(np.arange(EXPERTS) * region, 2)
    for parity in range(2):
        for t in range(2):
            for k in range(TOP):
                c[:, C_DEST + parity * 4 + t * 2 + k] = k * tokens + (parity - 2) * batch + t * P + np.arange(P)
    c[:, C_LOWER:C_LOWER + 64] = np.tril(np.ones((EXPERTS, EXPERTS))).reshape(-1)
    c[:, C_STEP:C_STEP + 16] = np.arange(16) * P
    c[:, C_TILE:C_TILE + C_PAD - C_TILE] = np.arange(C_PAD - C_TILE)
    c[:, C_SHARE:C_END] = np.arange(EXPERTS) * (region // P)
    c[:, C_PAD + P + 1] = TOP * tokens
    return c


def layouts(np, v):
    d = P
    def halves(w):
        return w.reshape(2, HD, HD, d).transpose(3, 0, 2, 1).reshape(d, d)
    wqk = np.stack([halves(v["L0_attn_w_q"]), halves(v["L0_attn_w_k"])], axis=1)
    gate = v["L0_ffn_gate_proj"].transpose(2, 0, 1)
    up = v["L0_ffn_up_proj"].transpose(2, 0, 1)
    gate_up = np.stack([gate, up], axis=2).reshape(d, -1)
    down = v["L0_ffn_down_proj"].transpose(0, 2, 1)
    down = down.reshape(EXPERTS, -1, P, d).transpose(2, 0, 1, 3).reshape(P, -1)
    norms = np.stack([v["L0_ffn_ln1_g"], v["L0_ffn_ln1_b"], v["L0_ffn_ln2_g"], v["L0_ffn_ln2_b"]], axis=1)
    x = v["L0_attn_hidden_state"]
    tokens = x.shape[0] * x.shape[1]
    return {
        "x": x, "wqk": wqk, "wv": v["L0_attn_w_v"].T, "wo": v["L0_attn_w_o"].T, "attn_w": v["L0_ffn_attn_w"].T,
        "gate_w": v["L0_ffn_gate_w"].T, "norms": norms, "gate_up": gate_up, "down": down,
        "consts": constants(np, tokens, x.shape[1], tokens + P),
    }


def kernel(**inputs):
    import numpy as np
    import concourse.bacc as bacc
    from concourse.bass_utils import run_bass_kernel_spmd

    nc = bacc.Bacc("TRN2", target_bir_lowering=False, num_devices=1)
    arrays, args = {}, []
    for name, a in layouts(np, {k: np.asarray(a) for k, a in inputs.items()}).items():
        a = np.ascontiguousarray(a)
        arrays[f"{name}_dram"] = a
        args.append(nc.dram_tensor(f"{name}_dram", a.shape, F32, kind="ExternalInput").ap())
    out = nc.dram_tensor("out_dram", inputs["L0_attn_hidden_state"].shape, F32, kind="ExternalOutput").ap()
    block_kernel(nc, *args, out)
    r = run_bass_kernel_spmd(nc, [arrays], core_ids=[0])
    return r.results[0]["out_dram"]
```
